# Optimizing a Trainium2 kernel written in Bass

```python
import numpy as np
import jax
import jax.numpy as jnp

def _softmax(x, axis=-1):
    return jax.nn.softmax(x, axis=axis)

def _gelu(x):
    return jax.nn.gelu(x, approximate=True)

def _silu(x):
    return jax.nn.silu(x)

def _sigmoid(x):
    return jax.nn.sigmoid(x)

def _layernorm(x, axis=-1, eps=1e-05):
    m = jnp.mean(x, axis=axis, keepdims=True)
    v = jnp.var(x, axis=axis, keepdims=True)
    return (x - m) / jnp.sqrt(v + eps)

def _scatter_add(tgt, idx, src, axis=0):
    return tgt.at[idx].add(src)

def _segment_sum(src, seg, n):
    return jax.ops.segment_sum(src, seg, n)
kernel_name = 'mk_vit_tower_d2_tok_img1024_r4_a0db8c'

def setup_inputs(seed: int=0):
    np.random.seed(seed)
    _w = jnp.asarray

    def _rec_inputs():
        import jax
        import jax.numpy as jnp
        _rk = jax.random.key(seed)
        x = -0.00016672 + 0.999947 * jax.random.normal(jax.random.fold_in(_rk, 1), (16, 3, 96, 96), jnp.float32)
        return x
    x = _rec_inputs()

    def _L0_tok_setup():
        import jax, jax.numpy as jnp
        import numpy as np
        B, C, H, W = (64, 3, 96, 96)
        P = 16
        HP, WP = (H // P, W // P)
        N = HP * WP
        F = C * P * P
        D = 256
        key = jax.random.key(seed)
        k1, k2, k3, k4, k5 = jax.random.split(key, 5)
        data = jax.random.normal(k1, (B, C, H, W), dtype=jnp.float32)
        lim = 1.0 / np.sqrt(F)
        W_lin = jax.random.uniform(k2, (D, F), minval=-lim, maxval=lim, dtype=jnp.float32)
        b_lin = jax.random.uniform(k3, (D,), minval=-lim, maxval=lim, dtype=jnp.float32)
        class_token = jax.random.normal(k4, (1, 1, D), dtype=jnp.float32)
        position_embeddings = jax.random.normal(k5, (1, N + 1, D), dtype=jnp.float32)
        return {'data': data, 'W_lin': W_lin, 'b_lin': b_lin, 'class_token': class_token, 'position_embeddings': position_embeddings}
    _L0_tok_all = _L0_tok_setup()
    _L0_tok_in = {k: v for k, v in _L0_tok_all.items() if k in ('W_lin', 'b_lin', 'class_token', 'position_embeddings')}
    del _L0_tok_all

    def _L0_attn_setup():
        import jax, jax.numpy as jnp
        import numpy as np
        D = 256
        H = 16
        KVH = 4
        HD = D // H
        LAT = 64
        WIN = 64
        B, S = (1, 512)
        BASE_G, BASE_L = (1000000.0, 10000.0)
        EPS = 1e-06

        def rmsnorm(x, w):
            return x * jax.lax.rsqrt(jnp.mean(x * x, axis=-1, keepdims=True) + EPS) * w

        def qk_norm(x):
            return x * jax.lax.rsqrt(jnp.mean(x * x, axis=-1, keepdims=True) + EPS)

        def rope(x, base):
            s, hd = (x.shape[-2], x.shape[-1])
            inv_freq = 1.0 / base ** (jnp.arange(0, hd, 2, dtype=jnp.float32) / hd)
            freqs = jnp.arange(s, dtype=jnp.float32)[:, None] * inv_freq[None, :]
            cos, sin = (jnp.cos(freqs), jnp.sin(freqs))
            xe, xo = (x[..., ::2], x[..., 1::2])
            out = jnp.stack([xe * cos - xo * sin, xe * sin + xo * cos], axis=-1)
            return out.reshape(x.shape)

        def split_heads(x, n_heads):
            b, s, _ = x.shape
            return x.reshape(b, s, n_heads, HD).transpose(0, 2, 1, 3)

        def repeat_kv(x):
            return jnp.repeat(x, H // KVH, axis=1)

        def sdpa(q, k, v, mask):
            scores = jnp.einsum('bhqd,bhkd->bhqk', q, k) / np.sqrt(HD).astype(np.float32)
            scores = jnp.where(mask, scores, jnp.float32(-1e+30))
            probs = jax.nn.softmax(scores, axis=-1)
            return jnp.einsum('bhqk,bhkd->bhqd', probs, v)

        def merge_heads(x):
            b, h, s, hd = x.shape
            return x.transpose(0, 2, 1, 3).reshape(b, s, h * hd)

        def global_latent_attn(x, wq, w_kv_down, w_k_up, w_v_up, wo):
            q = split_heads(x @ wq, H)
            latent = x @ w_kv_down
            k = split_heads(latent @ w_k_up, KVH)
            v = split_heads(latent @ w_v_up, KVH)
            q, k = (rope(q, BASE_G), rope(k, BASE_G))
            q, k = (qk_norm(q), qk_norm(k))
            k, v = (repeat_kv(k), repeat_kv(v))
            i = jnp.arange(x.shape[1])
            causal = i[:, None] >= i[None, :]
            return merge_heads(sdpa(q, k, v, causal)) @ wo

        def local_gqa_attn(x, wq, wk, wv, wo):
            q = split_heads(x @ wq, H)
            k = split_heads(x @ wk, KVH)
            v = split_heads(x @ wv, KVH)
            q, k = (rope(q, BASE_L), rope(k, BASE_L))
            q, k = (qk_norm(q), qk_norm(k))
            k, v = (repeat_kv(k), repeat_kv(v))
            i = jnp.arange(x.shape[1])
            diff = i[:, None] - i[None, :]
            mask = (diff >= 0) & (diff < WIN)
            return merge_heads(sdpa(q, k, v, mask)) @ wo
        key = jax.random.key(seed)
        ks = jax.random.split(key, 12)
        std = 0.02
        return {'hidden': jax.random.normal(ks[0], (B, S, D), dtype=jnp.float32), 'norm1_w': jnp.ones((D,), jnp.float32), 'norm2_w': jnp.ones((D,), jnp.float32), 'g_wq': jax.random.normal(ks[1], (D, H * HD), jnp.float32) * std, 'g_kv_down': jax.random.normal(ks[2], (D, LAT), jnp.float32) * std, 'g_k_up': jax.random.normal(ks[3], (LAT, KVH * HD), jnp.float32) * std, 'g_v_up': jax.random.normal(ks[4], (LAT, KVH * HD), jnp.float32) * std, 'g_wo': jax.random.normal(ks[5], (D, D), jnp.float32) * std, 'l_wq': jax.random.normal(ks[6], (D, H * HD), jnp.float32) * std, 'l_wk': jax.random.normal(ks[7], (D, KVH * HD), jnp.float32) * std, 'l_wv': jax.random.normal(ks[8], (D, KVH * HD), jnp.float32) * std, 'l_wo': jax.random.normal(ks[9], (D, D), jnp.float32) * std}
    _L0_attn_all = _L0_attn_setup()
    _L0_attn_in = {k: v for k, v in _L0_attn_all.items() if k in ('norm1_w', 'norm2_w', 'g_wq', 'g_kv_down', 'g_k_up', 'g_v_up', 'g_wo', 'l_wq', 'l_wk', 'l_wv', 'l_wo')}
    del _L0_attn_all

    def _L0_ffn_setup():
        import jax, jax.numpy as jnp
        import numpy as np
        N_EXPERTS = 32
        TOP_K = 8
        N_GROUP = 4
        TOPK_GROUP = 2
        ROUTED_SCALING = 2.5

        def _gate(x, gate_w, gate_bias):
            T, E = (x.shape[0], gate_w.shape[0])
            logits = jnp.einsum('th,eh->te', x, gate_w)
            scores = jax.nn.sigmoid(logits)
            scores_choice = scores + gate_bias[None, :]
            grp = scores_choice.reshape(T, N_GROUP, E // N_GROUP)
            top2, _ = jax.lax.top_k(grp, 2)
            group_scores = top2.sum(-1)
            _, grp_idx = jax.lax.top_k(group_scores, TOPK_GROUP)
            group_mask = jax.nn.one_hot(grp_idx, N_GROUP, dtype=scores.dtype).sum(1)
            expert_mask = jnp.repeat(group_mask, E // N_GROUP, axis=1)
            masked = jnp.where(expert_mask > 0, scores_choice, 0.0)
            _, topk_idx = jax.lax.top_k(masked, TOP_K)
            topk_w = jnp.take_along_axis(scores, topk_idx, axis=1)
            topk_w = topk_w / (topk_w.sum(-1, keepdims=True) + 1e-20)
            topk_w = topk_w * ROUTED_SCALING
            return (topk_idx, topk_w)

        def _mlp(x, wg, wu, wd):
            return jnp.einsum('...i,hi->...h', jax.nn.silu(jnp.einsum('...h,ih->...i', x, wg)) * jnp.einsum('...h,ih->...i', x, wu), wd)
        key = jax.random.key(seed)
        ks = jax.random.split(key, 9)
        B, S, H, I = (2, 128, 256, 128)
        w = 0.02
        return {'hidden_states': jax.random.normal(ks[0], (B, S, H), jnp.float32), 'gate_w': jax.random.normal(ks[1], (N_EXPERTS, H), jnp.float32) * w, 'gate_bias': jax.random.normal(ks[2], (N_EXPERTS,), jnp.float32) * w, 'expert_gate': jax.random.normal(ks[3], (N_EXPERTS, I, H), jnp.float32) * w, 'expert_up': jax.random.normal(ks[4], (N_EXPERTS, I, H), jnp.float32) * w, 'expert_down': jax.random.normal(ks[5], (N_EXPERTS, H, I), jnp.float32) * w, 'shared_gate': jax.random.normal(ks[6], (2 * I, H), jnp.float32) * w, 'shared_up': jax.random.normal(ks[7], (2 * I, H), jnp.float32) * w, 'shared_down': jax.random.normal(ks[8], (H, 2 * I), jnp.float32) * w}
    _L0_ffn_all = _L0_ffn_setup()
    _L0_ffn_in = {k: v for k, v in _L0_ffn_all.items() if k in ('gate_w', 'gate_bias', 'expert_gate', 'expert_up', 'expert_down', 'shared_gate', 'shared_up', 'shared_down')}
    del _L0_ffn_all

    def _L1_attn_setup():
        import jax, jax.numpy as jnp
        import numpy as np
        EMBED = 256
        HEADS = 16
        HEAD_DIM = EMBED // HEADS
        key = jax.random.key(seed)
        k1, k2, k3, k4, k5 = jax.random.split(key, 5)
        scale = 1.0 / np.sqrt(EMBED)
        return {'x': jax.random.normal(k1, (4, 512, EMBED), dtype=jnp.float32), 'qkv_w': jax.random.uniform(k2, (3 * EMBED, EMBED), minval=-scale, maxval=scale, dtype=jnp.float32), 'qkv_b': jax.random.uniform(k3, (3 * EMBED,), minval=-scale, maxval=scale, dtype=jnp.float32), 'out_w': jax.random.uniform(k4, (EMBED, EMBED), minval=-scale, maxval=scale, dtype=jnp.float32), 'out_b': jax.random.uniform(k5, (EMBED,), minval=-scale, maxval=scale, dtype=jnp.float32)}
    _L1_attn_all = _L1_attn_setup()
    _L1_attn_in = {k: v for k, v in _L1_attn_all.items() if k in ('qkv_w', 'qkv_b', 'out_w', 'out_b')}
    del _L1_attn_all

    def _L1_ffn_setup():
        import jax, jax.numpy as jnp
        import numpy as np
        QP = 127.0
        MIN_RANGE = 1e-06

        def _ste_round(x):
            return x + jax.lax.stop_gradient(jnp.round(x) - x)

        def _quant_per_tensor(x):
            scale = jnp.maximum(jnp.max(jnp.abs(x)), MIN_RANGE) / QP
            return (_ste_round(x / scale), scale)

        def _qlinear(x2d, w, b):
            xq, sx = _quant_per_tensor(x2d)
            wq, sw = _quant_per_tensor(w)
            out = jnp.matmul(xq, wq.T) + b[None, :]
            return out * (sw * sx)
        key = jax.random.key(seed)
        k = jax.random.split(key, 5)
        B, N, D, H = (8, 256, 256, 1024)
        return {'x': jax.random.normal(k[0], (B, N, D), dtype=jnp.float32), 'w1': jax.random.normal(k[1], (H, D), dtype=jnp.float32) * 0.02, 'b1': jax.random.normal(k[2], (H,), dtype=jnp.float32) * 0.02, 'w2': jax.random.normal(k[3], (D, H), dtype=jnp.float32) * 0.02, 'b2': jax.random.normal(k[4], (D,), dtype=jnp.float32) * 0.02}
    _L1_ffn_all = _L1_ffn_setup()
    _L1_ffn_in = {k: v for k, v in _L1_ffn_all.items() if k in ('w1', 'b1', 'w2', 'b2')}
    del _L1_ffn_all
    return {'x': x, 'L0_tok_W_lin': _L0_tok_in['W_lin'], 'L0_tok_b_lin': _L0_tok_in['b_lin'], 'L0_tok_class_token': _L0_tok_in['class_token'], 'L0_tok_position_embeddings': _L0_tok_in['position_embeddings'], 'L0_attn_norm1_w': _L0_attn_in['norm1_w'], 'L0_attn_norm2_w': _L0_attn_in['norm2_w'], 'L0_attn_g_wq': _L0_attn_in['g_wq'], 'L0_attn_g_kv_down': _L0_attn_in['g_kv_down'], 'L0_attn_g_k_up': _L0_attn_in['g_k_up'], 'L0_attn_g_v_up': _L0_attn_in['g_v_up'], 'L0_attn_g_wo': _L0_attn_in['g_wo'], 'L0_attn_l_wq': _L0_attn_in['l_wq'], 'L0_attn_l_wk': _L0_attn_in['l_wk'], 'L0_attn_l_wv': _L0_attn_in['l_wv'], 'L0_attn_l_wo': _L0_attn_in['l_wo'], 'L0_ffn_gate_w': _L0_ffn_in['gate_w'], 'L0_ffn_gate_bias': _L0_ffn_in['gate_bias'], 'L0_ffn_expert_gate': _L0_ffn_in['expert_gate'], 'L0_ffn_expert_up': _L0_ffn_in['expert_up'], 'L0_ffn_expert_down': _L0_ffn_in['expert_down'], 'L0_ffn_shared_gate': _L0_ffn_in['shared_gate'], 'L0_ffn_shared_up': _L0_ffn_in['shared_up'], 'L0_ffn_shared_down': _L0_ffn_in['shared_down'], 'L1_attn_qkv_w': _L1_attn_in['qkv_w'], 'L1_attn_qkv_b': _L1_attn_in['qkv_b'], 'L1_attn_out_w': _L1_attn_in['out_w'], 'L1_attn_out_b': _L1_attn_in['out_b'], 'L1_ffn_w1': _L1_ffn_in['w1'], 'L1_ffn_b1': _L1_ffn_in['b1'], 'L1_ffn_w2': _L1_ffn_in['w2'], 'L1_ffn_b2': _L1_ffn_in['b2']}

def reference(x, L0_tok_W_lin, L0_tok_b_lin, L0_tok_class_token, L0_tok_position_embeddings, L0_attn_norm1_w, L0_attn_norm2_w, L0_attn_g_wq, L0_attn_g_kv_down, L0_attn_g_k_up, L0_attn_g_v_up, L0_attn_g_wo, L0_attn_l_wq, L0_attn_l_wk, L0_attn_l_wv, L0_attn_l_wo, L0_ffn_gate_w, L0_ffn_gate_bias, L0_ffn_expert_gate, L0_ffn_expert_up, L0_ffn_expert_down, L0_ffn_shared_gate, L0_ffn_shared_up, L0_ffn_shared_down, L1_attn_qkv_w, L1_attn_qkv_b, L1_attn_out_w, L1_attn_out_b, L1_ffn_w1, L1_ffn_b1, L1_ffn_w2, L1_ffn_b2):
    import jax
    import jax.numpy as jnp

    def _L0_tok_ref(data, W_lin, b_lin, class_token, position_embeddings):
        import jax, jax.numpy as jnp
        import numpy as np
        B, C, H, W = (64, 3, 96, 96)
        P = 16
        HP, WP = (H // P, W // P)
        N = HP * WP
        F = C * P * P
        D = 256
        b = data.shape[0]
        x = data.reshape(b, C, HP, P, WP, P)
        x = x.transpose(0, 2, 4, 1, 3, 5).reshape(b, N, F)
        x = jnp.einsum('bnf,df->bnd', x, W_lin) + b_lin
        cls = jnp.broadcast_to(class_token, (b, 1, D))
        out = jnp.concatenate([cls, x], axis=1) + position_embeddings
        return out

    def _L0_attn_ref(hidden, norm1_w, norm2_w, g_wq, g_kv_down, g_k_up, g_v_up, g_wo, l_wq, l_wk, l_wv, l_wo):
        import jax, jax.numpy as jnp
        import numpy as np
        D = 256
        H = 16
        KVH = 4
        HD = D // H
        LAT = 64
        WIN = 64
        B, S = (1, 512)
        BASE_G, BASE_L = (1000000.0, 10000.0)
        EPS = 1e-06

        def rmsnorm(x, w):
            return x * jax.lax.rsqrt(jnp.mean(x * x, axis=-1, keepdims=True) + EPS) * w

        def qk_norm(x):
            return x * jax.lax.rsqrt(jnp.mean(x * x, axis=-1, keepdims=True) + EPS)

        def rope(x, base):
            s, hd = (x.shape[-2], x.shape[-1])
            inv_freq = 1.0 / base ** (jnp.arange(0, hd, 2, dtype=jnp.float32) / hd)
            freqs = jnp.arange(s, dtype=jnp.float32)[:, None] * inv_freq[None, :]
            cos, sin = (jnp.cos(freqs), jnp.sin(freqs))
            xe, xo = (x[..., ::2], x[..., 1::2])
            out = jnp.stack([xe * cos - xo * sin, xe * sin + xo * cos], axis=-1)
            return out.reshape(x.shape)

        def split_heads(x, n_heads):
            b, s, _ = x.shape
            return x.reshape(b, s, n_heads, HD).transpose(0, 2, 1, 3)

        def repeat_kv(x):
            return jnp.repeat(x, H // KVH, axis=1)

        def sdpa(q, k, v, mask):
            scores = jnp.einsum('bhqd,bhkd->bhqk', q, k) / np.sqrt(HD).astype(np.float32)
            scores = jnp.where(mask, scores, jnp.float32(-1e+30))
            probs = jax.nn.softmax(scores, axis=-1)
            return jnp.einsum('bhqk,bhkd->bhqd', probs, v)

        def merge_heads(x):
            b, h, s, hd = x.shape
            return x.transpose(0, 2, 1, 3).reshape(b, s, h * hd)

        def global_latent_attn(x, wq, w_kv_down, w_k_up, w_v_up, wo):
            q = split_heads(x @ wq, H)
            latent = x @ w_kv_down
            k = split_heads(latent @ w_k_up, KVH)
            v = split_heads(latent @ w_v_up, KVH)
            q, k = (rope(q, BASE_G), rope(k, BASE_G))
            q, k = (qk_norm(q), qk_norm(k))
            k, v = (repeat_kv(k), repeat_kv(v))
            i = jnp.arange(x.shape[1])
            causal = i[:, None] >= i[None, :]
            return merge_heads(sdpa(q, k, v, causal)) @ wo

        def local_gqa_attn(x, wq, wk, wv, wo):
            q = split_heads(x @ wq, H)
            k = split_heads(x @ wk, KVH)
            v = split_heads(x @ wv, KVH)
            q, k = (rope(q, BASE_L), rope(k, BASE_L))
            q, k = (qk_norm(q), qk_norm(k))
            k, v = (repeat_kv(k), repeat_kv(v))
            i = jnp.arange(x.shape[1])
            diff = i[:, None] - i[None, :]
            mask = (diff >= 0) & (diff < WIN)
            return merge_heads(sdpa(q, k, v, mask)) @ wo
        x = hidden
        x = x + global_latent_attn(rmsnorm(x, norm1_w), g_wq, g_kv_down, g_k_up, g_v_up, g_wo)
        x = x + local_gqa_attn(rmsnorm(x, norm2_w), l_wq, l_wk, l_wv, l_wo)
        return x

    def _L0_ffn_ref(hidden_states, gate_w, gate_bias, expert_gate, expert_up, expert_down, shared_gate, shared_up, shared_down):
        import jax, jax.numpy as jnp
        import numpy as np
        N_EXPERTS = 32
        TOP_K = 8
        N_GROUP = 4
        TOPK_GROUP = 2
        ROUTED_SCALING = 2.5

        def _gate(x, gate_w, gate_bias):
            T, E = (x.shape[0], gate_w.shape[0])
            logits = jnp.einsum('th,eh->te', x, gate_w)
            scores = jax.nn.sigmoid(logits)
            scores_choice = scores + gate_bias[None, :]
            grp = scores_choice.reshape(T, N_GROUP, E // N_GROUP)
            top2, _ = jax.lax.top_k(grp, 2)
            group_scores = top2.sum(-1)
            _, grp_idx = jax.lax.top_k(group_scores, TOPK_GROUP)
            group_mask = jax.nn.one_hot(grp_idx, N_GROUP, dtype=scores.dtype).sum(1)
            expert_mask = jnp.repeat(group_mask, E // N_GROUP, axis=1)
            masked = jnp.where(expert_mask > 0, scores_choice, 0.0)
            _, topk_idx = jax.lax.top_k(masked, TOP_K)
            topk_w = jnp.take_along_axis(scores, topk_idx, axis=1)
            topk_w = topk_w / (topk_w.sum(-1, keepdims=True) + 1e-20)
            topk_w = topk_w * ROUTED_SCALING
            return (topk_idx, topk_w)

        def _mlp(x, wg, wu, wd):
            return jnp.einsum('...i,hi->...h', jax.nn.silu(jnp.einsum('...h,ih->...i', x, wg)) * jnp.einsum('...h,ih->...i', x, wu), wd)
        orig_shape = hidden_states.shape
        H = orig_shape[-1]
        residuals = hidden_states
        x = hidden_states.reshape(-1, H)
        topk_idx, topk_w = _gate(x, gate_w, gate_bias)
        g = jnp.einsum('th,eih->eti', x, expert_gate)
        u = jnp.einsum('th,eih->eti', x, expert_up)
        outs = jnp.einsum('eti,ehi->eth', jax.nn.silu(g) * u, expert_down)
        outs_t = jnp.transpose(outs, (1, 0, 2))
        gathered = jnp.take_along_axis(outs_t, topk_idx[:, :, None], axis=1)
        final = (gathered * topk_w[:, :, None]).sum(1)
        shared = _mlp(residuals, shared_gate, shared_up, shared_down)
        return final.reshape(orig_shape) + shared

    def _L1_attn_ref(x, qkv_w, qkv_b, out_w, out_b):
        import jax, jax.numpy as jnp
        import numpy as np
        EMBED = 256
        HEADS = 16
        HEAD_DIM = EMBED // HEADS
        b, n, _ = x.shape
        qkv = (jnp.einsum('bne,fe->bnf', x, qkv_w) + qkv_b).reshape(b, n, 3, HEADS, HEAD_DIM)
        q, k, v = (qkv[:, :, 0], qkv[:, :, 1], qkv[:, :, 2])
        scores = jnp.einsum('bnhd,bmhd->bhnm', q, k) / jnp.sqrt(jnp.float32(HEAD_DIM))
        attn = jax.nn.softmax(scores, axis=-1)
        out = jnp.einsum('bhnm,bmhd->bnhd', attn, v).reshape(b, n, EMBED)
        return jnp.einsum('bne,fe->bnf', out, out_w) + out_b

    def _L1_ffn_ref(x, w1, b1, w2, b2):
        import jax, jax.numpy as jnp
        import numpy as np
        QP = 127.0
        MIN_RANGE = 1e-06

        def _ste_round(x):
            return x + jax.lax.stop_gradient(jnp.round(x) - x)

        def _quant_per_tensor(x):
            scale = jnp.maximum(jnp.max(jnp.abs(x)), MIN_RANGE) / QP
            return (_ste_round(x / scale), scale)

        def _qlinear(x2d, w, b):
            xq, sx = _quant_per_tensor(x2d)
            wq, sw = _quant_per_tensor(w)
            out = jnp.matmul(xq, wq.T) + b[None, :]
            return out * (sw * sx)
        B, N, D = x.shape
        h = _qlinear(x.reshape(-1, D), w1, b1)
        h = jax.nn.gelu(h, approximate=False)
        o = _qlinear(h, w2, b2)
        return o.reshape(B, N, -1)
    h = _L0_tok_ref(x, L0_tok_W_lin, L0_tok_b_lin, L0_tok_class_token, L0_tok_position_embeddings)
    h = h + _L0_attn_ref(_layernorm(h, axis=-1), L0_attn_norm1_w, L0_attn_norm2_w, L0_attn_g_wq, L0_attn_g_kv_down, L0_attn_g_k_up, L0_attn_g_v_up, L0_attn_g_wo, L0_attn_l_wq, L0_attn_l_wk, L0_attn_l_wv, L0_attn_l_wo)
    h = h + _L0_ffn_ref(_layernorm(h, axis=-1), L0_ffn_gate_w, L0_ffn_gate_bias, L0_ffn_expert_gate, L0_ffn_expert_up, L0_ffn_expert_down, L0_ffn_shared_gate, L0_ffn_shared_up, L0_ffn_shared_down)
    h = h + _L1_attn_ref(_layernorm(h, axis=-1), L1_attn_qkv_w, L1_attn_qkv_b, L1_attn_out_w, L1_attn_out_b)
    h = h + _L1_ffn_ref(_layernorm(h, axis=-1), L1_ffn_w1, L1_ffn_b1, L1_ffn_w2, L1_ffn_b2)
    return h

_drawn_inputs = setup_inputs


def setup_inputs(seed=0):
    import zlib

    import numpy as np

    out = dict(_drawn_inputs(seed))
    spreads = {'L0_attn_norm1_w': (1.0, 0.6), 'L0_attn_norm2_w': (1.0, 0.6)}
    factors = {'L0_tok_b_lin': 3.014,
     'L0_attn_g_wq': 8.0,
     'L0_attn_g_kv_down': 8.0,
     'L0_attn_g_k_up': 8.0,
     'L0_attn_g_v_up': 8.0,
     'L0_attn_g_wo': 8.0,
     'L0_attn_l_wq': 4.528,
     'L0_attn_l_wk': 4.475,
     'L0_attn_l_wv': 2.763,
     'L0_attn_l_wo': 2.795,
     'L0_ffn_gate_w': 8.0,
     'L0_ffn_gate_bias': 8.0,
     'L0_ffn_expert_gate': 8.0,
     'L0_ffn_expert_up': 8.0,
     'L0_ffn_expert_down': 8.0,
     'L0_ffn_shared_gate': 7.488,
     'L0_ffn_shared_up': 7.354,
     'L0_ffn_shared_down': 7.306,
     'L1_attn_qkv_b': 28.666,
     'L1_attn_out_b': 19.536,
     'L1_ffn_b1': 64.0,
     'L1_ffn_b2': 64.0,
     'L1_attn_qkv_w': 6.268,
     'L1_attn_out_w': 4.281,
     'L1_ffn_w1': 6.419,
     'L1_ffn_w2': 6.244}
    for name, (base, spread) in spreads.items():
        noise = np.random.default_rng([zlib.crc32(name.encode()), seed]).standard_normal(out[name].shape)
        drawn = base * np.exp(spread * noise) if base else spread * noise
        out[name] = jnp.asarray(drawn.astype(out[name].dtype))
    for name, factor in factors.items():
        out[name] = (out[name] * factor).astype(out[name].dtype)
    return out
```

```python
from contextlib import ExitStack

import concourse.bass as bass
from concourse import mybir

B = 16
PATCH, GRID = 16, 6
S = GRID * GRID + 1
T = B * S
D = 256
P = 128
C = D // P
KT = 3 * PATCH * PATCH // P
HEADS, KVH, HD = 16, 4, 16
LAT = 64
HALF = T // 2
HB = B // 2
PAIRS = B // 2
ROWS = 64 + S
TP = 640
HALFPOS = HEADS // 2
EC = HEADS * S
EXPERTS, TOPK, GROUPS, PER_GROUP = 32, 8, 4, 8
UNITS = EXPERTS + 2
INNER = 128
EW = 3 * D
TT = 5
FF = 1024
FC = FF // P
ROUTED_SCALING = 2.5
LN_EPS, RMS_EPS = 1e-5, 1e-6
QP, MIN_RANGE = 127.0, 1e-6
ROUND = 1.5 * 2.0 ** 23

CONST_COLS, VEC_COLS = {}, {}


def _columns(table, widths):
    at = 0
    for name, width in widths:
        table[name] = (at, at + width)
        at += width
    return at


NCONST = _columns(CONST_COLS, [
    ("ident", P), ("mean", P), ("headmean", P), ("ones", P), ("pairs", P), ("minus_ident", S),
    ("cos_g", S), ("sin_g", S), ("cos_l", S), ("sin_l", S), ("onehot", 4), ("tie", 16)])
NVEC = _columns(VEC_COLS, [
    ("pos", C * S), ("base", C * S), ("norm1", C), ("norm2", C), ("qkv_b", 6), ("out_b", C),
    ("b1", FC), ("b2", C), ("gate_bias", EXPERTS)])


NBF = P + S + UNITS


def program(nc, x, w_lin, consts, consts_bf, vecs, g_wq, g_down, g_k, g_v, g_wo, l_wq, l_wk, l_wv, l_wo,
            gate_w, experts, qkv_w, out_w, w1, w2, out):
    f32, f32r, bf16 = mybir.dt.float32, mybir.dt.float32r, mybir.dt.bfloat16
    ALU, ACT, AX = mybir.AluOpType, mybir.ActivationFunctionType, mybir.AxisListType

    with ExitStack() as ctx:
        def sb(name, shape, dt=f32):
            return ctx.enter_context(nc.sbuf_tensor(name, shape, dt))

        def sem(name):
            return ctx.enter_context(nc.semaphore(name))

        region = sb("region", [P, KT * (T + D)])
        patches = region[:, 0:KT * T].rearrange("p (k t) -> p k t", k=KT)
        w_lin_sb = region[:, KT * T:KT * (T + D)].rearrange("p (k d) -> p k d", k=KT)
        hid = region[:, 0:FC * T].rearrange("p (c t) -> p c t", c=FC)
        cst = sb("cst", [P, NCONST])
        cstb = sb("cstb", [P, NBF], bf16)
        vec = sb("vec", [P, NVEC])
        wq_sb = [sb(f"wq_sb{a}", [P, C, 2, D]) for a in range(2)]
        down_sb = sb("down_sb", [P, C, LAT])
        gk_sb = sb("gk_sb", [LAT, 2, P])
        gv_sb = sb("gv_sb", [LAT, KVH * HD])
        lk_sb = sb("lk_sb", [P, C, 2, P])
        lv_sb = sb("lv_sb", [P, C, KVH * HD])
        wo_sb = [sb(f"wo_sb{a}", [P, C, D]) for a in range(2)]
        gate_sb = sb("gate_sb", [P, C, EXPERTS])
        qkv_sb = sb("qkv_sb", [P, C, 3 * D])
        outw_sb = sb("outw_sb", [P, C, D])
        w1_sb = sb("w1_sb", [P, C * FF])
        w2_sb = sb("w2_sb", [P, FC * D])
        w1q = sb("w1q", [P, C, FF], bf16)
        w2q = sb("w2q", [P, FC, D], bf16)

        posb = sb("posb", [P, C, S])
        h = sb("h", [P, C, T])
        xc = sb("xc", [P, C, T])
        sq = sb("sq", [P, C, T])
        x0 = sb("x0", [P, C, T])
        xn = sb("xn", [P, C, TP])
        ars = sb("ars", [P, T])
        var = sb("var", [P, T])
        nt = sb("nt", [P, T])
        latent = sb("latent", [LAT, TP])
        qt = sb("qt", [P, C, TP])
        km = sb("km", [P, C, 4, TP])
        v4 = sb("v4", [P, PAIRS, KVH, HD + 1])
        V16 = PAIRS * HEADS * (HD + 1)
        v16 = region[:, 0:V16].rearrange("p (q h d) -> p q h d", q=PAIRS, h=HEADS)
        dg = region[:, V16:V16 + 2 * HEADS * S].rearrange("p (k h s) -> p k h s", k=2, h=HEADS)
        ra = sb("ra", [P, 2, HALF])
        rb = sb("rb", [P, 2, HALF])
        rt = sb("rt", [P, 2, HALF])
        sq2 = sb("sq2", [P, 2, HALF])
        ms = sb("ms", [P, 2, HALF])
        rs = sb("rs", [P, 2, HALF])
        rn = sb("rn", [P, HALF])
        e = sb("e", [P, 2, EC])
        on = sb("on", [P, 2, HEADS, HD])
        rden = sb("rden", [P, 2, HEADS])
        mx = sb("mx", [P, 2, HEADS])
        ot = sb("ot", [P, C, T])
        tmp = sq

        sig = sb("sig", [P, TT, EXPERTS])
        choice = sb("choice", [P, TT, EXPERTS])
        masked = sb("masked", [P, TT, EXPERTS])
        repl = sb("repl", [P, TT, EXPERTS])
        wts = sb("wts", [P, TT, EXPERTS])
        wres = sb("wres", [P, TT, EXPERTS])
        top = sb("top", [P, TT, GROUPS, 8])
        gsum = sb("gsum", [P, TT, GROUPS])
        grank = sb("grank", [P, TT, GROUPS])
        gcmp = sb("gcmp", [P, TT, GROUPS, GROUPS])
        geq = sb("geq", [P, TT, GROUPS, GROUPS])
        wsum = sb("wsum", [P, TT])
        wparts = sb("wparts", [P, TT, 3 * EXPERTS], bf16)
        wrow = sb("wrow", [P, TT * P], bf16)

        xh = sb("xh", [P, C, T], f32r)
        xl = sb("xl", [P, C, T], f32r)
        NRING = 4
        ring_all = km[:].rearrange("p c i t -> p (c i t)")
        ring = [ring_all[:, i * EW:(i + 1) * EW] for i in range(NRING)]
        wh = [sb(f"wh{i}", [P, EW], f32r) for i in range(NRING)]
        wl = [sb(f"wl{i}", [P, EW], f32r) for i in range(NRING)]
        sg, gu, act = ra, rb, rt
        ah = sb("ah", [P, 2, HALF], f32r)
        al = sb("al", [P, 2, HALF], f32r)

        hidq = km[:].rearrange("p c i t -> p (c i t)").bitcast(bf16)[:, 0:FC * T].rearrange("p (c t) -> p c t", c=FC)
        xq = sq[:].rearrange("p c t -> p (c t)").bitcast(bf16)[:, 0:C * T].rearrange("p (c t) -> p c t", c=C)
        peak = sb("peak", [P, 2 * FC])
        pk = sb("pk", [P, 4])
        pk1 = sb("pk1", [1, 4])
        scale = sb("scale", [P, 4])
        inv = sb("inv", [P, 4])
        sxw = sb("sxw", [P, 2])
        b1s = sb("b1s", [P, FC])
        eps = sb("eps", [P, 4])

        ps = [ctx.enter_context(nc.psum_tensor(f"bank{i}", [P, 512], f32)) for i in range(8)]

        def const(name, rows=P):
            a, b = CONST_COLS[name]
            return cst[0:rows, a:b]

        def vector(name):
            a, b = VEC_COLS[name]
            return vec[:, a:b]

        ident_bf = cstb[:, 0:P]
        causal_bf = cstb[:, P:P + S]
        select_bf = cstb[:, P + S:P + S + UNITS]

        def half(hf):
            return slice(hf * HALF, (hf + 1) * HALF)

        def image(b):
            return slice(b * S, (b + 1) * S)

        s_x = [sem(f"patches_loaded{k}") for k in range(KT)]
        s_cst = sem("constants_loaded")
        s_attn_w = [sem(f"attention_weights_loaded{a}") for a in range(2)]
        s_ffw = sem("ffn_weights_loaded")
        s_moe_w = sem("router_and_last_attention_weights_loaded")
        s_ring = [sem(f"expert_loaded{i}") for i in range(NRING)]
        s_init = sem("buffers_initialised")
        s_tok = sem("embedding_summed")
        s_h = sem("stream_ready")
        s_mean = sem("mean_summed")
        s_cent = sem("tokens_centred")
        s_sq = sem("squares_ready")
        s_var = sem("variance_summed")
        s_ars = sem("table_rsqrt_ready")
        s_xn = sem("normalised_ready")
        s_x0 = sem("attention_stream_ready")
        s_lat = sem("latent_summed")
        s_latv = sem("latent_copied")
        s_proj = sem("qk_projected")
        s_rope = sem("rope_products_ready")
        s_rsum = sem("rope_summed")
        s_qsq = sem("qk_squares_ready")
        s_qms = sem("qk_mean_square_summed")
        s_qars = sem("qk_table_rsqrt_ready")
        s_qk = sem("qk_ready")
        s_vps = sem("values_projected")
        s_v = sem("values_copied")
        s_s = sem("scores_summed")
        s_e = sem("exponentials_ready")
        s_o = sem("outputs_summed")
        s_on = sem("outputs_normalised")
        s_ott = sem("outputs_transposed")
        s_ot = sem("outputs_copied")
        s_wo = sem("attention_projected")
        s_log = sem("router_logits_summed")
        s_sig = sem("router_scores_ready")
        s_wp = sem("weight_parts_ready")
        s_wt = sem("weight_parts_transposed")
        s_wrow = sem("weight_rows_ready")
        s_xs = sem("tokens_split")
        s_wsh = sem("expert_high_parts_ready")
        s_wsl = sem("expert_low_parts_ready")
        s_g = sem("gate_summed")
        s_u = sem("up_and_weight_summed")
        s_sg = sem("silu_ready")
        s_act = sem("weighted_activation_ready")
        s_ah = sem("activation_high_part_ready")
        s_al = sem("activation_low_part_ready")
        s_down = sem("down_summed")
        s_acc = sem("experts_all_summed")
        s_qkps = sem("last_qk_projected")
        s_qkev = sem("last_q_copied")
        s_kev = sem("last_k_copied")
        s_sq_s = sem("row_scores_summed")
        s_mx = sem("row_maxima_read")
        s_dg = sem("maxima_on_diagonals")
        s_pk = sem("peaks_ready")
        s_pkt = sem("peaks_in_a_row")
        s_pk1 = sem("peak_reduced")
        s_pkb = sem("peak_broadcast")
        s_sc = sem("scales_ready")
        s_wqt = sem("ffn_weight_scaled")
        s_wq = sem("ffn_weights_quantised")
        s_xq = sem("ffn_input_quantised")
        s_f1 = sem("ffn_first_summed")
        s_hid = sem("hidden_ready")
        s_hpk = sem("hidden_peak_read")
        s_hs = sem("hidden_scaled")
        s_hq = sem("hidden_quantised")
        s_f2 = sem("ffn_second_summed")
        s_fin = sem("result_ready")
        s_out = sem("result_stored")
        s_dve = sem("vector_step")
        s_act_own = sem("scalar_step")
        s_mulc = sem("expert_product_ready")
        s_pool_own = sem("pool_step")

        block = ctx.enter_context(nc.Block())
        NPROJ = 3 * 2

        def cent_count(n, hf):
            return 2 * {0: 0, 2: 1, 3: 2, 4: 3}[n] + hf + 1

        def score_bank(a, p):
            return 4 + 2 * (p % 2) if a < 2 else 6

        def head_at(a, gp, k):
            if a < 2:
                i, c = k // 2, k % 2
                return i, c, i * 4 + 2 * c + gp, i
            c, i = k // 4, k % 4
            hd = c * 8 + gp * 4 + i
            return i, c, hd, hd

        @block.sync
        def _(sp):
            for k in range(KT):
                sp.dma_start(patches[:, k, :], x[:, k, :]).then_inc(s_x[k], 16)
                sp.dma_start(w_lin_sb[:, k, :], w_lin[:, k, :]).then_inc(s_x[k], 16)
            sp.dma_start(wq_sb[0][:], g_wq).then_inc(s_attn_w[0], 16)
            sp.dma_start(wo_sb[0][:], g_wo).then_inc(s_attn_w[0], 16)
            sp.dma_start(wq_sb[1][:], l_wq).then_inc(s_attn_w[1], 16)
            sp.dma_start(lk_sb[:], l_wk).then_inc(s_attn_w[1], 16)
            sp.dma_start(lv_sb[:], l_wv).then_inc(s_attn_w[1], 16)
            sp.dma_start(wo_sb[1][:], l_wo).then_inc(s_attn_w[1], 16)
            sp.dma_start(w1_sb[:], w1).then_inc(s_ffw, 16)
            sp.dma_start(w2_sb[:], w2).then_inc(s_ffw, 16)
            sp.dma_start(gate_sb[:], gate_w).then_inc(s_moe_w, 16)
            sp.dma_start(qkv_sb[:], qkv_w).then_inc(s_moe_w, 16)
            sp.dma_start(outw_sb[:], out_w).then_inc(s_moe_w, 16)
            sp.wait_ge(s_s, 2 * PAIRS)
            for i in range(NRING):
                sp.dma_start(ring[i], experts[i, :, :]).then_inc(s_ring[i], 16)
            with sp.Fori(1, UNITS // NRING) as r:
                for i in range(NRING):
                    sp.wait_ge(s_wsh, r * NRING + (i + 1 - NRING))
                    sp.wait_ge(s_wsl, r * NRING + (i + 1 - NRING))
                    sp.dma_start(ring[i],
                                 experts[bass.ds(r * NRING + i, 1), :, :].rearrange("a p n -> (a p) n"))\
                        .then_inc(s_ring[i], 16)
            for u in range(UNITS - UNITS % NRING, UNITS):
                i = u % NRING
                sp.wait_ge(s_wsh, u + 1 - NRING)
                sp.wait_ge(s_wsl, u + 1 - NRING)
                sp.dma_start(ring[i], experts[u, :, :]).then_inc(s_ring[i], 16)
            for hf in range(2):
                sp.wait_ge(s_fin, hf + 1)
                sp.dma_start(out[:, :, half(hf)], x0[:, :, half(hf)]).then_inc(s_out, 16)
            sp.wait_ge(s_out, 32)

        @block.gpsimd
        def _(pool):
            nc.gpsimd.memset(eps[:, 0:1], LN_EPS).then_inc(s_init, 1)
            nc.gpsimd.memset(eps[:, 1:2], RMS_EPS * LN_EPS).then_inc(s_init, 1)
            nc.gpsimd.memset(eps[:, 2:3], RMS_EPS).then_inc(s_init, 1)
            nc.gpsimd.memset(xn[:, :, T:TP], 0.0).then_inc(s_init, 1)
            nc.gpsimd.memset(latent[:, T:TP], 0.0).then_inc(s_init, 1)
            nc.gpsimd.memset(qt[:, :, T:TP], 0.0).then_inc(s_init, 1)
            nc.gpsimd.memset(v4[:, :, :, HD:HD + 1], 1.0).then_inc(s_init, 1)
            nc.gpsimd.memset(on[:], 0.0).then_inc(s_init, 1)

            def rope_sums(a):
                for u in range(NPROJ):
                    n = a * NPROJ + u
                    pool.wait_ge(s_rope, n + 1)
                    if n >= 2:
                        pool.wait_ge(s_qk, n - 1)
                    nc.gpsimd.tensor_tensor(rt[:, u % 2, :], ra[:, u % 2, :], rb[:, u % 2, :], ALU.add)\
                        .then_inc(s_rsum, 1)

            pool.wait_ge(s_tok, 2)
            nc.gpsimd.memset(v16[:, :, :, HD:HD + 1], 1.0).then_inc(s_init, 1)
            rope_sums(0)
            rope_sums(1)
            pool.wait_ge(s_sc, 1)
            for k, (w, wq_) in enumerate(((w1_sb, w1q), (w2_sb, w2q))):
                nc.gpsimd.tensor_scalar(w[:], w[:], inv[:, k:k + 1], ROUND, ALU.mult, ALU.add).then_inc(s_wqt, 1)
            for k, (w, wq_) in enumerate(((w1_sb, w1q), (w2_sb, w2q))):
                pool.wait_ge(s_wqt, k + 1)
                nc.gpsimd.tensor_scalar(wq_[:].rearrange("p c n -> p (c n)"), w[:], 1.0, -ROUND, ALU.mult, ALU.add)\
                    .then_inc(s_wq, 1)
            def low_part(u, i):
                pool.wait_ge(s_wsh, u + 1)
                nc.gpsimd.tensor_tensor(wl[i][:], ring[i], wh[i][:].bitcast(f32), ALU.subtract)\
                    .then_inc(s_wsl, 1)

            with pool.Fori(0, UNITS // NRING) as r:
                for i in range(NRING):
                    low_part(r * NRING + i, i)
            for u in range(UNITS - UNITS % NRING, UNITS):
                low_part(u, u % NRING)

        @block.scalar
        def _(act_e):
            own = [0]

            def link(ins):
                own[0] += 1
                ins.then_inc(s_act_own, 1)
                act_e.wait_ge(s_act_own, own[0])

            act_e.dma_start(cst[:], consts).then_inc(s_cst, 16)
            act_e.dma_start(vec[:], vecs).then_inc(s_cst, 16)
            act_e.dma_start(nt[:, 0:NBF], consts_bf).then_inc(s_cst, 16)
            act_e.dma_start(down_sb[:], g_down).then_inc(s_attn_w[0], 16)
            act_e.dma_start(gk_sb[:], g_k).then_inc(s_attn_w[0], 16)
            act_e.dma_start(gv_sb[:], g_v).then_inc(s_attn_w[0], 16)
            act_e.wait_ge(s_init, 10)
            act_e.wait_ge(s_cst, 48)

            def norm(n, mean=True, eps_at=0, twice=False):
                for hf in range(2):
                    if mean:
                        act_e.wait_ge(s_cent, cent_count(n, hf))
                        src = xc
                    else:
                        act_e.wait_ge(s_x0, 2 + hf + 1)
                        src = x0
                    nc.scalar.activation(sq[:, :, half(hf)], src[:, :, half(hf)], ACT.Square).then_inc(s_sq, 1)
                for hf in range(2):
                    act_e.wait_ge(s_var, 2 * n + hf + 1)
                    nc.scalar.activation(var[:, half(hf)], ps[2 + hf][:, 0:HALF], ACT.Identity,
                                         bias=eps[:, eps_at:eps_at + 1])
                    nc.scalar.activation(ars[:, half(hf)], ps[2 + hf][:, 0:HALF], ACT.Abs_reciprocal_sqrt,
                                         bias=eps[:, eps_at:eps_at + 1]).then_inc(s_ars, 1)

            def qk_units(a):
                for u in range(NPROJ + 1):
                    n = a * NPROJ + u
                    if u < NPROJ:
                        act_e.wait_ge(s_proj, n + 1)
                        nc.scalar.activation(sq2[:, u % 2, :], ps[4 + 2 * (u % 2)][:, 0:HALF], ACT.Square)\
                            .then_inc(s_qsq, 1)
                    if u >= 1:
                        m = n - 1
                        act_e.wait_ge(s_qms, m + 1)
                        if m >= 2:
                            act_e.wait_ge(s_qk, m - 1)
                        nc.scalar.activation(ms[:, (u - 1) % 2, :], ps[(u - 1) % 2][:, 0:HALF], ACT.Identity,
                                             bias=eps[:, 2:3])
                        nc.scalar.activation(rs[:, (u - 1) % 2, :], ps[(u - 1) % 2][:, 0:HALF],
                                             ACT.Abs_reciprocal_sqrt, bias=eps[:, 2:3]).then_inc(s_qars, 1)

            def outputs_copied(a, g):
                act_e.wait_ge(s_ott, a * PAIRS + 2 * g + 2)
                src = ps[2 + g % 2][:].rearrange("p (q c w) -> p c q w", q=2, c=C)
                for c in range(C):
                    dst = ot[:, c, 4 * g * S:4 * (g + 1) * S].rearrange("p (q b s) -> p q b s", q=2, b=2)
                    view = src[:, c, :, :].rearrange("p q (b w) -> p q b w", b=2)[:, :, :, 0:S]
                    if a < 2:
                        ins = nc.scalar.activation(dst, view, ACT.Copy)
                    else:
                        ins = nc.scalar.activation(dst, view, ACT.Identity, bias=vector("qkv_b")[:, 4 + c:5 + c])
                ins.then_inc(s_ot, 1)

            def attention(a):
                for p in range(PAIRS + 2):
                    if p < PAIRS:
                        n = a * PAIRS + p
                        act_e.wait_ge(s_s, n + 1)
                        if n >= 2:
                            act_e.wait_ge(s_o, n - 1)
                        sb0 = score_bank(a, p)
                        for k in range(2):
                            ins = nc.scalar.activation(e[0:ROWS, p % 2, k * HALFPOS * S:(k + 1) * HALFPOS * S],
                                                       ps[sb0 + k][0:ROWS, 0:HALFPOS * S], ACT.Exp,
                                                       scale=HD ** -0.5)
                        ins.then_inc(s_e, 1)
                    if p >= 4 and p % 2 == 0:
                        outputs_copied(a, (p - 4) // 2)
                outputs_copied(a, PAIRS // 2 - 1)

            norm(0, eps_at=0)
            for hf in range(2):
                act_e.wait_ge(s_x0, hf + 1)
                nc.scalar.activation(var[:, half(hf)], ps[2 + hf][:, 0:HALF], ACT.Identity,
                                     bias=eps[:, 1:2], scale=1.0 + RMS_EPS)
                nc.scalar.activation(ars[:, half(hf)], ps[2 + hf][:, 0:HALF], ACT.Abs_reciprocal_sqrt,
                                     bias=eps[:, 1:2], scale=1.0 + RMS_EPS).then_inc(s_ars, 1)
            for hf in range(2):
                act_e.wait_ge(s_lat, hf + 1)
                nc.scalar.activation(latent[:, half(hf)], ps[2 + hf][0:LAT, 0:HALF], ACT.Copy).then_inc(s_latv, 1)
            for a in range(2):
                if a == 1:
                    norm(1, mean=False, eps_at=2)
                qk_units(a)
                act_e.wait_ge(s_vps, a + 1)
                nc.scalar.activation(v4[:, :, :, 0:HD],
                                     ps[2][:].rearrange("p (q h d) -> p q h d", q=PAIRS, h=KVH),
                                     ACT.Copy).then_inc(s_v, 1)
                attention(a)

            norm(2)
            act_e.wait_ge(s_log, 1)
            nc.scalar.activation(sig[:].rearrange("p t n -> p (t n)"), ps[4][:, 0:TT * EXPERTS], ACT.Sigmoid)\
                .then_inc(s_sig, 1)
            nc.scalar.activation(xh[:], xn[:, :, 0:T], ACT.Copy).then_inc(s_xs, 1)

            def high_part(u, i, r, reused=True):
                act_e.wait_ge(s_ring[i], r * 16 + 16)
                if reused:
                    act_e.wait_ge(s_down, 2 * (u - NRING + 1))
                    act_e.wait_ge(s_wsl, u - NRING + 1)
                nc.scalar.activation(wh[i][:], ring[i], ACT.Copy).then_inc(s_wsh, 1)

            def expert_unit(n, j):
                act_e.wait_ge(s_g, n + 1)
                nc.scalar.activation(sg[:, j, :], ps[4][:, 0:HALF], ACT.Silu).then_inc(s_sg, 1)
                act_e.wait_ge(s_act, n + 1)
                nc.scalar.activation(ah[:, j, :], act[:, j, :], ACT.Copy).then_inc(s_ah, 1)

            AHEAD = 2
            for i in range(AHEAD):
                high_part(i, i, 0, False)
            for i in range(NRING):
                expert_unit(2 * i, 0)
                high_part(i + AHEAD, (i + AHEAD) % NRING, (i + AHEAD) // NRING, i + AHEAD >= NRING)
                expert_unit(2 * i + 1, 1)
            with act_e.Fori(1, (UNITS - AHEAD) // NRING) as r:
                for i in range(NRING):
                    u = r * NRING + i
                    expert_unit(2 * u, 0)
                    high_part(u + AHEAD, (i + AHEAD) % NRING, r + (i + AHEAD) // NRING)
                    expert_unit(2 * u + 1, 1)
            for u in range(UNITS - AHEAD, UNITS):
                expert_unit(2 * u, 0)
                expert_unit(2 * u + 1, 1)
            act_e.wait_ge(s_acc, 1)
            for hf in range(2):
                for m in range(C):
                    ins = nc.scalar.activation(h[:, m, half(hf)], ps[2 * m + hf][:, 0:HALF], ACT.Copy)
                ins.then_inc(s_h, 1)

            norm(3)
            for c in range(C):
                for hf in range(2):
                    act_e.wait_ge(s_qkps, 2 * c + hf + 1)
                    nc.scalar.activation(qt[:, c, half(hf)], ps[4 + 2 * c + hf][:, 0:HALF], ACT.Identity,
                                         bias=vector("qkv_b")[:, c:c + 1]).then_inc(s_qkev, 1)
            for b in range(4):
                act_e.wait_ge(s_vps, 2 + b + 1)
                nc.scalar.activation(v16[:, 2 * b:2 * b + 2, :, 0:HD],
                                     ps[4 + b][:].rearrange("p (q h d) -> p q h d", q=2, h=HEADS),
                                     ACT.Copy).then_inc(s_v, 1)
            attention(2)

            norm(4)
            for u in range(2 * FC):
                hf, ch = u // FC, u % FC
                act_e.wait_ge(s_f1, u + 1)
                if u == 0:
                    act_e.wait_ge(s_sc, 4)
                nc.scalar.activation(hid[:, ch, half(hf)], ps[4 + u % 4][:, 0:HALF], ACT.Gelu,
                                     bias=b1s[:, ch:ch + 1], scale=sxw[:, 0:1]).then_inc(s_hid, 1)
            act_e.wait_ge(s_sc, 5)
            for ch in range(FC):
                nc.scalar.activation(hid[:, ch, :], hid[:, ch, :], ACT.Copy, bias=ROUND, scale=inv[:, 3:4])\
                    .then_inc(s_hs, 1)

        @block.vector
        def _(dve):
            own = [0]

            def link(ins):
                own[0] += 1
                ins.then_inc(s_dve, 1)
                dve.wait_ge(s_dve, own[0])

            def bc(ap, dims):
                return ap.broadcast_to(dims)

            def newton(y, v, t):
                link(nc.vector.scalar_tensor_tensor(t, v, -0.5, y, ALU.mult, ALU.mult))
                link(nc.vector.tensor_tensor(t, t, y, ALU.mult))
                link(nc.vector.scalar_tensor_tensor(y, t, 1.5, y, ALU.add, ALU.mult))

            def centre(n):
                for hf in range(2):
                    dve.wait_ge(s_mean, cent_count(n, hf))
                    nc.vector.tensor_tensor(xc[:, :, half(hf)], h[:, :, half(hf)],
                                            bc(ps[hf][:, 0:HALF].unsqueeze(1), [P, C, HALF]), ALU.subtract)\
                        .then_inc(s_cent, 1)

            def scaled(dst, src, hf, weight=None):
                last = None
                for c in range(C):
                    if weight is None:
                        last = nc.vector.tensor_tensor(dst[:, c, half(hf)], src[:, c, half(hf)],
                                                       ars[:, half(hf)], ALU.mult)
                    else:
                        last = nc.vector.scalar_tensor_tensor(dst[:, c, half(hf)], src[:, c, half(hf)],
                                                              weight[:, c:c + 1], ars[:, half(hf)],
                                                              ALU.mult, ALU.mult)
                return last

            def norm_apply(dst, src, count, sig_to, weight=None):
                for hf in range(2):
                    dve.wait_ge(s_ars, count + hf + 1)
                    newton(ars[:, half(hf)], var[:, half(hf)], nt[:, half(hf)])
                    scaled(dst, src, hf, weight).then_inc(sig_to, 1)

            def reduce_peaks(k, n, bank, count):
                dve.wait_ge(s_pkt, count)
                nc.vector.tensor_reduce(pk1[0:1, k:k + n], ps[bank][0:1, 0:n * P].rearrange("p (n c) -> p n c", n=n),
                                        AX.X, ALU.max).then_inc(s_pk1, 1)

            def scales_of(k, n, bank, count):
                dve.wait_ge(s_pkb, count)
                link(nc.vector.tensor_scalar(scale[:, k:k + n], ps[bank][:, 0:n], MIN_RANGE, 1.0 / QP,
                                             ALU.max, ALU.mult))
                return nc.vector.reciprocal(inv[:, k:k + n], scale[:, k:k + n])

            def qk_units(a):
                names = (("cos_g", "sin_g"), ("cos_l", "sin_l"))[a]
                cos, sin = (bc(const(x).unsqueeze(1), [P, HB, S]) for x in names)

                def images(ap):
                    return ap.rearrange("p (b s) -> p b s", s=S)

                for u in range(NPROJ + 1):
                    n = a * NPROJ + u
                    if u < NPROJ:
                        dve.wait_ge(s_proj, n + 1)
                        b0 = 4 + 2 * (u % 2)
                        if n >= 2:
                            dve.wait_ge(s_rsum, n - 1)
                        nc.vector.tensor_tensor(images(rb[:, u % 2, :]), images(ps[b0 + 1][:, 0:HALF]), sin,
                                                ALU.mult)
                        dve.wait_ge(s_qsq, n + 1)
                        nc.vector.tensor_tensor(images(ra[:, u % 2, :]), images(ps[b0][:, 0:HALF]), cos,
                                                ALU.mult).then_inc(s_rope, 1)
                    if u >= 1:
                        w, k = u - 1, (u - 1) % 2
                        dve.wait_ge(s_qars, n)
                        newton(rs[:, k, :], ms[:, k, :], rn[:])
                        dve.wait_ge(s_rsum, n)
                        j, hf = w // 2, w % 2
                        if j < 2:
                            ins = nc.vector.tensor_tensor(qt[:, j, half(hf)], rt[:, k, :], rs[:, k, :], ALU.mult)
                        else:
                            for i in range(4):
                                ins = nc.vector.scalar_tensor_tensor(
                                    km[:, 0, i, half(hf)], rt[:, k, :], const("onehot")[:, i:i + 1],
                                    rs[:, k, :], ALU.mult, ALU.mult)
                        ins.then_inc(s_qk, 1)
                    if a == 1 and u == 2:
                        reduce_peaks(0, 2, 3, 1)
                    if a == 1 and u == 4:
                        scales_of(0, 2, 3, 1).then_inc(s_sc, 1)

            def normalise_outputs(a, p):
                n = a * PAIRS + p
                dve.wait_ge(s_o, n + 1)
                o = [ps[b][64 * b:64 * b + S, 0:HEADS * (HD + 1)].rearrange("p (h d) -> p h d", h=HEADS)
                     for b in range(2)]
                den = [rden[64 * b:64 * b + S, p % 2, :] for b in range(2)]
                for b in range(2):
                    ins = nc.vector.reciprocal(den[b], o[b][:, :, HD])
                link(ins)
                if n >= 2:
                    dve.wait_ge(s_ott, n - 1)
                for b in range(2):
                    ins = nc.vector.tensor_tensor(on[64 * b:64 * b + S, p % 2, :, :], o[b][:, :, 0:HD],
                                                  bc(den[b].unsqueeze(2), [S, HEADS, HD]), ALU.mult)
                ins.then_inc(s_on, 1)

            nc.vector.memset(wrow[96:97, :], 1.0).then_inc(s_init, 1)
            dve.wait_ge(s_cst, 48)
            nc.vector.tensor_copy(cstb[:], nt[:, 0:NBF]).then_inc(s_init, 1)
            link(nc.vector.tensor_tensor(posb[:].rearrange("p c s -> p (c s)"), vector("pos"), vector("base"),
                                         ALU.add))
            for hf in range(2):
                dve.wait_ge(s_tok, hf + 1)
                for c in range(C):
                    ins = nc.vector.tensor_tensor(
                        h[:, c, half(hf)].rearrange("p (b s) -> p b s", s=S),
                        ps[2 * c + hf][:, 0:HALF].rearrange("p (b s) -> p b s", s=S),
                        bc(posb[:, c, :].unsqueeze(1), [P, HB, S]), ALU.add)
                ins.then_inc(s_h, 1)

            centre(0)
            norm_apply(x0, xc, 0, s_x0)
            norm_apply(xn, xc, 2, s_xn, vector("norm1"))
            for a in range(2):
                if a == 1:
                    norm_apply(xn, x0, 4, s_xn, vector("norm2"))
                qk_units(a)
                for p in range(PAIRS):
                    normalise_outputs(a, p)
                    if a == 0 and p == 1:
                        dve.wait_ge(s_ffw, 32)
                    if a == 0 and p in (1, 4):
                        nc.vector.tensor_reduce(pk[:, p // 4:p // 4 + 1], (w1_sb, w2_sb)[p // 4][:], AX.X, ALU.max,
                                                apply_absolute_value=True).then_inc(s_pk, 1)
                for hf in range(2):
                    dve.wait_ge(s_wo, 2 * a + hf + 1)
                    for m in range(C):
                        dst = x0[:, m, half(hf)] if a == 0 else tmp[:, m, half(hf)]
                        ins = nc.vector.tensor_tensor(dst, x0[:, m, half(hf)], ps[4 + 2 * m + hf][:, 0:HALF], ALU.add)
                    if a == 0:
                        ins.then_inc(s_x0, 1)
                    else:
                        link(ins)
                        nc.vector.tensor_tensor(h[:, :, half(hf)], h[:, :, half(hf)], tmp[:, :, half(hf)], ALU.add)\
                            .then_inc(s_h, 1)

            centre(2)
            norm_apply(xn, xc, 6, s_xn)
            dve.wait_ge(s_sig, 1)
            bias = bc(vector("gate_bias").unsqueeze(1), [P, TT, EXPERTS])
            link(nc.vector.tensor_tensor(choice[:], sig[:], bias, ALU.add))
            for t in range(TT):
                for g in range(GROUPS):
                    ins = nc.vector.max(top[:, t, g, :], choice[:, t, g * PER_GROUP:(g + 1) * PER_GROUP])
            link(ins)
            link(nc.vector.tensor_tensor(gsum[:], top[:, :, :, 0], top[:, :, :, 1], ALU.add))
            for t in range(TT):
                mine = bc(gsum[:, t, :].unsqueeze(2), [P, GROUPS, GROUPS])
                others = bc(gsum[:, t, :].unsqueeze(1), [P, GROUPS, GROUPS])
                nc.vector.tensor_tensor(gcmp[:, t, :, :], others, mine, ALU.is_gt)
                ins = nc.vector.tensor_tensor(geq[:, t, :, :], others, mine, ALU.is_equal)
            link(ins)
            flat = lambda ap: ap.rearrange("p t a b -> p t (a b)")
            link(nc.vector.tensor_tensor(flat(geq[:]), flat(geq[:]),
                                         bc(const("tie").unsqueeze(1), [P, TT, 16]), ALU.mult))
            link(nc.vector.tensor_tensor(flat(gcmp[:]), flat(gcmp[:]), flat(geq[:]), ALU.add))
            link(nc.vector.tensor_reduce(grank[:], gcmp[:], AX.X, ALU.add))
            link(nc.vector.tensor_scalar(grank[:], grank[:], 2.0, None, ALU.is_lt))
            for t in range(TT):
                ins = nc.vector.tensor_tensor(
                    masked[:, t, :].rearrange("p (g k) -> p g k", g=GROUPS),
                    choice[:, t, :].rearrange("p (g k) -> p g k", g=GROUPS),
                    bc(grank[:, t, :].unsqueeze(2), [P, GROUPS, PER_GROUP]), ALU.mult)
            link(ins)
            link(nc.vector.tensor_scalar(masked[:], masked[:], 0.0, None, ALU.add))
            for t in range(TT):
                ins = nc.vector.max(top[:, t, 0, :], masked[:, t, :])
            link(ins)
            for t in range(TT):
                ins = nc.vector.match_replace(repl[:, t, :], top[:, t, 0, :], masked[:, t, :], -3.0e38)
            link(ins)
            link(nc.vector.tensor_tensor(repl[:], repl[:], masked[:], ALU.not_equal))
            link(nc.vector.tensor_tensor(wts[:], repl[:], sig[:], ALU.mult))
            link(nc.vector.tensor_reduce(wsum[:], wts[:], AX.X, ALU.add))
            link(nc.vector.tensor_scalar(wsum[:], wsum[:], 1e-20, None, ALU.add))
            link(nc.vector.reciprocal(wsum[:], wsum[:]))
            link(nc.vector.tensor_scalar(wsum[:], wsum[:], ROUTED_SCALING, None, ALU.mult))
            link(nc.vector.tensor_tensor(wts[:], wts[:], bc(wsum[:].unsqueeze(2), [P, TT, EXPERTS]), ALU.mult))
            link(nc.vector.tensor_copy(wparts[:, :, 0:EXPERTS], wts[:]))
            link(nc.vector.tensor_tensor(wres[:], wts[:], wparts[:, :, 0:EXPERTS], ALU.subtract))
            link(nc.vector.tensor_copy(wparts[:, :, EXPERTS:2 * EXPERTS], wres[:]))
            link(nc.vector.tensor_tensor(wres[:], wres[:], wparts[:, :, EXPERTS:2 * EXPERTS], ALU.subtract))
            nc.vector.tensor_copy(wparts[:, :, 2 * EXPERTS:3 * EXPERTS], wres[:]).then_inc(s_wp, 1)
            dve.wait_ge(s_xs, 1)
            nc.vector.tensor_tensor(xl[:], xn[:, :, 0:T], xh[:].bitcast(f32), ALU.subtract).then_inc(s_xs, 1)
            dve.wait_ge(s_wt, 1)
            nc.vector.tensor_copy(wrow[0:96, :], ps[5][:].bitcast(bf16)[0:96, 0:TT * P]).then_inc(s_wrow, 1)

            def expert_unit(n, j):
                dve.wait_ge(s_sg, n + 1)
                dve.wait_ge(s_u, n + 1)
                ins = nc.vector.tensor_tensor(gu[:, j, :], sg[:, j, :], ps[5][:, 0:HALF], ALU.mult)
                ins.then_inc(s_mulc, 1)
                dve.wait_ge(s_mulc, n + 1)
                nc.vector.tensor_tensor(act[:, j, :], gu[:, j, :], ps[6][:, 0:HALF], ALU.mult).then_inc(s_act, 1)
                dve.wait_ge(s_ah, n + 1)
                nc.vector.tensor_tensor(al[:, j, :], act[:, j, :], ah[:, j, :].bitcast(f32), ALU.subtract)\
                    .then_inc(s_al, 1)

            with dve.Fori(0, UNITS // 2) as r:
                for j in range(4):
                    expert_unit(r * 4 + j, j % 2)

            centre(3)
            norm_apply(xn, xc, 8, s_xn)
            for c in range(C):
                for hf in range(2):
                    dve.wait_ge(s_qkps, 4 + 2 * c + hf + 1)
                    for i in range(4):
                        ins = nc.vector.tensor_scalar(km[:, c, i, half(hf)], ps[2 * c + hf][:, 0:HALF],
                                                      vector("qkv_b")[:, 2 + c:3 + c],
                                                      const("onehot")[:, i:i + 1], ALU.add, ALU.mult)
                    ins.then_inc(s_kev, 1)
            for p in range(PAIRS + 2):
                if p < PAIRS:
                    dve.wait_ge(s_sq_s, p + 1)
                    for k in range(2):
                        ins = nc.vector.tensor_reduce(
                            mx[:, p % 2, k * HALFPOS:(k + 1) * HALFPOS],
                            ps[4 + k][:, 0:HALFPOS * S].rearrange("p (h s) -> p h s", s=S), AX.X, ALU.max)
                    ins.then_inc(s_mx, 1)
                    dve.wait_ge(s_mx, p + 1)
                    if p >= 2:
                        dve.wait_ge(s_s, 2 * PAIRS + p - 1)
                    nc.vector.tensor_tensor(dg[:, p % 2, :, :], bc(mx[:, p % 2, :].unsqueeze(2), [P, HEADS, S]),
                                            bc(const("minus_ident").unsqueeze(1), [P, HEADS, S]), ALU.mult)\
                        .then_inc(s_dg, 1)
                if p >= 2:
                    normalise_outputs(2, p - 2)
            for hf in range(2):
                dve.wait_ge(s_wo, 4 + hf + 1)
                for m in range(C):
                    ins = nc.vector.scalar_tensor_tensor(h[:, m, half(hf)], ps[4 + 2 * m + hf][:, 0:HALF],
                                                         vector("out_b")[:, m:m + 1], h[:, m, half(hf)],
                                                         ALU.add, ALU.add)
                ins.then_inc(s_h, 1)

            centre(4)
            norm_apply(xn, xc, 10, s_xn)
            dve.wait_ge(s_xn, 10)
            nc.vector.tensor_reduce(pk[:, 2:3], xn[:, :, 0:T], AX.XY, ALU.max, apply_absolute_value=True)\
                .then_inc(s_pk, 1)
            reduce_peaks(2, 1, 7, 2)
            scales_of(2, 1, 7, 2).then_inc(s_sc, 1)
            dve.wait_ge(s_sc, 2)
            link(nc.vector.tensor_scalar(xn[:, :, 0:T], xn[:, :, 0:T], inv[:, 2:3], ROUND, ALU.mult, ALU.add))
            nc.vector.tensor_scalar(xq[:], xn[:, :, 0:T], -ROUND, None, ALU.add).then_inc(s_xq, 1)
            nc.vector.tensor_tensor(sxw[:, 0:1], scale[:, 0:1], scale[:, 2:3], ALU.mult).then_inc(s_sc, 1)
            dve.wait_ge(s_sc, 3)
            nc.vector.tensor_scalar(b1s[:], vector("b1"), sxw[:, 0:1], None, ALU.mult).then_inc(s_sc, 1)
            for u in range(2 * FC):
                hf, ch = u // FC, u % FC
                dve.wait_ge(s_hid, u + 1)
                ins = nc.vector.tensor_reduce(peak[:, u:u + 1], hid[:, ch, half(hf)], AX.X, ALU.max,
                                              apply_absolute_value=True)
            link(ins)
            nc.vector.tensor_reduce(pk[:, 3:4], peak[:], AX.X, ALU.max).then_inc(s_pk, 1)
            reduce_peaks(3, 1, 7, 3)
            scales_of(3, 1, 7, 3).then_inc(s_sc, 1)
            nc.vector.tensor_tensor(sxw[:, 1:2], scale[:, 1:2], scale[:, 3:4], ALU.mult).then_inc(s_sc, 1)
            for ch in range(FC):
                dve.wait_ge(s_hs, ch + 1)
                nc.vector.tensor_scalar(hidq[:, ch, :], hid[:, ch, :], -ROUND, None, ALU.add).then_inc(s_hq, 1)
            dve.wait_ge(s_sc, 6)
            for hf in range(2):
                dve.wait_ge(s_f2, hf + 1)
                for m in range(C):
                    ins = nc.vector.tensor_scalar(tmp[:, m, half(hf)], ps[2 * m + hf][:, 0:HALF],
                                                  vector("b2")[:, m:m + 1], sxw[:, 1:2], ALU.add, ALU.mult)
                link(ins)
                nc.vector.tensor_tensor(x0[:, :, half(hf)], h[:, :, half(hf)], tmp[:, :, half(hf)], ALU.add).then_inc(s_fin, 1)

        @block.tensor
        def _(pe):
            def mm(out_, lhsT, rhs, start, stop):
                return nc.tensor.matmul(out_, lhsT, rhs, start=start, stop=stop, skip_group_check=True)

            def norm(n, mean=True):
                if mean:
                    for hf in range(2):
                        pe.wait_ge(s_h, cent_count(n, hf))
                        for c in range(C):
                            ins = mm(ps[hf][:, 0:HALF], const("mean"), h[:, c, half(hf)], c == 0, c == C - 1)
                        ins.then_inc(s_mean, 1)
                for hf in range(2):
                    pe.wait_ge(s_sq, 2 * n + hf + 1)
                    for c in range(C):
                        ins = mm(ps[2 + hf][:, 0:HALF], const("mean"), sq[:, c, half(hf)], c == 0, c == C - 1)
                    ins.then_inc(s_var, 1)

            def qk_units(a):
                for u in range(NPROJ + 1):
                    n = a * NPROJ + u
                    if u < NPROJ:
                        j, hf = u // 2, u % 2
                        if u >= 2:
                            pe.wait_ge(s_rope, n - 1)
                        for sw in range(2):
                            bank = ps[4 + 2 * (u % 2) + sw][:, 0:HALF]
                            if j == 2 and a == 0:
                                ins = mm(bank, gk_sb[:, sw, :], latent[:, half(hf)], True, True)
                                continue
                            for c in range(C):
                                w = wq_sb[a][:, c, sw, j * P:(j + 1) * P] if j < 2 else lk_sb[:, c, sw, :]
                                ins = mm(bank, w, xn[:, c, half(hf)], c == 0, c == C - 1)
                        ins.then_inc(s_proj, 1)
                    if u >= 1:
                        pe.wait_ge(s_qsq, n)
                        if u >= 3:
                            pe.wait_ge(s_qars, n - 2)
                        mm(ps[(u - 1) % 2][:, 0:HALF], const("headmean"), sq2[:, (u - 1) % 2, :], True, True)\
                            .then_inc(s_qms, 1)
                    if a == 1 and u == 1:
                        peak_rows(0, 2, 3, 2)
                    if a == 1 and u == 3:
                        peak_broadcast(0, 2, 3, 1)

            def row_scores(p):
                if p >= 1:
                    pe.wait_ge(s_mx, p)
                for c in range(C):
                    for gp in range(2):
                        for b in range(2):
                            rows = slice(64 * gp, 64 * gp + 64)
                            at = (2 * p + b) * S
                            ins = mm(ps[4 + gp][64 * b:64 * b + 64, c * 4 * S:(c + 1) * 4 * S],
                                     qt[rows, c, at:at + 64], km[rows, c, :, at:at + S], True, True)
                ins.then_inc(s_sq_s, 1)

            def scores(a, p):
                n = a * PAIRS + p
                b0 = score_bank(a, p)
                if a < 2:
                    if p >= 2:
                        pe.wait_ge(s_e, n - 1)
                    for gp in range(2):
                        mm(ps[b0 + gp][0:ROWS, 0:HALFPOS * S].rearrange("p (h s) -> p h s", s=S),
                           ident_bf[:, 0:ROWS], causal_bf.unsqueeze(1).broadcast_to([P, HALFPOS, S]), True, False)
                else:
                    pe.wait_ge(s_dg, p + 1)
                    if p >= 1:
                        pe.wait_ge(s_e, n)
                    for gp in range(2):
                        mm(ps[b0 + gp][0:ROWS, 0:HALFPOS * S], const("pairs")[:, 0:ROWS],
                           dg[:, p % 2, gp * HALFPOS:(gp + 1) * HALFPOS, :].rearrange("p h s -> p (h s)"),
                           True, False)
                for k in range(0, HALFPOS, 2 if a < 2 else 1):
                    for gp in range(2):
                        for b in range(2):
                            cols = image(2 * p + b)
                            rows = slice(64 * gp, 64 * gp + 64)
                            i, c, _, _ = head_at(a, gp, k)
                            out_ = ps[b0 + gp][64 * b:64 * b + S, :]
                            if a < 2:
                                ins = mm(out_[:, k * S:(k + 2) * S].rearrange("p (c s) -> p c s", c=C),
                                         km[rows, 0, i, cols], qt[rows, :, cols], False, True)
                            else:
                                ins = mm(out_[:, k * S:(k + 1) * S], km[rows, c, i, cols], qt[rows, c, cols],
                                         False, True)
                ins.then_inc(s_s, 1)

            def weighted_values(a, p):
                n = a * PAIRS + p
                pe.wait_ge(s_e, n + 1)
                if p >= 1:
                    pe.wait_ge(s_on, n)
                v = v4 if a < 2 else v16
                for gp in range(2):
                    for k in range(HALFPOS):
                        for b in range(2):
                            rows = slice(64 * b, 64 * b + S)
                            _, _, hd, vh = head_at(a, gp, k)
                            at = (gp * HALFPOS + k) * S
                            ins = mm(ps[b][rows, hd * (HD + 1):(hd + 1) * (HD + 1)],
                                     e[rows, p % 2, at:at + S], v[rows, p, vh, :], True, True)
                ins.then_inc(s_o, 1)

            def transposes(a, p):
                n = a * PAIRS + p
                pe.wait_ge(s_on, n + 1)
                g = p // 2
                if p % 2 == 0 and g >= 2:
                    pe.wait_ge(s_ot, a * (PAIRS // 2) + g - 1)
                for c in range(C):
                    at = ((p % 2) * C + c) * P
                    ins = nc.tensor.transpose(
                        ps[2 + g % 2][:, at:at + ROWS],
                        on[0:ROWS, p % 2, :, :].rearrange("p h d -> p (h d)")[:, c * P:(c + 1) * P],
                        const("ident", ROWS)[:, 0:ROWS])
                ins.then_inc(s_ott, 1)

            def project_out(a, w):
                for hf in range(2):
                    pe.wait_ge(s_ot, a * (PAIRS // 2) + 2 * (hf + 1))
                    for m in range(C):
                        for c in range(C):
                            ins = mm(ps[4 + 2 * m + hf][:, 0:HALF], w[:, c, m * P:(m + 1) * P],
                                     ot[:, c, half(hf)], c == 0, c == C - 1)
                    ins.then_inc(s_wo, 1)

            def attention(a):
                lead = 1 if a == 2 else 0
                for p in range(PAIRS + 2 + lead):
                    if a == 2 and p < PAIRS:
                        row_scores(p)
                    if 0 <= p - lead < PAIRS:
                        scores(a, p - lead)
                    if 0 <= p - lead - 1 < PAIRS:
                        weighted_values(a, p - lead - 1)
                    if 0 <= p - lead - 2:
                        transposes(a, p - lead - 2)

            def peak_rows(k, n, bank, count):
                pe.wait_ge(s_pk, count)
                for q in range(n):
                    ins = mm(ps[bank][0:1, q * P:(q + 1) * P], pk[:, k + q:k + q + 1], const("ident"), True, True)
                ins.then_inc(s_pkt, 1)

            def peak_broadcast(k, n, bank, count):
                pe.wait_ge(s_pk1, count)
                mm(ps[bank][:, 0:n], const("ones", 1), pk1[0:1, k:k + n], True, True).then_inc(s_pkb, 1)

            for k in range(KT):
                pe.wait_ge(s_x[k], 32)
                for hf in range(2):
                    for c in range(C):
                        ins = mm(ps[2 * c + hf][:, 0:HALF], w_lin_sb[:, k, c * P:(c + 1) * P],
                                 patches[:, k, half(hf)], k == 0, k == KT - 1)
                    if k == KT - 1:
                        ins.then_inc(s_tok, 1)

            pe.wait_ge(s_init, 10)
            pe.wait_ge(s_cst, 48)
            norm(0)
            pe.wait_ge(s_attn_w[0], 80)
            for hf in range(2):
                pe.wait_ge(s_xn, hf + 1)
                for c in range(C):
                    ins = mm(ps[2 + hf][0:LAT, 0:HALF], down_sb[:, c, :], xn[:, c, half(hf)], c == 0, c == C - 1)
                ins.then_inc(s_lat, 1)
            pe.wait_ge(s_latv, 2)
            for a in range(2):
                if a == 1:
                    norm(1, mean=False)
                    pe.wait_ge(s_attn_w[1], 64)
                    pe.wait_ge(s_xn, 4)
                qk_units(a)
                for b in range(B):
                    out_ = ps[2][64 * (b % 2):64 * (b % 2) + 64, b // 2 * KVH * HD:(b // 2 + 1) * KVH * HD]
                    if a == 0:
                        ins = mm(out_, latent[:, b * S:b * S + 64], gv_sb[:], True, True)
                    else:
                        for c in range(C):
                            ins = mm(out_, xn[:, c, b * S:b * S + 64], lv_sb[:, c, :], c == 0, c == C - 1)
                ins.then_inc(s_vps, 1)
                pe.wait_ge(s_qk, NPROJ * (a + 1))
                pe.wait_ge(s_v, a + 1)
                if a == 1:
                    pe.wait_ge(s_sc, 1)
                attention(a)
                project_out(a, wo_sb[a])

            norm(2)
            pe.wait_ge(s_moe_w, 48)
            pe.wait_ge(s_xn, 6)
            for t in range(TT):
                for c in range(C):
                    ins = mm(ps[4][:, t * EXPERTS:(t + 1) * EXPERTS], xn[:, c, t * P:(t + 1) * P],
                             gate_sb[:, c, :], c == 0, c == C - 1)
            ins.then_inc(s_log, 1)
            for hf in range(2):
                for m in range(C):
                    mm(ps[2 * m + hf][:, 0:HALF], const("ident"), h[:, m, half(hf)], True, False)
            pe.wait_ge(s_wp, 1)
            for t in range(TT):
                ins = nc.tensor.transpose(ps[5][:].bitcast(bf16)[0:96, t * P:(t + 1) * P], wparts[:, t, :],
                                          ident_bf)
            ins.then_inc(s_wt, 1)
            pe.wait_ge(s_wrow, 1)
            pe.wait_ge(s_xs, 2)

            def three(out_, parts_w, parts_x, start, stop):
                (w_hi, w_lo), (x_hi, x_lo) = parts_w, parts_x
                mm(out_, w_hi, x_hi, start, False)
                mm(out_, w_hi, x_lo, False, False)
                return mm(out_, w_lo, x_hi, False, stop)

            def up_sums(u, i, hf, first=False):
                n = 2 * u + hf
                if hf == 0:
                    pe.wait_ge(s_wsl, u + 1)
                if not first:
                    pe.wait_ge(s_sg, n)
                for c in range(C):
                    cols = slice(c * INNER, (c + 1) * INNER)
                    ins = three(ps[4][:, 0:HALF], (wh[i][:, cols], wl[i][:, cols]),
                                (xh[:, c, half(hf)], xl[:, c, half(hf)]), c == 0, c == C - 1)
                ins.then_inc(s_g, 1)
                if not first:
                    pe.wait_ge(s_act, n)
                for c in range(C):
                    cols = slice(D + c * INNER, D + (c + 1) * INNER)
                    three(ps[5][:, 0:HALF], (wh[i][:, cols], wl[i][:, cols]),
                          (xh[:, c, half(hf)], xl[:, c, half(hf)]), c == 0, c == C - 1)
                sel = select_bf[0:97, bass.ds(u, 1)].broadcast_to([97, P])
                mm(ps[6][:, 0:HALF], sel, wrow[0:97, half(hf)], True, True).then_inc(s_u, 1)

            def down_sums(u, i, hf):
                n = 2 * u + hf
                pe.wait_ge(s_al, n + 1)
                for m in range(C):
                    cols = slice(2 * D + m * P, 2 * D + (m + 1) * P)
                    ins = three(ps[2 * m + hf][:, 0:HALF], (wh[i][:, cols], wl[i][:, cols]),
                                (ah[:, hf, :], al[:, hf, :]), False, False)
                ins.then_inc(s_down, 1)

            up_sums(0, 0, 0, first=True)
            with pe.Fori(0, (UNITS - 1) // NRING) as r:
                for i in range(NRING):
                    u, nxt = r * NRING + i, (i + 1) % NRING
                    up_sums(u, i, 1)
                    down_sums(u, i, 0)
                    up_sums(u + 1, nxt, 0)
                    down_sums(u, i, 1)
            for u in range((UNITS - 1) // NRING * NRING, UNITS):
                i = u % NRING
                up_sums(u, i, 1)
                down_sums(u, i, 0)
                if u + 1 < UNITS:
                    up_sums(u + 1, (i + 1) % NRING, 0)
                down_sums(u, i, 1)
            pe.wait_ge(s_down, 2 * UNITS)
            mm(ps[7][0:1, 0:1], const("ones")[:, 0:1], const("ones")[:, 0:1], True, True).then_inc(s_acc, 1)

            norm(3)
            pe.wait_ge(s_xn, 8)
            for part in range(2):
                for c in range(C):
                    for hf in range(2):
                        bank = ps[4 * (1 - part) + 2 * c + hf][:, 0:HALF]
                        for k in range(C):
                            ins = mm(bank, qkv_sb[:, k, part * D + c * P:part * D + (c + 1) * P],
                                     xn[:, k, half(hf)], k == 0, k == C - 1)
                        ins.then_inc(s_qkps, 1)
            for b in range(4):
                pe.wait_ge(s_qkev, b + 1)
                for q in range(4):
                    at = (4 * b + q) * S
                    for k in range(C):
                        ins = mm(ps[4 + b][64 * (q % 2):64 * (q % 2) + 64, q // 2 * D:(q // 2 + 1) * D],
                                 xn[:, k, at:at + 64], qkv_sb[:, k, 2 * D:3 * D], k == 0, k == C - 1)
                ins.then_inc(s_vps, 1)
            pe.wait_ge(s_kev, 4)
            pe.wait_ge(s_v, 6)
            pe.wait_ge(s_init, 11)
            attention(2)
            project_out(2, outw_sb)

            norm(4)
            peak_rows(2, 1, 7, 3)
            peak_broadcast(2, 1, 7, 2)
            pe.wait_ge(s_wq, 2)
            pe.wait_ge(s_xq, 1)
            for u in range(2 * FC):
                hf, ch = u // FC, u % FC
                if u >= 4:
                    pe.wait_ge(s_hid, u - 3)
                for c in range(C):
                    ins = mm(ps[4 + u % 4][:, 0:HALF], w1q[:, c, ch * P:(ch + 1) * P], xq[:, c, half(hf)],
                             c == 0, c == C - 1)
                ins.then_inc(s_f1, 1)
            peak_rows(3, 1, 7, 4)
            peak_broadcast(3, 1, 7, 3)
            for ch in range(FC):
                pe.wait_ge(s_hq, ch + 1)
                for hf in range(2):
                    for m in range(C):
                        ins = mm(ps[2 * m + hf][:, 0:HALF], w2q[:, ch, m * P:(m + 1) * P],
                                 hidq[:, ch, half(hf)], ch == 0, ch == FC - 1)
                    if ch == FC - 1:
                        ins.then_inc(s_f2, 1)


def constants():
    import numpy as np

    f = np.float32
    c = np.zeros((P, NCONST), f)
    row = np.arange(P)

    def put(name, a):
        lo, hi = CONST_COLS[name]
        c[:, lo:hi] = a

    put("ident", np.eye(P))
    put("mean", 1.0 / D)
    put("headmean", (row[:, None] // HD == row[None, :] // HD) / HD)
    put("ones", 1.0)
    token = row % 64
    real = token < S
    put("pairs", (row[:, None] // 64 == row[None, :] // 64) & real[:, None])
    put("minus_ident", -((token[:, None] == np.arange(S)[None, :]) & real[:, None]).astype(f))
    d = row % HD
    for name, base in (("g", 1000000.0), ("l", 10000.0)):
        inv_freq = f(1.0) / f(base) ** (np.arange(0, HD, 2, dtype=f) / f(HD))
        freqs = np.arange(S, dtype=f)[:, None] * inv_freq[None, :].astype(f)
        put("cos_" + name, np.cos(freqs).astype(f).T[d // 2, :])
        put("sin_" + name, np.sin(freqs).astype(f).T[d // 2, :] * np.where(d % 2 == 0, -1, 1)[:, None])
    put("onehot", (row[:, None] % 64) // HD == np.arange(4)[None, :])
    g = np.arange(GROUPS)
    put("tie", (g[None, :] < g[:, None]).astype(f).reshape(1, 16))
    b = np.zeros((P, NBF), f)
    b[:, 0:P] = np.eye(P)
    b[:, P:P + S] = np.where(real[:, None] & (token[:, None] > np.arange(S)[None, :]), -32768.0, 0.0)
    for u in range(UNITS):
        for part in range(3):
            if u < EXPERTS:
                b[part * EXPERTS + u, P + S + u] = 1.0
        if u >= EXPERTS:
            b[96, P + S + u] = 1.0
    return c, b


def layouts(i):
    import numpy as np

    def chunks(w):
        k, n = w.shape
        return np.ascontiguousarray(w.reshape(k // P, P, n).transpose(1, 0, 2))

    x = i["x"].reshape(B, 3, GRID, PATCH, GRID, PATCH).transpose(1, 3, 5, 0, 2, 4).reshape(KT * P, B, S - 1)
    xp = np.zeros((KT * P, B, S), x.dtype)
    xp[:, :, 1:] = x
    a = {"x": chunks(xp.reshape(KT * P, T)), "w_lin": chunks(i["L0_tok_W_lin"].T)}

    v = np.zeros((P, NVEC), np.float32)

    def put(name, rows):
        lo, hi = VEC_COLS[name]
        v[:, lo:hi] = rows.reshape(P, hi - lo)

    put("pos", chunks(i["L0_tok_position_embeddings"][0].T))
    base = np.concatenate([i["L0_tok_class_token"][0], np.repeat(i["L0_tok_b_lin"][None], S - 1, 0)], 0)
    put("base", chunks(base.T))
    col = lambda w: w.reshape(-1, P).T
    put("norm1", col(i["L0_attn_norm1_w"]))
    put("norm2", col(i["L0_attn_norm2_w"]))
    put("qkv_b", col(i["L1_attn_qkv_b"]))
    put("out_b", col(i["L1_attn_out_b"]))
    put("b1", col(i["L1_ffn_b1"]))
    put("b2", col(i["L1_ffn_b2"]))
    put("gate_bias", np.repeat(i["L0_ffn_gate_bias"][None], P, 0))
    a["vecs"] = v

    c, gp, kv, d = np.meshgrid(np.arange(C), np.arange(2), np.arange(KVH), np.arange(HD), indexing="ij")
    q_col = ((kv * 4 + 2 * c + gp) * HD + d).reshape(-1)
    k_col = (kv * HD + d)[0].reshape(-1)
    swap = lambda at: at ^ 1
    both = lambda w, at: np.ascontiguousarray(np.stack([w[..., at], w[..., swap(at)]], -2))
    a["g_wq"] = both(chunks(i["L0_attn_g_wq"]), q_col)
    a["g_down"] = chunks(i["L0_attn_g_kv_down"])
    a["g_k"] = both(i["L0_attn_g_k_up"], k_col)
    a["g_v"] = i["L0_attn_g_v_up"]
    a["g_wo"] = chunks(i["L0_attn_g_wo"])
    a["l_wq"] = both(chunks(i["L0_attn_l_wq"]), q_col)
    a["l_wk"] = both(chunks(i["L0_attn_l_wk"]), k_col)
    a["l_wv"] = chunks(i["L0_attn_l_wv"])
    a["l_wo"] = chunks(i["L0_attn_l_wo"])
    a["gate_w"] = chunks(i["L0_ffn_gate_w"].T)
    wg = np.concatenate([i["L0_ffn_expert_gate"], i["L0_ffn_shared_gate"].reshape(2, INNER, D)], 0)
    wu = np.concatenate([i["L0_ffn_expert_up"], i["L0_ffn_shared_up"].reshape(2, INNER, D)], 0)
    wd = np.concatenate([i["L0_ffn_expert_down"],
                         i["L0_ffn_shared_down"].reshape(D, 2, INNER).transpose(1, 0, 2)], 0)
    up = lambda w: w.reshape(UNITS, INNER, C, P).transpose(0, 3, 2, 1).reshape(UNITS, P, D)
    a["experts"] = np.concatenate([up(wg), up(wu), wd.transpose(0, 2, 1)], 2)
    a["qkv_w"] = chunks(i["L1_attn_qkv_w"].T)
    a["out_w"] = chunks(i["L1_attn_out_w"].T)
    a["w1"] = chunks(i["L1_ffn_w1"].T).reshape(P, C * FF)
    a["w2"] = chunks(i["L1_ffn_w2"].T).reshape(P, FC * D)
    return {k: np.ascontiguousarray(w) for k, w in a.items()}


_ORDER = ["x", "w_lin", "consts", "consts_bf", "vecs", "g_wq", "g_down", "g_k", "g_v", "g_wo", "l_wq", "l_wk",
          "l_wv", "l_wo", "gate_w", "experts", "qkv_w", "out_w", "w1", "w2"]


def kernel(**inputs):
    import numpy as np
    import concourse.bacc as bacc
    from concourse.bass_utils import run_bass_kernel_spmd

    arrays = layouts({k: np.asarray(v) for k, v in inputs.items()})
    arrays["consts"], arrays["consts_bf"] = constants()
    nc = bacc.Bacc("TRN2", target_bir_lowering=False, num_devices=1)
    args = [nc.dram_tensor(f"in_{k}", arrays[k].shape, mybir.dt.from_np(arrays[k].dtype), kind="ExternalInput").ap()
            for k in _ORDER]
    out = nc.dram_tensor("out", (P, C, T), mybir.dt.float32, kind="ExternalOutput").ap()
    program(nc, *args, out)
    r = run_bass_kernel_spmd(nc, [{f"in_{k}": arrays[k] for k in _ORDER}], core_ids=[0])
    got = r.results[0]["out"]
    return np.ascontiguousarray(got.transpose(2, 1, 0).reshape(B, S, D))
```

```python
from contextlib import ExitStack

import concourse.bass as bass
from concourse import mybir

B = 16
PATCH, GRID = 16, 6
S = GRID * GRID + 1
T = B * S
D = 256
P = 128
C = D // P
KT = 3 * PATCH * PATCH // P
HEADS, KVH, HD = 16, 4, 16
LAT = 64
HALF = T // 2
HB = B // 2
PAIRS = B // 2
EP = 64
ROWS = 64 + S
TP = 640
HALFPOS = HEADS // 2
G4 = HEADS // KVH
VP = 2 * HD
EC = HEADS * S
EXPERTS, TOPK, GROUPS, PER_GROUP = 32, 8, 4, 8
UNITS = EXPERTS + 2
INNER = 128
EW = 3 * D
TT = 5
FF = 1024
FC = FF // P
ROUTED_SCALING = 2.5
LN_EPS, RMS_EPS = 1e-5, 1e-6
QK_UNITS = ((0, 0), (1, 0), (2, 0), (2, 1), (0, 1), (1, 1))
ACT_VARIANTS = 5
QP, MIN_RANGE = 127.0, 1e-6
ROUND = 1.5 * 2.0 ** 23

CONST_COLS, VEC_COLS = {}, {}


def _columns(table, widths):
    at = 0
    for name, width in widths:
        table[name] = (at, at + width)
        at += width
    return at


NCONST = _columns(CONST_COLS, [
    ("ident", P), ("mean", P), ("headmean", P), ("ones", P), ("pairs", P), ("pair_ones", VP), ("minus_ident", S),
    ("cos_g", S), ("sin_g", S), ("cos_l", S), ("sin_l", S), ("onehot8", 8),
    ("tie", 16)])
NVEC = _columns(VEC_COLS, [
    ("pos", C * S), ("base", C * S), ("norm1", C), ("norm2", C), ("qkv_b", 6), ("out_b", C),
    ("b1", FC), ("b2", C), ("gate_bias", EXPERTS)])


NBF = P + S + UNITS


def program(nc, x, w_lin, consts, consts_bf, vecs, g_wq, g_down, g_k, g_v, g_wo, l_wq, l_wk, l_wv, l_wo,
            gate_w, experts, qkv_w, out_w, w1, w2, out):
    f32, f32r, bf16 = mybir.dt.float32, mybir.dt.float32r, mybir.dt.bfloat16
    ALU, ACT, AX = mybir.AluOpType, mybir.ActivationFunctionType, mybir.AxisListType

    with ExitStack() as ctx:
        def sb(name, shape, dt=f32):
            return ctx.enter_context(nc.sbuf_tensor(name, shape, dt))

        def sem(name):
            return ctx.enter_context(nc.semaphore(name))

        region = sb("region", [P, KT * (T + D)])
        patches = region[:, 0:KT * T].rearrange("p (k t) -> p k t", k=KT)
        w_lin_sb = region[:, KT * T:KT * (T + D)].rearrange("p (k d) -> p k d", k=KT)
        hid = region[:, 0:FC * T].rearrange("p (c t) -> p c t", c=FC)
        cst = sb("cst", [P, NCONST])
        cstb = sb("cstb", [P, NBF], bf16)
        vec = sb("vec", [P, NVEC])
        wq_sb = [sb(f"wq_sb{a}", [P, C, 2, D]) for a in range(2)]
        down_sb = sb("down_sb", [P, C, LAT])
        gk_sb = sb("gk_sb", [LAT, 2, P])
        gv_sb = sb("gv_sb", [LAT, KVH * HD])
        lk_sb = sb("lk_sb", [P, C, 2, P])
        lv_sb = sb("lv_sb", [P, C, KVH * HD])
        V4 = PAIRS * KVH * VP
        OT = G4 * PAIRS * S
        wo_sb = region[:, OT + V4:OT + V4 + 2 * G4 * D].rearrange("p (b g d) -> p b g d", b=2, g=G4)
        gate_sb = sb("gate_sb", [P, C, EXPERTS])
        qkv_sb = sb("qkv_sb", [P, C, 3 * D])
        outw_sb = sb("outw_sb", [P, C, D])
        w1_sb = sb("w1_sb", [P, C * FF])
        w2_sb = sb("w2_sb", [P, FC * D])
        w1q = sb("w1q", [P, C, FF], bf16)
        w2q = sb("w2q", [P, FC, D], bf16)

        posb = sb("posb", [P, C, S])
        h = sb("h", [P, C, T])
        xc = sb("xc", [P, C, T])
        sq = sb("sq", [P, C, T])
        x0 = sb("x0", [P, C, T])
        xn = sb("xn", [P, C, TP])
        ars = sb("ars", [P, T])
        ars0 = sb("ars0", [P, T])
        var = sb("var", [P, T])
        nt = sb("nt", [P, T])
        latent = sb("latent", [LAT, TP])
        qt = sb("qt", [P, C, TP])
        km = sb("km", [P, C, 4, TP])
        PAIRCOLS = C * 8 * 2 * S
        km_flat = km[:].rearrange("p c i t -> p (c i t)")
        kvar, qvar = (km_flat[:, j * 2 * PAIRCOLS:(j + 1) * 2 * PAIRCOLS]
                      .rearrange("p (k c g t) -> p k c g t", k=2, c=C, g=8) for j in range(2))
        ot4 = region[:, 0:OT].rearrange("p (g t) -> p g t", g=G4)
        v4 = region[:, OT:OT + V4].rearrange("p (q h b d) -> p q h b d", q=PAIRS, h=KVH, b=2)
        V16 = PAIRS * HEADS * 2 * (HD + 1)
        v16 = region[:, 0:V16].rearrange("p (q h b d) -> p q h b d", q=PAIRS, h=HEADS, b=2)
        ra = sb("ra", [P, 2, HALF])
        rb = sb("rb", [P, 2, HALF])
        rt = sb("rt", [P, 2, HALF])
        sq2 = sb("sq2", [P, 2, HALF])
        rs = sb("rs", [P, 2, HALF])
        rn = sb("rn", [P, HALF])
        e = sb("e", [P, 2, EC + EP - S])
        on = sb("on", [P, 2, 2, P])
        rden = sb("rden", [P, 2, HEADS])
        mx = sb("mx", [P, 2, HEADS])
        kt = xc
        ot = sb("ot", [P, C, T])
        tmp = sq

        sig = sb("sig", [P, TT, EXPERTS])
        choice = sb("choice", [P, TT, EXPERTS])
        masked = sb("masked", [P, TT, EXPERTS])
        repl = sb("repl", [P, TT, EXPERTS])
        wts = sb("wts", [P, TT, EXPERTS])
        wres = sb("wres", [P, TT, EXPERTS])
        top = sb("top", [P, TT, GROUPS, 8])
        gsum = sb("gsum", [P, TT, GROUPS])
        grank = sb("grank", [P, TT, GROUPS])
        gcmp = sb("gcmp", [P, TT, GROUPS, GROUPS])
        geq = sb("geq", [P, TT, GROUPS, GROUPS])
        wsum = sb("wsum", [P, TT])
        wparts = sb("wparts", [P, TT, 3 * EXPERTS], bf16)
        wrow = sb("wrow", [P, TT * P], bf16)

        xh = sb("xh", [P, C, T], f32r)
        xl = sb("xl", [P, C, T], f32r)
        dg = xl[:].rearrange("p c t -> p (c t)").rearrange("p (k h s) -> p k h s", k=2, h=HEADS)
        NRING = 4
        ring_all = km[:].rearrange("p c i t -> p (c i t)")
        ring = [ring_all[:, i * EW:(i + 1) * EW] for i in range(NRING)]
        split_all = sb("split_all", [P, 2 * NRING * EW], f32r)
        wh = [split_all[:, i * EW:(i + 1) * EW] for i in range(NRING)]
        wl = [split_all[:, (NRING + i) * EW:(NRING + i + 1) * EW] for i in range(NRING)]
        pairs_r = split_all[:, 0:P]
        sg, gu, act = ra, rb, rt
        ah = sb("ah", [P, 2, HALF], f32r)
        al = sb("al", [P, 2, HALF], f32r)

        hidq = km[:].rearrange("p c i t -> p (c i t)").bitcast(bf16)[:, 0:FC * T].rearrange("p (c t) -> p c t", c=FC)
        xq = sq[:].rearrange("p c t -> p (c t)").bitcast(bf16)[:, 0:C * T].rearrange("p (c t) -> p c t", c=C)
        peak = sb("peak", [P, 2 * FC])
        pk = sb("pk", [P, 4])
        pk1 = sb("pk1", [1, 4])
        scale = sb("scale", [P, 4])
        inv = sb("inv", [P, 4])
        sxw = sb("sxw", [P, 2])
        b1s = sb("b1s", [P, FC])
        eps = sb("eps", [P, 4])
        spare = sb("spare", [P, 16])
        rc = sb("rc", [P, G4 * S])

        ps = [ctx.enter_context(nc.psum_tensor(f"bank{i}", [P, 512], f32)) for i in range(8)]

        def const(name, rows=P):
            a, b = CONST_COLS[name]
            return cst[0:rows, a:b]

        def vector(name):
            a, b = VEC_COLS[name]
            return vec[:, a:b]

        ident_bf = cstb[:, 0:P]
        causal_bf = cstb[:, P:P + S]
        select_bf = cstb[:, P + S:P + S + UNITS]

        def half(hf):
            return slice(hf * HALF, (hf + 1) * HALF)

        def image(b):
            return slice(b * S, (b + 1) * S)

        s_x = [sem(f"patches_loaded{k}") for k in range(KT)]
        s_cst = sem("constants_loaded")
        s_attn_w = [sem(f"attention_weights_loaded{a}") for a in range(2)]
        s_wo_w = sem("output_weights_loaded")
        s_ffw = sem("ffn_weights_loaded")
        s_moe_w = sem("router_and_last_attention_weights_loaded")
        s_ring = [sem(f"expert_loaded{i}") for i in range(NRING)]
        s_init = sem("buffers_initialised")
        s_tok = sem("embedding_summed")
        s_h = sem("stream_ready")
        s_mean = sem("mean_summed")
        s_cent = sem("tokens_centred")
        s_sq = sem("squares_ready")
        s_var = sem("variance_summed")
        s_ars = sem("table_rsqrt_ready")
        s_xn = sem("normalised_ready")
        s_x0 = sem("attention_stream_ready")
        s_lat = sem("latent_summed")
        s_latv = sem("latent_copied")
        s_proj = sem("qk_projected")
        s_rope = sem("rope_products_ready")
        s_rsum = sem("rope_summed")
        s_qsq = sem("qk_squares_ready")
        s_qms = sem("qk_mean_square_summed")
        s_qars = sem("qk_table_rsqrt_ready")
        s_qk = sem("qk_ready")
        s_kn = sem("keys_normalised")
        s_km = sem("key_variants_ready")
        s_vps = sem("values_projected")
        s_v = sem("values_copied")
        s_s = sem("scores_summed")
        s_e = sem("exponentials_ready")
        s_o = sem("outputs_summed")
        s_on = sem("outputs_normalised")
        s_ott = sem("outputs_transposed")
        s_ot = sem("outputs_copied")
        s_wo = sem("attention_projected")
        s_log = sem("router_logits_summed")
        s_sig = sem("router_scores_ready")
        s_wp = sem("weight_parts_ready")
        s_wt = sem("weight_parts_transposed")
        s_wrow = sem("weight_rows_ready")
        s_xs = sem("tokens_split")
        s_wsh = sem("expert_high_parts_ready")
        s_wsl = sem("expert_low_parts_ready")
        s_g = sem("gate_summed")
        s_u = sem("up_and_weight_summed")
        s_sg = sem("silu_ready")
        s_act = sem("weighted_activation_ready")
        s_ah = sem("activation_high_part_ready")
        s_al = sem("activation_low_part_ready")
        s_down = sem("down_summed")
        s_acc = sem("experts_all_summed")
        s_qkps = sem("last_qk_projected")
        s_qkev = sem("last_q_copied")
        s_kev = sem("last_k_copied")
        s_kmr = sem("pair_blocks_rounded")
        s_kvar = sem("last_key_variants_ready")
        s_qvar = sem("last_query_variants_ready")
        s_sq_s = sem("row_scores_summed")
        s_mx = sem("row_maxima_read")
        s_dg = sem("maxima_on_diagonals")
        s_pk = sem("peaks_ready")
        s_pkt = sem("peaks_in_a_row")
        s_pk1 = sem("peak_reduced")
        s_pkb = sem("peak_broadcast")
        s_sc = sem("scales_ready")
        s_wqt = sem("ffn_weight_scaled")
        s_wq = sem("ffn_weights_quantised")
        s_xq = sem("ffn_input_quantised")
        s_f1 = sem("ffn_first_summed")
        s_hid = sem("hidden_ready")
        s_hpk = sem("hidden_peak_read")
        s_hs = sem("hidden_scaled")
        s_hq = sem("hidden_quantised")
        s_f2 = sem("ffn_second_summed")
        s_fin = sem("result_ready")
        s_out = sem("result_stored")
        s_dve = sem("vector_step")
        s_act_own = sem("scalar_step")
        s_mulc = sem("expert_product_ready")
        s_pool_own = sem("pool_step")

        block = ctx.enter_context(nc.Block())
        NPROJ = 3 * 2

        def cent_count(n, hf):
            return 2 * {0: 0, 2: 1, 3: 2, 4: 3}[n] + hf + 1

        def score_bank(a, p):
            return 4 + 2 * (p % 2) if a < 2 else 6

        def variants(engine, dst, src, p, c):
            shape = [P, 8, 2 * S]
            return engine.tensor_tensor(dst[:, p % 2, c, :, :],
                                        src[:, c, 2 * p * S:2 * (p + 1) * S].unsqueeze(1).broadcast_to(shape),
                                        const("onehot8").unsqueeze(2).broadcast_to(shape), ALU.mult)

        @block.sync
        def _(sp):
            for k in range(KT):
                sp.dma_start(patches[:, k, :], x[:, k, :]).then_inc(s_x[k], 16)
                sp.dma_start(w_lin_sb[:, k, :], w_lin[:, k, :]).then_inc(s_x[k], 16)
            sp.dma_start(wq_sb[0][:], g_wq).then_inc(s_attn_w[0], 16)
            sp.dma_start(wq_sb[1][:], l_wq).then_inc(s_attn_w[1], 16)
            sp.dma_start(lk_sb[:], l_wk).then_inc(s_attn_w[1], 16)
            sp.dma_start(lv_sb[:], l_wv).then_inc(s_attn_w[1], 16)
            sp.dma_start(w1_sb[:], w1).then_inc(s_ffw, 16)
            sp.dma_start(w2_sb[:], w2).then_inc(s_ffw, 16)
            sp.wait_ge(s_tok, 2)
            sp.dma_start(wo_sb, g_wo).then_inc(s_wo_w, 16)
            sp.dma_start(gate_sb[:], gate_w).then_inc(s_moe_w, 16)
            sp.dma_start(qkv_sb[:], qkv_w).then_inc(s_moe_w, 16)
            sp.dma_start(outw_sb[:], out_w).then_inc(s_moe_w, 16)
            sp.wait_ge(s_wo, 2)
            sp.dma_start(wo_sb, l_wo).then_inc(s_wo_w, 16)
            sp.wait_ge(s_s, 2 * PAIRS)
            for i in range(NRING):
                sp.dma_start(ring[i], experts[i, :, :]).then_inc(s_ring[i], 16)
            with sp.Fori(1, UNITS // NRING) as r:
                for i in range(NRING):
                    sp.wait_ge(s_wsh, r * NRING + (i + 1 - NRING))
                    sp.wait_ge(s_wsl, r * NRING + (i + 1 - NRING))
                    sp.dma_start(ring[i],
                                 experts[bass.ds(r * NRING + i, 1), :, :].rearrange("a p n -> (a p) n"))\
                        .then_inc(s_ring[i], 16)
            for u in range(UNITS - UNITS % NRING, UNITS):
                i = u % NRING
                sp.wait_ge(s_wsh, u + 1 - NRING)
                sp.wait_ge(s_wsl, u + 1 - NRING)
                sp.dma_start(ring[i], experts[u, :, :]).then_inc(s_ring[i], 16)
            for hf in range(2):
                sp.wait_ge(s_fin, hf + 1)
                sp.dma_start(out[:, :, half(hf)], x0[:, :, half(hf)]).then_inc(s_out, 16)
            sp.wait_ge(s_out, 32)

        @block.gpsimd
        def _(pool):
            nc.gpsimd.memset(eps[:, 0:1], LN_EPS).then_inc(s_init, 1)
            nc.gpsimd.memset(eps[:, 1:2], RMS_EPS * LN_EPS / (1.0 + RMS_EPS)).then_inc(s_init, 1)
            nc.gpsimd.memset(eps[:, 2:3], RMS_EPS).then_inc(s_init, 1)
            nc.gpsimd.memset(xn[:, :, T:TP], 0.0).then_inc(s_init, 1)
            nc.gpsimd.memset(latent[:, T:TP], 0.0).then_inc(s_init, 1)
            nc.gpsimd.memset(qt[:, :, T:TP], 0.0).then_inc(s_init, 1)
            nc.gpsimd.memset(e[:, :, EC:], 1.0).then_inc(s_init, 1)

            def rope_sums(a):
                for u in range(NPROJ):
                    n = a * NPROJ + u
                    pool.wait_ge(s_rope, n + 1)
                    if n >= 2:
                        pool.wait_ge(s_qk, n - 1)
                    nc.gpsimd.tensor_tensor(rt[:, u % 2, :], ra[:, u % 2, :], rb[:, u % 2, :], ALU.add)\
                        .then_inc(s_rsum, 1)

            pool.wait_ge(s_tok, 2)
            nc.gpsimd.memset(region[:, OT:OT + V4], 0.0).then_inc(s_init, 1)
            rope_sums(0)
            rope_sums(1)
            pool.wait_ge(s_sc, 1)
            for k, (w, wq_) in enumerate(((w1_sb, w1q), (w2_sb, w2q))):
                nc.gpsimd.tensor_scalar(w[:], w[:], inv[:, k:k + 1], ROUND, ALU.mult, ALU.add).then_inc(s_wqt, 1)
            for k, (w, wq_) in enumerate(((w1_sb, w1q), (w2_sb, w2q))):
                pool.wait_ge(s_wqt, k + 1)
                nc.gpsimd.tensor_scalar(wq_[:].rearrange("p c n -> p (c n)"), w[:], 1.0, -ROUND, ALU.mult, ALU.add)\
                    .then_inc(s_wq, 1)
            pool.wait_ge(s_wo, 4)
            nc.gpsimd.memset(region[:, 0:V16], 0.0).then_inc(s_init, 1)
            pool.wait_ge(s_init, 11)
            for b in range(2):
                nc.gpsimd.memset(v16[64 * b:64 * b + S, :, :, b, HD:HD + 1], 1.0).then_inc(s_init, 1)
            pool.wait_ge(s_init, 13)
            def low_part(u, i):
                pool.wait_ge(s_wsh, u + 1)
                nc.gpsimd.tensor_tensor(wl[i], ring[i], wh[i].bitcast(f32), ALU.subtract)\
                    .then_inc(s_wsl, 1)

            with pool.Fori(0, UNITS // NRING) as r:
                for i in range(NRING):
                    low_part(r * NRING + i, i)
            for u in range(UNITS - UNITS % NRING, UNITS):
                low_part(u, u % NRING)

            pool.wait_ge(s_qkev, 4)
            for p in range(PAIRS):
                if p >= 2:
                    pool.wait_ge(s_s, 2 * PAIRS + p - 1)
                for c in range(C):
                    ins = variants(nc.gpsimd, qvar, qt, p, c)
                    if c == C - 1:
                        ins.then_inc(s_qvar, 1)

        @block.scalar
        def _(act_e):
            own = [0]

            def link(ins):
                own[0] += 1
                ins.then_inc(s_act_own, 1)
                act_e.wait_ge(s_act_own, own[0])

            act_e.dma_start(cst[:], consts).then_inc(s_cst, 16)
            act_e.dma_start(vec[:], vecs).then_inc(s_cst, 16)
            act_e.dma_start(nt[:, 0:NBF], consts_bf).then_inc(s_cst, 16)
            act_e.dma_start(down_sb[:], g_down).then_inc(s_attn_w[0], 16)
            act_e.dma_start(gk_sb[:], g_k).then_inc(s_attn_w[0], 16)
            act_e.dma_start(gv_sb[:], g_v).then_inc(s_attn_w[0], 16)
            act_e.wait_ge(s_init, 9)
            act_e.wait_ge(s_cst, 48)

            warmed = [0]

            def load_table(func):
                k = warmed[0]
                warmed[0] += 1
                nc.scalar.activation(spare[:, k:k + 1], eps[:, 0:1], func)

            def norm(n, mean=True, eps_at=0):
                for hf in range(2):
                    if mean:
                        act_e.wait_ge(s_cent, cent_count(n, hf))
                        src = xc
                    else:
                        act_e.wait_ge(s_x0, 2 + hf + 1)
                        src = x0
                    nc.scalar.activation(sq[:, :, half(hf)], src[:, :, half(hf)], ACT.Square).then_inc(s_sq, 1)
                load_table(ACT.Abs_reciprocal_sqrt)
                for hf in range(2):
                    act_e.wait_ge(s_var, 2 * n + hf + 1)
                    nc.scalar.activation(ars[:, half(hf)], ps[2 + hf][:, 0:HALF], ACT.Abs_reciprocal_sqrt,
                                         bias=eps[:, eps_at:eps_at + 1]).then_inc(s_ars, 1)

            def layer_norm_scale(hf):
                act_e.wait_ge(s_xn, hf + 1)
                nc.scalar.activation(var[:, half(hf)], ps[2 + hf][:, 0:HALF], ACT.Copy)
                nc.scalar.activation(ars0[:, half(hf)], ps[2 + hf][:, 0:HALF], ACT.Abs_reciprocal_sqrt,
                                     bias=eps[:, 0:1]).then_inc(s_ars, 1)

            def latent_copied(hf):
                act_e.wait_ge(s_lat, hf + 1)
                nc.scalar.activation(latent[:, half(hf)], ps[2 + hf][0:LAT, 0:HALF], ACT.Copy).then_inc(s_latv, 1)

            def key_variants(a, hf):
                act_e.wait_ge(s_kn, 2 * a + hf + 1)
                if a == 1:
                    act_e.wait_ge(s_s, PAIRS)
                for g in range(ACT_VARIANTS):
                    ins = nc.scalar.activation(km[:, g // 4, g % 4, half(hf)], sq[:, 0, half(hf)], ACT.Copy,
                                               scale=const("onehot8")[:, g:g + 1])
                ins.then_inc(s_km, 1)

            def qk_units(a):
                for u in range(NPROJ + 1):
                    n = a * NPROJ + u
                    if a == 0 and u < 2:
                        layer_norm_scale(u)
                    if a == 0 and 1 <= u < 3:
                        latent_copied(u - 1)
                    if u < NPROJ:
                        act_e.wait_ge(s_proj, n + 1)
                        nc.scalar.activation(sq2[:, u % 2, :], ps[4 + 2 * (u % 2)][:, 0:HALF], ACT.Square)\
                            .then_inc(s_qsq, 1)
                    if u >= 1:
                        m = n - 1
                        act_e.wait_ge(s_qms, m + 1)
                        if m >= 2:
                            act_e.wait_ge(s_qk, m - 1)
                        nc.scalar.activation(rs[:, (u - 1) % 2, :], ps[(u - 1) % 2][:, 0:HALF],
                                             ACT.Abs_reciprocal_sqrt, bias=eps[:, 2:3]).then_inc(s_qars, 1)
                    if u >= 2 and QK_UNITS[u - 2][0] == 2:
                        key_variants(a, QK_UNITS[u - 2][1])

            def outputs_copied(g):
                act_e.wait_ge(s_ott, 2 * g + 2)
                src = ps[2 + g % 2][:].rearrange("p (i w) -> p i w", i=4)
                for c in range(C):
                    dst = ot[:, c, 4 * g * S:4 * (g + 1) * S].rearrange("p (i s) -> p i s", i=4)
                    ins = nc.scalar.activation(dst, src[:, :, 64 * c:64 * c + S], ACT.Identity,
                                               bias=vector("qkv_b")[:, 4 + c:5 + c])
                ins.then_inc(s_ot, 1)

            def attention(a):
                for p in range(PAIRS + 2):
                    if p < PAIRS:
                        n = a * PAIRS + p
                        act_e.wait_ge(s_s, n + 1)
                        if n >= 2:
                            act_e.wait_ge(s_o, n - 1)
                        sb0 = score_bank(a, p)
                        for k in range(2):
                            ins = nc.scalar.activation(e[0:ROWS, p % 2, k * HALFPOS * S:(k + 1) * HALFPOS * S],
                                                       ps[sb0 + k][0:ROWS, 0:HALFPOS * S], ACT.Exp,
                                                       scale=HD ** -0.5)
                        ins.then_inc(s_e, 1)
                    if a == 2 and p >= 4 and p % 2 == 0:
                        outputs_copied((p - 4) // 2)
                if a == 2:
                    outputs_copied(PAIRS // 2 - 1)

            norm(0, eps_at=1)
            for a in range(2):
                if a == 1:
                    norm(1, mean=False, eps_at=2)
                qk_units(a)
                load_table(ACT.Exp)
                act_e.wait_ge(s_vps, a + 1)
                act_e.wait_ge(s_init, 10)
                for b in range(2):
                    rows = slice(64 * b, 64 * b + S)
                    ins = nc.scalar.activation(v4[rows, :, :, b, :],
                                               ps[2][rows, :].rearrange("p (q h d) -> p q h d", q=PAIRS, h=KVH),
                                               ACT.Copy)
                ins.then_inc(s_v, 1)
                attention(a)

            norm(2)
            load_table(ACT.Sigmoid)
            act_e.wait_ge(s_log, 1)
            nc.scalar.activation(sig[:].rearrange("p t n -> p (t n)"), ps[4][:, 0:TT * EXPERTS], ACT.Sigmoid)\
                .then_inc(s_sig, 1)
            nc.scalar.activation(xh[:], xn[:, :, 0:T], ACT.Copy).then_inc(s_xs, 1)
            load_table(ACT.Silu)

            def high_part(u, i, r, reused=True):
                act_e.wait_ge(s_ring[i], r * 16 + 16)
                if reused:
                    act_e.wait_ge(s_down, 2 * (u - NRING + 1))
                    act_e.wait_ge(s_wsl, u - NRING + 1)
                nc.scalar.activation(wh[i], ring[i], ACT.Copy).then_inc(s_wsh, 1)

            def expert_unit(n, j):
                act_e.wait_ge(s_g, n + 1)
                nc.scalar.activation(sg[:, j, :], ps[4][:, 0:HALF], ACT.Silu).then_inc(s_sg, 1)
                act_e.wait_ge(s_act, n + 1)
                nc.scalar.activation(ah[:, j, :], act[:, j, :], ACT.Copy).then_inc(s_ah, 1)

            AHEAD = 2
            for i in range(AHEAD):
                high_part(i, i, 0, False)
            for i in range(NRING):
                expert_unit(2 * i, 0)
                high_part(i + AHEAD, (i + AHEAD) % NRING, (i + AHEAD) // NRING, i + AHEAD >= NRING)
                expert_unit(2 * i + 1, 1)
            with act_e.Fori(1, (UNITS - AHEAD) // NRING) as r:
                for i in range(NRING):
                    u = r * NRING + i
                    expert_unit(2 * u, 0)
                    high_part(u + AHEAD, (i + AHEAD) % NRING, r + (i + AHEAD) // NRING)
                    expert_unit(2 * u + 1, 1)
            for u in range(UNITS - AHEAD, UNITS):
                expert_unit(2 * u, 0)
                expert_unit(2 * u + 1, 1)
            act_e.wait_ge(s_acc, 1)
            for hf in range(2):
                for m in range(C):
                    ins = nc.scalar.activation(h[:, m, half(hf)], ps[2 * m + hf][:, 0:HALF], ACT.Copy)
                ins.then_inc(s_h, 1)

            norm(3)
            load_table(ACT.Exp)
            for c in range(C):
                for hf in range(2):
                    act_e.wait_ge(s_qkps, 2 * c + hf + 1)
                    nc.scalar.activation(qt[:, c, half(hf)], ps[4 + 2 * c + hf][:, 0:HALF], ACT.Identity,
                                         bias=vector("qkv_b")[:, c:c + 1]).then_inc(s_qkev, 1)
            for b in range(4):
                act_e.wait_ge(s_vps, 2 + b + 1)
                if b == 0:
                    act_e.wait_ge(s_init, 13)
                for j in range(2):
                    rows = slice(64 * j, 64 * j + S)
                    ins = nc.scalar.activation(v16[rows, 2 * b:2 * b + 2, :, j, 0:HD],
                                               ps[4 + b][rows, :].rearrange("p (q h d) -> p q h d", q=2, h=HEADS),
                                               ACT.Copy)
                ins.then_inc(s_v, 1)
            attention(2)

            norm(4)
            load_table(ACT.Gelu)
            for u in range(2 * FC):
                hf, ch = u // FC, u % FC
                act_e.wait_ge(s_f1, u + 1)
                if u == 0:
                    act_e.wait_ge(s_sc, 4)
                nc.scalar.activation(hid[:, ch, half(hf)], ps[4 + u % 4][:, 0:HALF], ACT.Gelu,
                                     bias=b1s[:, ch:ch + 1], scale=sxw[:, 0:1]).then_inc(s_hid, 1)
            act_e.wait_ge(s_sc, 5)
            for ch in range(FC):
                nc.scalar.activation(hid[:, ch, :], hid[:, ch, :], ACT.Copy, bias=ROUND, scale=inv[:, 3:4])\
                    .then_inc(s_hs, 1)

        @block.vector
        def _(dve):
            own = [0]

            def link(ins):
                own[0] += 1
                ins.then_inc(s_dve, 1)
                dve.wait_ge(s_dve, own[0])

            def bc(ap, dims):
                return ap.broadcast_to(dims)

            def newton(y, v, t, eps_at, factor=1.0):
                link(nc.vector.scalar_tensor_tensor(t, v, eps[:, eps_at:eps_at + 1], y, ALU.add, ALU.mult))
                link(nc.vector.scalar_tensor_tensor(t, t, -0.5 * factor, y, ALU.mult, ALU.mult))
                link(nc.vector.scalar_tensor_tensor(y, t, 1.5 * factor, y, ALU.add, ALU.mult))

            def centre(n):
                for hf in range(2):
                    dve.wait_ge(s_mean, cent_count(n, hf))
                    nc.vector.tensor_tensor(xc[:, :, half(hf)], h[:, :, half(hf)],
                                            bc(ps[hf][:, 0:HALF].unsqueeze(1), [P, C, HALF]), ALU.subtract)\
                        .then_inc(s_cent, 1)

            def scaled(dst, src, hf, by, weight=None):
                last = None
                for c in range(C):
                    if weight is None:
                        last = nc.vector.tensor_tensor(dst[:, c, half(hf)], src[:, c, half(hf)],
                                                       by[:, half(hf)], ALU.mult)
                    else:
                        last = nc.vector.scalar_tensor_tensor(dst[:, c, half(hf)], src[:, c, half(hf)],
                                                              weight[:, c:c + 1], by[:, half(hf)],
                                                              ALU.mult, ALU.mult)
                return last

            def norm_apply(dst, src, count, sig_to, weight=None, eps_at=0, factor=1.0):
                for hf in range(2):
                    dve.wait_ge(s_ars, count + hf + 1)
                    newton(ars[:, half(hf)], ps[2 + hf][:, 0:HALF], nt[:, half(hf)], eps_at, factor)
                    scaled(dst, src, hf, ars, weight).then_inc(sig_to, 1)

            def layer_norm_stream():
                for hf in range(2):
                    dve.wait_ge(s_ars, 2 + hf + 1)
                    newton(ars0[:, half(hf)], var[:, half(hf)], nt[:, half(hf)], 0)
                    scaled(x0, xc, hf, ars0).then_inc(s_x0, 1)

            def reduce_peaks(k, n, bank, count):
                dve.wait_ge(s_pkt, count)
                nc.vector.tensor_reduce(pk1[0:1, k:k + n], ps[bank][0:1, 0:n * P].rearrange("p (n c) -> p n c", n=n),
                                        AX.X, ALU.max).then_inc(s_pk1, 1)

            def scales_of(k, n, bank, count):
                dve.wait_ge(s_pkb, count)
                link(nc.vector.tensor_scalar(scale[:, k:k + n], ps[bank][:, 0:n], MIN_RANGE, 1.0 / QP,
                                             ALU.max, ALU.mult))
                return nc.vector.reciprocal(inv[:, k:k + n], scale[:, k:k + n])

            def qk_units(a):
                names = (("cos_g", "sin_g"), ("cos_l", "sin_l"))[a]
                cos, sin = (bc(const(x).unsqueeze(1), [P, HB, S]) for x in names)

                def images(ap):
                    return ap.rearrange("p (b s) -> p b s", s=S)

                for u in range(NPROJ + 1):
                    n = a * NPROJ + u
                    if u < NPROJ:
                        dve.wait_ge(s_proj, n + 1)
                        b0 = 4 + 2 * (u % 2)
                        if n >= 2:
                            dve.wait_ge(s_rsum, n - 1)
                        nc.vector.tensor_tensor(images(rb[:, u % 2, :]), images(ps[b0 + 1][:, 0:HALF]), sin,
                                                ALU.mult)
                        dve.wait_ge(s_qsq, n + 1)
                        nc.vector.tensor_tensor(images(ra[:, u % 2, :]), images(ps[b0][:, 0:HALF]), cos,
                                                ALU.mult).then_inc(s_rope, 1)
                    if u >= 1:
                        w, k = u - 1, (u - 1) % 2
                        dve.wait_ge(s_qars, n)
                        newton(rs[:, k, :], ps[k][:, 0:HALF], rn[:], 2)
                        dve.wait_ge(s_rsum, n)
                        j, hf = QK_UNITS[w]
                        if j < 2:
                            ins = nc.vector.tensor_tensor(qt[:, j, half(hf)], rt[:, k, :], rs[:, k, :], ALU.mult)
                        else:
                            nc.vector.tensor_tensor(sq[:, 0, half(hf)], rt[:, k, :], rs[:, k, :], ALU.mult)\
                                .then_inc(s_kn, 1)
                            for g in range(ACT_VARIANTS, 8):
                                ins = nc.vector.scalar_tensor_tensor(
                                    km[:, g // 4, g % 4, half(hf)], rt[:, k, :], const("onehot8")[:, g:g + 1],
                                    rs[:, k, :], ALU.mult, ALU.mult)
                        ins.then_inc(s_qk, 1)
                    if a == 1 and u == 4:
                        reduce_peaks(0, 2, 3, 1)
                    if a == 1 and u == 6:
                        scales_of(0, 2, 3, 1).then_inc(s_sc, 1)

            def normalise_grouped(a, p):
                n = a * PAIRS + p
                dve.wait_ge(s_o, n + 1)
                bank = ps[p % 2]
                if n >= 1:
                    dve.wait_ge(s_on, n)
                link(nc.vector.reciprocal(rc[:], bank[:, G4 * S:2 * G4 * S]))
                nc.vector.tensor_tensor(ot4[:, :, p * S:(p + 1) * S],
                                        bank[:, 0:G4 * S].rearrange("p (g s) -> p g s", g=G4),
                                        rc[:].rearrange("p (g s) -> p g s", g=G4), ALU.mult).then_inc(s_on, 1)

            def normalise_outputs(p):
                n = 2 * PAIRS + p
                dve.wait_ge(s_o, n + 1)
                o = ps[p % 2][:, 0:HEADS * (HD + 1)].rearrange("p (h b d) -> p h b d", h=HALFPOS, b=2)
                den = rden[:, p % 2, :].rearrange("p (h b) -> p h b", h=HALFPOS)
                if p >= 2:
                    dve.wait_ge(s_on, n - 1)
                link(nc.vector.reciprocal(den, o[:, :, :, HD]))
                if p >= 2:
                    dve.wait_ge(s_ott, p - 1)
                nc.vector.tensor_tensor(on[:, p % 2, :, :].rearrange("p b (h d) -> p h b d", h=HALFPOS),
                                        o[:, :, :, 0:HD],
                                        bc(den.unsqueeze(3), [P, HALFPOS, 2, HD]), ALU.mult).then_inc(s_on, 1)

            nc.vector.memset(wrow[96:97, :], 1.0).then_inc(s_init, 1)
            dve.wait_ge(s_cst, 48)
            nc.vector.tensor_copy(cstb[:], nt[:, 0:NBF]).then_inc(s_init, 1)
            link(nc.vector.tensor_tensor(posb[:].rearrange("p c s -> p (c s)"), vector("pos"), vector("base"),
                                         ALU.add))
            for hf in range(2):
                dve.wait_ge(s_tok, hf + 1)
                for c in range(C):
                    ins = nc.vector.tensor_tensor(
                        h[:, c, half(hf)].rearrange("p (b s) -> p b s", s=S),
                        ps[2 * c + hf][:, 0:HALF].rearrange("p (b s) -> p b s", s=S),
                        bc(posb[:, c, :].unsqueeze(1), [P, HB, S]), ALU.add)
                ins.then_inc(s_h, 1)

            centre(0)
            norm_apply(xn, xc, 0, s_xn, vector("norm1"), 1, (1.0 + RMS_EPS) ** -0.5)
            for a in range(2):
                if a == 1:
                    norm_apply(xn, x0, 4, s_xn, vector("norm2"), 2)
                qk_units(a)
                if a == 0:
                    layer_norm_stream()
                for p in range(PAIRS):
                    normalise_grouped(a, p)
                    if a == 0 and p == 1:
                        dve.wait_ge(s_ffw, 32)
                    if a == 0 and p in (1, 4):
                        nc.vector.tensor_reduce(pk[:, p // 4:p // 4 + 1], (w1_sb, w2_sb)[p // 4][:], AX.X, ALU.max,
                                                apply_absolute_value=True).then_inc(s_pk, 1)
                for hf in range(2):
                    dve.wait_ge(s_wo, 2 * a + hf + 1)
                    for m in range(C):
                        dst, src = (z[:, m, half(hf)].rearrange("p (q b s) -> p q b s", b=2, s=S)
                                    for z in ((x0, tmp)[a], x0))
                        ins = nc.vector.tensor_tensor(
                            dst, src, ps[4 + 2 * m + hf][:, 0:HALF].rearrange("p (b q s) -> p q b s", b=2, s=S),
                            ALU.add)
                    if a == 0:
                        ins.then_inc(s_x0, 1)
                    else:
                        link(ins)
                        nc.vector.tensor_tensor(h[:, :, half(hf)], h[:, :, half(hf)], tmp[:, :, half(hf)], ALU.add)\
                            .then_inc(s_h, 1)

            centre(2)
            norm_apply(xn, xc, 6, s_xn)
            dve.wait_ge(s_sig, 1)
            bias = bc(vector("gate_bias").unsqueeze(1), [P, TT, EXPERTS])
            link(nc.vector.tensor_tensor(choice[:], sig[:], bias, ALU.add))
            for t in range(TT):
                for g in range(GROUPS):
                    ins = nc.vector.max(top[:, t, g, :], choice[:, t, g * PER_GROUP:(g + 1) * PER_GROUP])
            link(ins)
            link(nc.vector.tensor_tensor(gsum[:], top[:, :, :, 0], top[:, :, :, 1], ALU.add))
            for t in range(TT):
                mine = bc(gsum[:, t, :].unsqueeze(2), [P, GROUPS, GROUPS])
                others = bc(gsum[:, t, :].unsqueeze(1), [P, GROUPS, GROUPS])
                nc.vector.tensor_tensor(gcmp[:, t, :, :], others, mine, ALU.is_gt)
                ins = nc.vector.tensor_tensor(geq[:, t, :, :], others, mine, ALU.is_equal)
            link(ins)
            flat = lambda ap: ap.rearrange("p t a b -> p t (a b)")
            link(nc.vector.tensor_tensor(flat(geq[:]), flat(geq[:]),
                                         bc(const("tie").unsqueeze(1), [P, TT, 16]), ALU.mult))
            link(nc.vector.tensor_tensor(flat(gcmp[:]), flat(gcmp[:]), flat(geq[:]), ALU.add))
            link(nc.vector.tensor_reduce(grank[:], gcmp[:], AX.X, ALU.add))
            link(nc.vector.tensor_scalar(grank[:], grank[:], 2.0, None, ALU.is_lt))
            for t in range(TT):
                ins = nc.vector.tensor_tensor(
                    masked[:, t, :].rearrange("p (g k) -> p g k", g=GROUPS),
                    choice[:, t, :].rearrange("p (g k) -> p g k", g=GROUPS),
                    bc(grank[:, t, :].unsqueeze(2), [P, GROUPS, PER_GROUP]), ALU.mult)
            link(ins)
            link(nc.vector.tensor_scalar(masked[:], masked[:], 0.0, None, ALU.add))
            for t in range(TT):
                ins = nc.vector.max(top[:, t, 0, :], masked[:, t, :])
            link(ins)
            for t in range(TT):
                ins = nc.vector.match_replace(repl[:, t, :], top[:, t, 0, :], masked[:, t, :], -3.0e38)
            link(ins)
            link(nc.vector.tensor_tensor(repl[:], repl[:], masked[:], ALU.not_equal))
            link(nc.vector.tensor_tensor(wts[:], repl[:], sig[:], ALU.mult))
            link(nc.vector.tensor_reduce(wsum[:], wts[:], AX.X, ALU.add))
            link(nc.vector.tensor_scalar(wsum[:], wsum[:], 1e-20, None, ALU.add))
            link(nc.vector.reciprocal(wsum[:], wsum[:]))
            link(nc.vector.tensor_scalar(wsum[:], wsum[:], ROUTED_SCALING, None, ALU.mult))
            link(nc.vector.tensor_tensor(wts[:], wts[:], bc(wsum[:].unsqueeze(2), [P, TT, EXPERTS]), ALU.mult))
            link(nc.vector.tensor_copy(wparts[:, :, 0:EXPERTS], wts[:]))
            link(nc.vector.tensor_tensor(wres[:], wts[:], wparts[:, :, 0:EXPERTS], ALU.subtract))
            link(nc.vector.tensor_copy(wparts[:, :, EXPERTS:2 * EXPERTS], wres[:]))
            link(nc.vector.tensor_tensor(wres[:], wres[:], wparts[:, :, EXPERTS:2 * EXPERTS], ALU.subtract))
            nc.vector.tensor_copy(wparts[:, :, 2 * EXPERTS:3 * EXPERTS], wres[:]).then_inc(s_wp, 1)
            dve.wait_ge(s_xs, 1)
            nc.vector.tensor_tensor(xl[:], xn[:, :, 0:T], xh[:].bitcast(f32), ALU.subtract).then_inc(s_xs, 1)
            dve.wait_ge(s_wt, 1)
            nc.vector.tensor_copy(wrow[0:96, :], ps[5][:].bitcast(bf16)[0:96, 0:TT * P]).then_inc(s_wrow, 1)

            def expert_unit(n, j):
                dve.wait_ge(s_sg, n + 1)
                dve.wait_ge(s_u, n + 1)
                ins = nc.vector.tensor_tensor(gu[:, j, :], sg[:, j, :], ps[5][:, 0:HALF], ALU.mult)
                ins.then_inc(s_mulc, 1)
                dve.wait_ge(s_mulc, n + 1)
                nc.vector.tensor_tensor(act[:, j, :], gu[:, j, :], ps[6][:, 0:HALF], ALU.mult).then_inc(s_act, 1)
                dve.wait_ge(s_ah, n + 1)
                nc.vector.tensor_tensor(al[:, j, :], act[:, j, :], ah[:, j, :].bitcast(f32), ALU.subtract)\
                    .then_inc(s_al, 1)

            with dve.Fori(0, UNITS // 2) as r:
                for j in range(4):
                    expert_unit(r * 4 + j, j % 2)

            centre(3)
            norm_apply(xn, xc, 8, s_xn)
            for c in range(C):
                for hf in range(2):
                    dve.wait_ge(s_qkps, 4 + 2 * c + hf + 1)
                    nc.vector.tensor_scalar(kt[:, c, half(hf)], ps[2 * c + hf][:, 0:HALF],
                                            vector("qkv_b")[:, 2 + c:3 + c], None, ALU.add).then_inc(s_kev, 1)
            nc.vector.tensor_copy(pairs_r, const("pairs")).then_inc(s_kmr, 1)
            dve.wait_ge(s_kev, 4)
            for p in range(-1, PAIRS + 2):
                if p + 1 < PAIRS:
                    if p + 1 >= 2:
                        dve.wait_ge(s_sq_s, p)
                    for c in range(C):
                        ins = variants(nc.vector, kvar, kt, p + 1, c)
                    ins.then_inc(s_kvar, 1)
                if 0 <= p < PAIRS:
                    dve.wait_ge(s_sq_s, p + 1)
                    for k in range(2):
                        ins = nc.vector.tensor_reduce(
                            mx[:, p % 2, k * HALFPOS:(k + 1) * HALFPOS],
                            ps[4 + k][:, 0:HALFPOS * S].rearrange("p (h s) -> p h s", s=S), AX.X, ALU.max)
                    ins.then_inc(s_mx, 1)
                    dve.wait_ge(s_mx, p + 1)
                    if p >= 2:
                        dve.wait_ge(s_s, 2 * PAIRS + p - 1)
                    nc.vector.tensor_tensor(dg[:, p % 2, :, :], bc(mx[:, p % 2, :].unsqueeze(2), [P, HEADS, S]),
                                            bc(const("minus_ident").unsqueeze(1), [P, HEADS, S]), ALU.mult)\
                        .then_inc(s_dg, 1)
                if p >= 2:
                    normalise_outputs(p - 2)
            for hf in range(2):
                dve.wait_ge(s_wo, 4 + hf + 1)
                for m in range(C):
                    ins = nc.vector.scalar_tensor_tensor(h[:, m, half(hf)], ps[4 + 2 * m + hf][:, 0:HALF],
                                                         vector("out_b")[:, m:m + 1], h[:, m, half(hf)],
                                                         ALU.add, ALU.add)
                ins.then_inc(s_h, 1)

            centre(4)
            norm_apply(xn, xc, 10, s_xn)
            dve.wait_ge(s_xn, 10)
            nc.vector.tensor_reduce(pk[:, 2:3], xn[:, :, 0:T], AX.XY, ALU.max, apply_absolute_value=True)\
                .then_inc(s_pk, 1)
            reduce_peaks(2, 1, 7, 2)
            scales_of(2, 1, 7, 2).then_inc(s_sc, 1)
            dve.wait_ge(s_sc, 2)
            link(nc.vector.tensor_scalar(xn[:, :, 0:T], xn[:, :, 0:T], inv[:, 2:3], ROUND, ALU.mult, ALU.add))
            nc.vector.tensor_scalar(xq[:], xn[:, :, 0:T], -ROUND, None, ALU.add).then_inc(s_xq, 1)
            nc.vector.tensor_tensor(sxw[:, 0:1], scale[:, 0:1], scale[:, 2:3], ALU.mult).then_inc(s_sc, 1)
            dve.wait_ge(s_sc, 3)
            nc.vector.tensor_scalar(b1s[:], vector("b1"), sxw[:, 0:1], None, ALU.mult).then_inc(s_sc, 1)
            for u in range(2 * FC):
                hf, ch = u // FC, u % FC
                dve.wait_ge(s_hid, u + 1)
                ins = nc.vector.tensor_reduce(peak[:, u:u + 1], hid[:, ch, half(hf)], AX.X, ALU.max,
                                              apply_absolute_value=True)
            link(ins)
            nc.vector.tensor_reduce(pk[:, 3:4], peak[:], AX.X, ALU.max).then_inc(s_pk, 1)
            reduce_peaks(3, 1, 7, 3)
            scales_of(3, 1, 7, 3).then_inc(s_sc, 1)
            nc.vector.tensor_tensor(sxw[:, 1:2], scale[:, 1:2], scale[:, 3:4], ALU.mult).then_inc(s_sc, 1)
            for ch in range(FC):
                dve.wait_ge(s_hs, ch + 1)
                nc.vector.tensor_scalar(hidq[:, ch, :], hid[:, ch, :], -ROUND, None, ALU.add).then_inc(s_hq, 1)
            dve.wait_ge(s_sc, 6)
            for hf in range(2):
                dve.wait_ge(s_f2, hf + 1)
                for m in range(C):
                    ins = nc.vector.tensor_scalar(tmp[:, m, half(hf)], ps[2 * m + hf][:, 0:HALF],
                                                  vector("b2")[:, m:m + 1], sxw[:, 1:2], ALU.add, ALU.mult)
                link(ins)
                nc.vector.tensor_tensor(x0[:, :, half(hf)], h[:, :, half(hf)], tmp[:, :, half(hf)], ALU.add).then_inc(s_fin, 1)

        @block.tensor
        def _(pe):
            def mm(out_, lhsT, rhs, start, stop):
                return nc.tensor.matmul(out_, lhsT, rhs, start=start, stop=stop, skip_group_check=True)

            def norm(n, mean=True):
                if mean:
                    for hf in range(2):
                        pe.wait_ge(s_h, cent_count(n, hf))
                        for c in range(C):
                            ins = mm(ps[hf][:, 0:HALF], const("mean"), h[:, c, half(hf)], c == 0, c == C - 1)
                        ins.then_inc(s_mean, 1)
                for hf in range(2):
                    pe.wait_ge(s_sq, 2 * n + hf + 1)
                    for c in range(C):
                        ins = mm(ps[2 + hf][:, 0:HALF], const("mean"), sq[:, c, half(hf)], c == 0, c == C - 1)
                    ins.then_inc(s_var, 1)

            def latent_sums(hf):
                pe.wait_ge(s_xn, hf + 1)
                pe.wait_ge(s_ars, 2 + hf + 1)
                for c in range(C):
                    ins = mm(ps[2 + hf][0:LAT, 0:HALF], down_sb[:, c, :], xn[:, c, half(hf)], c == 0, c == C - 1)
                ins.then_inc(s_lat, 1)

            def qk_units(a):
                for u in range(NPROJ + 1):
                    n = a * NPROJ + u
                    if u < NPROJ:
                        j, hf = QK_UNITS[u]
                        if a == 0 and 1 <= u < 3:
                            latent_sums(u - 1)
                        pe.wait_ge(s_xn, 2 * a + hf + 1)
                        if a == 0 and j == 2:
                            pe.wait_ge(s_latv, hf + 1)
                        if u >= 2:
                            pe.wait_ge(s_rope, n - 1)
                        for sw in range(2):
                            bank = ps[4 + 2 * (u % 2) + sw][:, 0:HALF]
                            if j == 2 and a == 0:
                                ins = mm(bank, gk_sb[:, sw, :], latent[:, half(hf)], True, True)
                                continue
                            for c in range(C):
                                w = wq_sb[a][:, c, sw, j * P:(j + 1) * P] if j < 2 else lk_sb[:, c, sw, :]
                                ins = mm(bank, w, xn[:, c, half(hf)], c == 0, c == C - 1)
                        ins.then_inc(s_proj, 1)
                    if u >= 1:
                        pe.wait_ge(s_qsq, n)
                        if u >= 3:
                            pe.wait_ge(s_qk, n - 2)
                        mm(ps[(u - 1) % 2][:, 0:HALF], const("headmean"), sq2[:, (u - 1) % 2, :], True, True)\
                            .then_inc(s_qms, 1)
                    if a == 1 and u == 3:
                        peak_rows(0, 2, 3, 2)
                    if a == 1 and u == 5:
                        peak_broadcast(0, 2, 3, 1)

            def row_scores(p):
                pe.wait_ge(s_kvar, p + 1)
                if p >= 1:
                    pe.wait_ge(s_mx, p)
                for c in range(C):
                    for b in range(2):
                        at = (2 * p + b) * S
                        ins = mm(ps[4 + c][64 * b:64 * b + 64, 0:HALF].rearrange("p (g s) -> p g s", g=8),
                                 qt[:, c, at:at + 64], kvar[:, p % 2, c, :, b * S:(b + 1) * S], True, True)
                ins.then_inc(s_sq_s, 1)

            def scores(a, p):
                n = a * PAIRS + p
                b0 = score_bank(a, p)
                if a < 2:
                    if p >= 2:
                        pe.wait_ge(s_e, n - 1)
                    for gp in range(2):
                        mm(ps[b0 + gp][0:ROWS, 0:HALFPOS * S].rearrange("p (h s) -> p h s", s=S),
                           ident_bf[:, 0:ROWS], causal_bf.unsqueeze(1).broadcast_to([P, HALFPOS, S]), True, False)
                else:
                    pe.wait_ge(s_dg, p + 1)
                    pe.wait_ge(s_qvar, p + 1)
                    if p >= 1:
                        pe.wait_ge(s_e, n)
                    for gp in range(2):
                        mm(ps[b0 + gp][0:ROWS, 0:HALFPOS * S], pairs_r[:, 0:ROWS],
                           dg[:, p % 2, gp * HALFPOS:(gp + 1) * HALFPOS, :].rearrange("p h s -> p (h s)"),
                           True, False)
                if a == 2:
                    for c in range(C):
                        for b in range(2):
                            ins = mm(ps[b0 + c][64 * b:64 * b + S, 0:HALF].rearrange("p (g s) -> p g s", g=8),
                                     kt[:, c, image(2 * p + b)], qvar[:, p % 2, c, :, b * S:(b + 1) * S], False, True)
                    ins.then_inc(s_s, 1)
                    return
                for k in range(0, HALFPOS, 2):
                    for gp in range(2):
                        for b in range(2):
                            cols = image(2 * p + b)
                            out_ = ps[b0 + gp][64 * b:64 * b + S, :]
                            ins = mm(out_[:, k * S:(k + 2) * S].rearrange("p (c s) -> p c s", c=C),
                                     km[:, gp, k // 2, cols], qt[:, :, cols], False, True)
                ins.then_inc(s_s, 1)

            def grouped_values(a, p):
                n = a * PAIRS + p
                pe.wait_ge(s_e, n + 1)
                if p >= 2:
                    pe.wait_ge(s_on, n - 1)
                for part in range(2):
                    for kv in range(KVH):
                        w = v4[0:ROWS, p, kv, :, :].rearrange("p b d -> p (b d)") if part == 0 else \
                            const("pair_ones", ROWS)
                        ex = e[0:ROWS, p % 2, 0:EC].rearrange("p (g n) -> p g n", g=2)
                        ins = mm(ps[p % 2][VP * kv:VP * (kv + 1), part * G4 * S:(part + 1) * G4 * S]
                                 .rearrange("p (g n) -> p g n", g=2),
                                 w, ex[:, :, kv * 2 * S:(kv + 1) * 2 * S], True, True)
                ins.then_inc(s_o, 1)

            def weighted_values(p):
                pe.wait_ge(s_e, 2 * PAIRS + p + 1)
                if p >= 2:
                    pe.wait_ge(s_on, 2 * PAIRS + p - 1)
                for hd in range(HEADS):
                    rows = slice(64 * (hd % 2), 64 * (hd % 2) + EP)
                    cols = slice(hd // 2 * 2 * (HD + 1), (hd // 2 + 1) * 2 * (HD + 1))
                    ins = mm(ps[p % 2][rows, cols], e[0:ROWS, p % 2, hd * S:hd * S + EP],
                             v16[0:ROWS, p, hd, :, :].rearrange("p b d -> p (b d)"), True, True)
                ins.then_inc(s_o, 1)

            def transposes(p):
                pe.wait_ge(s_on, 2 * PAIRS + p + 1)
                g = p // 2
                if p % 2 == 0 and g >= 2:
                    pe.wait_ge(s_ot, g - 1)
                for b in range(2):
                    at = ((p % 2) * 2 + b) * P
                    ins = nc.tensor.transpose(ps[2 + g % 2][:, at:at + P], on[:, p % 2, b, :], const("ident"))
                ins.then_inc(s_ott, 1)

            def project_grouped(a):
                N = HALF // 2
                for hf in range(2):
                    pe.wait_ge(s_on, a * PAIRS + PAIRS // 2 * (hf + 1))
                    for m in range(C):
                        for b in range(2):
                            for g in range(G4):
                                ins = mm(ps[4 + 2 * m + hf][:, b * N:(b + 1) * N], wo_sb[:, b, g, m * P:(m + 1) * P],
                                         ot4[:, g, hf * N:(hf + 1) * N], g == 0, g == G4 - 1)
                    ins.then_inc(s_wo, 1)

            def project_out():
                for hf in range(2):
                    pe.wait_ge(s_ot, 2 * (hf + 1))
                    for m in range(C):
                        for c in range(C):
                            ins = mm(ps[4 + 2 * m + hf][:, 0:HALF], outw_sb[:, c, m * P:(m + 1) * P],
                                     ot[:, c, half(hf)], c == 0, c == C - 1)
                    ins.then_inc(s_wo, 1)

            def attention(a):
                lead = 1 if a == 2 else 0
                for p in range(PAIRS + 2 + lead):
                    if a == 2 and p < PAIRS:
                        row_scores(p)
                    if 0 <= p - lead < PAIRS:
                        scores(a, p - lead)
                    if 0 <= p - lead - 1 < PAIRS:
                        if a < 2:
                            grouped_values(a, p - 1)
                        else:
                            weighted_values(p - 2)
                    if a == 2 and 0 <= p - lead - 2:
                        transposes(p - 3)

            def peak_rows(k, n, bank, count):
                pe.wait_ge(s_pk, count)
                for q in range(n):
                    ins = mm(ps[bank][0:1, q * P:(q + 1) * P], pk[:, k + q:k + q + 1], const("ident"), True, True)
                ins.then_inc(s_pkt, 1)

            def peak_broadcast(k, n, bank, count):
                pe.wait_ge(s_pk1, count)
                mm(ps[bank][:, 0:n], const("ones", 1), pk1[0:1, k:k + n], True, True).then_inc(s_pkb, 1)

            for k in range(KT):
                pe.wait_ge(s_x[k], 32)
                for hf in range(2):
                    for c in range(C):
                        ins = mm(ps[2 * c + hf][:, 0:HALF], w_lin_sb[:, k, c * P:(c + 1) * P],
                                 patches[:, k, half(hf)], k == 0, k == KT - 1)
                    if k == KT - 1:
                        ins.then_inc(s_tok, 1)

            pe.wait_ge(s_init, 9)
            pe.wait_ge(s_cst, 48)
            norm(0)
            pe.wait_ge(s_attn_w[0], 64)
            for a in range(2):
                if a == 1:
                    norm(1, mean=False)
                    pe.wait_ge(s_attn_w[1], 48)
                qk_units(a)
                for b in range(B):
                    out_ = ps[2][64 * (b % 2):64 * (b % 2) + 64, b // 2 * KVH * HD:(b // 2 + 1) * KVH * HD]
                    if a == 0:
                        ins = mm(out_, latent[:, b * S:b * S + 64], gv_sb[:], True, True)
                    else:
                        for c in range(C):
                            ins = mm(out_, xn[:, c, b * S:b * S + 64], lv_sb[:, c, :], c == 0, c == C - 1)
                ins.then_inc(s_vps, 1)
                pe.wait_ge(s_qk, NPROJ * (a + 1))
                pe.wait_ge(s_km, 2 * (a + 1))
                pe.wait_ge(s_v, a + 1)
                pe.wait_ge(s_init, 10)
                if a == 1:
                    pe.wait_ge(s_sc, 1)
                attention(a)
                pe.wait_ge(s_wo_w, 16 * (a + 1))
                project_grouped(a)

            norm(2)
            pe.wait_ge(s_moe_w, 48)
            pe.wait_ge(s_xn, 6)
            for t in range(TT):
                for c in range(C):
                    ins = mm(ps[4][:, t * EXPERTS:(t + 1) * EXPERTS], xn[:, c, t * P:(t + 1) * P],
                             gate_sb[:, c, :], c == 0, c == C - 1)
            ins.then_inc(s_log, 1)
            for hf in range(2):
                for m in range(C):
                    mm(ps[2 * m + hf][:, 0:HALF], const("ident"), h[:, m, half(hf)], True, False)
            pe.wait_ge(s_wp, 1)
            for t in range(TT):
                ins = nc.tensor.transpose(ps[5][:].bitcast(bf16)[0:96, t * P:(t + 1) * P], wparts[:, t, :],
                                          ident_bf)
            ins.then_inc(s_wt, 1)
            pe.wait_ge(s_wrow, 1)
            pe.wait_ge(s_xs, 2)

            def three(out_, parts_w, parts_x, start, stop):
                (w_hi, w_lo), (x_hi, x_lo) = parts_w, parts_x
                mm(out_, w_hi, x_hi, start, False)
                mm(out_, w_hi, x_lo, False, False)
                return mm(out_, w_lo, x_hi, False, stop)

            def up_sums(u, i, hf, first=False):
                n = 2 * u + hf
                if hf == 0:
                    pe.wait_ge(s_wsl, u + 1)
                if not first:
                    pe.wait_ge(s_sg, n)
                for c in range(C):
                    cols = slice(c * INNER, (c + 1) * INNER)
                    ins = three(ps[4][:, 0:HALF], (wh[i][:, cols], wl[i][:, cols]),
                                (xh[:, c, half(hf)], xl[:, c, half(hf)]), c == 0, c == C - 1)
                ins.then_inc(s_g, 1)
                if not first:
                    pe.wait_ge(s_act, n)
                for c in range(C):
                    cols = slice(D + c * INNER, D + (c + 1) * INNER)
                    three(ps[5][:, 0:HALF], (wh[i][:, cols], wl[i][:, cols]),
                          (xh[:, c, half(hf)], xl[:, c, half(hf)]), c == 0, c == C - 1)
                sel = select_bf[0:97, bass.ds(u, 1)].broadcast_to([97, P])
                mm(ps[6][:, 0:HALF], sel, wrow[0:97, half(hf)], True, True).then_inc(s_u, 1)

            def down_sums(u, i, hf):
                n = 2 * u + hf
                pe.wait_ge(s_al, n + 1)
                for m in range(C):
                    cols = slice(2 * D + m * P, 2 * D + (m + 1) * P)
                    ins = three(ps[2 * m + hf][:, 0:HALF], (wh[i][:, cols], wl[i][:, cols]),
                                (ah[:, hf, :], al[:, hf, :]), False, False)
                ins.then_inc(s_down, 1)

            up_sums(0, 0, 0, first=True)
            with pe.Fori(0, (UNITS - 1) // NRING) as r:
                for i in range(NRING):
                    u, nxt = r * NRING + i, (i + 1) % NRING
                    up_sums(u, i, 1)
                    down_sums(u, i, 0)
                    up_sums(u + 1, nxt, 0)
                    down_sums(u, i, 1)
            for u in range((UNITS - 1) // NRING * NRING, UNITS):
                i = u % NRING
                up_sums(u, i, 1)
                down_sums(u, i, 0)
                if u + 1 < UNITS:
                    up_sums(u + 1, (i + 1) % NRING, 0)
                down_sums(u, i, 1)
            pe.wait_ge(s_down, 2 * UNITS)
            mm(ps[7][0:1, 0:1], const("ones")[:, 0:1], const("ones")[:, 0:1], True, True).then_inc(s_acc, 1)

            norm(3)
            pe.wait_ge(s_xn, 8)
            for part in range(2):
                for c in range(C):
                    for hf in range(2):
                        bank = ps[4 * (1 - part) + 2 * c + hf][:, 0:HALF]
                        for k in range(C):
                            ins = mm(bank, qkv_sb[:, k, part * D + c * P:part * D + (c + 1) * P],
                                     xn[:, k, half(hf)], k == 0, k == C - 1)
                        ins.then_inc(s_qkps, 1)
            for b in range(4):
                pe.wait_ge(s_qkev, b + 1)
                for q in range(4):
                    at = (4 * b + q) * S
                    for k in range(C):
                        ins = mm(ps[4 + b][64 * (q % 2):64 * (q % 2) + 64, q // 2 * D:(q // 2 + 1) * D],
                                 xn[:, k, at:at + 64], qkv_sb[:, k, 2 * D:3 * D], k == 0, k == C - 1)
                ins.then_inc(s_vps, 1)
            pe.wait_ge(s_kev, 4)
            pe.wait_ge(s_kmr, 1)
            pe.wait_ge(s_v, 6)
            pe.wait_ge(s_init, 13)
            attention(2)
            project_out()

            norm(4)
            peak_rows(2, 1, 7, 3)
            peak_broadcast(2, 1, 7, 2)
            pe.wait_ge(s_wq, 2)
            pe.wait_ge(s_xq, 1)
            for u in range(2 * FC):
                hf, ch = u // FC, u % FC
                if u >= 4:
                    pe.wait_ge(s_hid, u - 3)
                for c in range(C):
                    ins = mm(ps[4 + u % 4][:, 0:HALF], w1q[:, c, ch * P:(ch + 1) * P], xq[:, c, half(hf)],
                             c == 0, c == C - 1)
                ins.then_inc(s_f1, 1)
            peak_rows(3, 1, 7, 4)
            peak_broadcast(3, 1, 7, 3)
            for ch in range(FC):
                pe.wait_ge(s_hq, ch + 1)
                for hf in range(2):
                    for m in range(C):
                        ins = mm(ps[2 * m + hf][:, 0:HALF], w2q[:, ch, m * P:(m + 1) * P],
                                 hidq[:, ch, half(hf)], ch == 0, ch == FC - 1)
                    if ch == FC - 1:
                        ins.then_inc(s_f2, 1)


def constants():
    import numpy as np

    f = np.float32
    c = np.zeros((P, NCONST), f)
    row = np.arange(P)

    def put(name, a):
        lo, hi = CONST_COLS[name]
        c[:, lo:hi] = a

    put("ident", np.eye(P))
    put("mean", 1.0 / D)
    put("headmean", (row[:, None] // HD == row[None, :] // HD) / HD)
    put("ones", 1.0)
    token = row % 64
    real = token < S
    put("pair_ones", (row[:, None] // 64 == np.arange(VP)[None, :] // HD) & real[:, None])
    put("pairs", (row[:, None] // 64 == row[None, :] // 64) & real[:, None] & real[None, :])
    put("minus_ident", -((token[:, None] == np.arange(S)[None, :]) & real[:, None]).astype(f))
    d = row % HD
    for name, base in (("g", 1000000.0), ("l", 10000.0)):
        inv_freq = f(1.0) / f(base) ** (np.arange(0, HD, 2, dtype=f) / f(HD))
        freqs = np.arange(S, dtype=f)[:, None] * inv_freq[None, :].astype(f)
        put("cos_" + name, np.cos(freqs).astype(f).T[d // 2, :])
        put("sin_" + name, np.sin(freqs).astype(f).T[d // 2, :] * np.where(d % 2 == 0, -1, 1)[:, None])
    put("onehot8", row[:, None] // HD == np.arange(8)[None, :])
    g = np.arange(GROUPS)
    put("tie", (g[None, :] < g[:, None]).astype(f).reshape(1, 16))
    b = np.zeros((P, NBF), f)
    b[:, 0:P] = np.eye(P)
    b[:, P:P + S] = np.where(real[:, None] & (token[:, None] > np.arange(S)[None, :]), -32768.0, 0.0)
    for u in range(UNITS):
        for part in range(3):
            if u < EXPERTS:
                b[part * EXPERTS + u, P + S + u] = 1.0
        if u >= EXPERTS:
            b[96, P + S + u] = 1.0
    return c, b


def layouts(i):
    import numpy as np

    def chunks(w):
        k, n = w.shape
        return np.ascontiguousarray(w.reshape(k // P, P, n).transpose(1, 0, 2))

    x = i["x"].reshape(B, 3, GRID, PATCH, GRID, PATCH).transpose(1, 3, 5, 0, 2, 4).reshape(KT * P, B, S - 1)
    xp = np.zeros((KT * P, B, S), x.dtype)
    xp[:, :, 1:] = x
    a = {"x": chunks(xp.reshape(KT * P, T)), "w_lin": chunks(i["L0_tok_W_lin"].T)}

    v = np.zeros((P, NVEC), np.float32)

    def put(name, rows):
        lo, hi = VEC_COLS[name]
        v[:, lo:hi] = rows.reshape(P, hi - lo)

    put("pos", chunks(i["L0_tok_position_embeddings"][0].T))
    base = np.concatenate([i["L0_tok_class_token"][0], np.repeat(i["L0_tok_b_lin"][None], S - 1, 0)], 0)
    put("base", chunks(base.T))
    col = lambda w: w.reshape(-1, P).T
    put("norm1", col(i["L0_attn_norm1_w"]))
    put("norm2", col(i["L0_attn_norm2_w"]))
    o_row = np.arange(D).reshape(HALFPOS, 2, HD).transpose(1, 0, 2).reshape(D)
    put("qkv_b", np.concatenate([col(i["L1_attn_qkv_b"][:2 * D]), col(i["L1_attn_qkv_b"][2 * D:][o_row])], 1))
    put("out_b", col(i["L1_attn_out_b"]))
    put("b1", col(i["L1_ffn_b1"]))
    put("b2", col(i["L1_ffn_b2"]))
    put("gate_bias", np.repeat(i["L0_ffn_gate_bias"][None], P, 0))
    a["vecs"] = v

    c, gp, kv, d = np.meshgrid(np.arange(C), np.arange(2), np.arange(KVH), np.arange(HD), indexing="ij")
    q_col = ((kv * 4 + 2 * c + gp) * HD + d).reshape(-1)
    k_col = (kv * HD + d)[0].reshape(-1)
    swap = lambda at: at ^ 1
    both = lambda w, at: np.ascontiguousarray(np.stack([w[..., at], w[..., swap(at)]], -2))

    def by_group(w):
        rows = w.reshape(KVH, C, 2, HD, D).transpose(0, 3, 2, 1, 4).reshape(KVH, HD, G4, D)
        padded = np.zeros((KVH, 2, HD, 2, G4, D), w.dtype)
        for b in range(2):
            padded[:, b, :, b] = rows
        return padded.reshape(P, 2, G4, D)

    a["g_wq"] = both(chunks(i["L0_attn_g_wq"]), q_col)
    a["g_down"] = chunks(i["L0_attn_g_kv_down"])
    a["g_k"] = both(i["L0_attn_g_k_up"], k_col)
    a["g_v"] = i["L0_attn_g_v_up"]
    a["g_wo"] = by_group(i["L0_attn_g_wo"])
    a["l_wq"] = both(chunks(i["L0_attn_l_wq"]), q_col)
    a["l_wk"] = both(chunks(i["L0_attn_l_wk"]), k_col)
    a["l_wv"] = chunks(i["L0_attn_l_wv"])
    a["l_wo"] = by_group(i["L0_attn_l_wo"])
    a["gate_w"] = chunks(i["L0_ffn_gate_w"].T)
    wg = np.concatenate([i["L0_ffn_expert_gate"], i["L0_ffn_shared_gate"].reshape(2, INNER, D)], 0)
    wu = np.concatenate([i["L0_ffn_expert_up"], i["L0_ffn_shared_up"].reshape(2, INNER, D)], 0)
    wd = np.concatenate([i["L0_ffn_expert_down"],
                         i["L0_ffn_shared_down"].reshape(D, 2, INNER).transpose(1, 0, 2)], 0)
    up = lambda w: w.reshape(UNITS, INNER, C, P).transpose(0, 3, 2, 1).reshape(UNITS, P, D)
    a["experts"] = np.concatenate([up(wg), up(wu), wd.transpose(0, 2, 1)], 2)
    a["qkv_w"] = chunks(i["L1_attn_qkv_w"].T)
    a["out_w"] = chunks(i["L1_attn_out_w"].T[o_row])
    a["w1"] = chunks(i["L1_ffn_w1"].T).reshape(P, C * FF)
    a["w2"] = chunks(i["L1_ffn_w2"].T).reshape(P, FC * D)
    return {k: np.ascontiguousarray(w) for k, w in a.items()}


_ORDER = ["x", "w_lin", "consts", "consts_bf", "vecs", "g_wq", "g_down", "g_k", "g_v", "g_wo", "l_wq", "l_wk",
          "l_wv", "l_wo", "gate_w", "experts", "qkv_w", "out_w", "w1", "w2"]


def kernel(**inputs):
    import numpy as np
    import concourse.bacc as bacc
    from concourse.bass_utils import run_bass_kernel_spmd

    arrays = layouts({k: np.asarray(v) for k, v in inputs.items()})
    arrays["consts"], arrays["consts_bf"] = constants()
    nc = bacc.Bacc("TRN2", target_bir_lowering=False, num_devices=1)
    args = [nc.dram_tensor(f"in_{k}", arrays[k].shape, mybir.dt.from_np(arrays[k].dtype), kind="ExternalInput").ap()
            for k in _ORDER]
    out = nc.dram_tensor("out", (P, C, T), mybir.dt.float32, kind="ExternalOutput").ap()
    program(nc, *args, out)
    r = run_bass_kernel_spmd(nc, [{f"in_{k}": arrays[k] for k in _ORDER}], core_ids=[0])
    got = r.results[0]["out"]
    return np.ascontiguousarray(got.transpose(2, 1, 0).reshape(B, S, D))
```

```python
from contextlib import ExitStack

import concourse.bass as bass
from concourse import mybir

B = 16
PATCH, GRID = 16, 6
S = GRID * GRID + 1
T = B * S
D = 256
P = 128
C = D // P
KT = 3 * PATCH * PATCH // P
HEADS, KVH, HD = 16, 4, 16
LAT = 64
HALF = T // 2
HB = B // 2
PAIRS = B // 2
EP = 64
ROWS = 64 + S
TP = 640
HALFPOS = HEADS // 2
G4 = HEADS // KVH
VP = 2 * HD
EC = HEADS * S
EXPERTS, TOPK, GROUPS, PER_GROUP = 32, 8, 4, 8
SHARED = 2
UNITS = EXPERTS + SHARED
INNER = 128
EW = 3 * D
TT = 5
FF = 1024
FC = FF // P
DVE_CHUNKS, ACT_CHUNKS, POOL_CHUNKS = (4, 5), 4, (6, 7)
ROUTED_SCALING = 2.5
LN_EPS, RMS_EPS = 1e-5, 1e-6
START_BUSY = 16
BUSY = ((7, (0, 4, 24)), (0, (5, 0, 18)), (3, (5, 4, 14)), (7, (6, 4, 24)), (3, (5, 4, 18)))
LEAD = 3
QK_UNITS = ((0, 0), (1, 0), (2, 0), (2, 1), (0, 1), (1, 1))
ACT_VARIANTS = 4
QP, MIN_RANGE = 127.0, 1e-6
ROUND = 1.5 * 2.0 ** 23

CONST_COLS, VEC_COLS = {}, {}


def _columns(table, widths):
    at = 0
    for name, width in widths:
        table[name] = (at, at + width)
        at += width
    return at


NCONST = _columns(CONST_COLS, [
    ("ident", P), ("mean", P), ("headmean", P), ("swap", P), ("ones", P), ("pairs", P), ("pair_ones", VP), ("minus_ident", S),
    ("cos_g", S), ("sin_g", S), ("cos_l", S), ("sin_l", S), ("onehot8", 8),
    ("tie", 16)])
NVEC = _columns(VEC_COLS, [
    ("pos", C * S), ("base", C * S), ("norm1", C), ("norm2", C), ("qkv_b", 6), ("out_b", C),
    ("b1", FC), ("b2", C), ("gate_bias", EXPERTS)])


NBF = P + S + UNITS


def program(nc, x, w_lin, consts, consts_bf, vecs, g_wq, g_down, g_k, g_v, g_wo, l_wq, l_wk, l_wv, l_wo,
            gate_w, experts, qkv_w, out_w, w1, w2, out):
    f32, f32r, bf16 = mybir.dt.float32, mybir.dt.float32r, mybir.dt.bfloat16
    ALU, ACT, AX = mybir.AluOpType, mybir.ActivationFunctionType, mybir.AxisListType

    with ExitStack() as ctx:
        def sb(name, shape, dt=f32):
            return ctx.enter_context(nc.sbuf_tensor(name, shape, dt))

        def sem(name):
            return ctx.enter_context(nc.semaphore(name))

        region = sb("region", [P, KT * (T + D)])
        patches = region[:, 0:KT * T].rearrange("p (k t) -> p k t", k=KT)
        w_lin_sb = region[:, KT * T:KT * (T + D)].rearrange("p (k d) -> p k d", k=KT)
        hid = region[:, 0:FC * T].rearrange("p (c t) -> p c t", c=FC)
        cst = sb("cst", [P, NCONST])
        cstb = sb("cstb", [P, NBF], bf16)
        vec = sb("vec", [P, NVEC])
        wq_sb = [sb(f"wq_sb{a}", [P, C, D]) for a in range(2)]
        down_sb = sb("down_sb", [P, C, LAT])
        gk_sb = sb("gk_sb", [LAT, P])
        gv_sb = sb("gv_sb", [LAT, KVH * HD])
        lk_sb = sb("lk_sb", [P, C, P])
        lv_sb = sb("lv_sb", [P, C, KVH * HD])
        V4 = PAIRS * KVH * VP
        OT = G4 * PAIRS * S
        wo_sb = region[:, OT + V4:OT + V4 + 2 * G4 * D].rearrange("p (b g d) -> p b g d", b=2, g=G4)
        gate_sb = sb("gate_sb", [P, C, EXPERTS])
        qkv_sb = sb("qkv_sb", [P, C, 3 * D])
        outw_sb = sb("outw_sb", [P, C, D])
        w1_sb = sb("w1_sb", [P, C * FF])
        w2_sb = sb("w2_sb", [P, FC * D])
        w1q = sb("w1q", [P, C, FF], bf16)
        w2q = sb("w2q", [P, FC, D], bf16)

        posb = sb("posb", [P, C, S])
        h = sb("h", [P, C, T])
        xc = sb("xc", [P, C, T])
        sq = sb("sq", [P, C, T])
        x0 = sb("x0", [P, C, T])
        xn = sb("xn", [P, C, TP])
        ars = sb("ars", [P, T])
        ars0 = sb("ars0", [P, T])
        var = sb("var", [P, T])
        nt = sb("nt", [P, T])
        latent = sb("latent", [LAT, TP])
        qt = sb("qt", [P, C, TP])
        km = sb("km", [P, C, 4, TP])
        PAIRCOLS = C * 8 * 2 * S
        km_flat = km[:].rearrange("p c i t -> p (c i t)")
        kvar, qvar = (km_flat[:, j * 2 * PAIRCOLS:(j + 1) * 2 * PAIRCOLS]
                      .rearrange("p (k c g t) -> p k c g t", k=2, c=C, g=8) for j in range(2))
        ot4 = region[:, 0:OT].rearrange("p (g t) -> p g t", g=G4)
        v4 = region[:, OT:OT + V4].rearrange("p (q h b d) -> p q h b d", q=PAIRS, h=KVH, b=2)
        V16 = PAIRS * HEADS * 2 * (HD + 1)
        v16 = region[:, 0:V16].rearrange("p (q h b d) -> p q h b d", q=PAIRS, h=HEADS, b=2)
        ra = sb("ra", [P, 2, HALF])
        qcopy = sb("qcopy", [P, 2, HALF])
        rb = sb("rb", [P, 2, HALF])
        rt = sb("rt", [P, 2, HALF])
        sq2 = sb("sq2", [P, 2, HALF])
        rs = sb("rs", [P, 2, HALF])
        rn = sb("rn", [P, HALF])
        e = sb("e", [P, 2, EC + EP - S])
        on = sb("on", [P, 2, 2, P])
        rden = sb("rden", [P, 2, HEADS])
        mx = sb("mx", [P, 2, HEADS])
        kt = xc
        ot = sb("ot", [P, C, T])
        tmp = sq

        sig = sb("sig", [P, TT, EXPERTS])
        choice = sb("choice", [P, TT, EXPERTS])
        masked = sb("masked", [P, TT, EXPERTS])
        repl = sb("repl", [P, TT, EXPERTS])
        wts = sb("wts", [P, TT, EXPERTS])
        wres = sb("wres", [P, TT, EXPERTS])
        top = sb("top", [P, TT, GROUPS, 8])
        gsum = sb("gsum", [P, TT, GROUPS])
        grank = sb("grank", [P, TT, GROUPS])
        gcmp = sb("gcmp", [P, TT, GROUPS, GROUPS])
        geq = sb("geq", [P, TT, GROUPS, GROUPS])
        wsum = sb("wsum", [P, TT])
        wparts = sb("wparts", [P, TT, 3 * EXPERTS], bf16)
        wrow = sb("wrow", [P, TT * P], bf16)

        xh = sb("xh", [P, C, T], f32r)
        xl = sb("xl", [P, C, T], f32r)
        dg = xl[:].rearrange("p c t -> p (c t)").rearrange("p (k h s) -> p k h s", k=2, h=HEADS)
        NRING = 4
        ring_all = km[:].rearrange("p c i t -> p (c i t)")
        ring = [ring_all[:, i * EW:(i + 1) * EW] for i in range(NRING)]
        split_all = sb("split_all", [P, 2 * NRING * EW], f32r)
        wh = [split_all[:, i * EW:(i + 1) * EW] for i in range(NRING)]
        wl = [split_all[:, (NRING + i) * EW:(NRING + i + 1) * EW] for i in range(NRING)]
        pairs_r = split_all[:, 0:P]
        sg, gu, act = ra, rb, rt
        ah = sb("ah", [P, 2, HALF], f32r)
        al = sb("al", [P, 2, HALF], f32r)

        hidq = km[:].rearrange("p c i t -> p (c i t)").bitcast(bf16)[:, 0:FC * T].rearrange("p (c t) -> p c t", c=FC)
        xq = sq[:].rearrange("p c t -> p (c t)").bitcast(bf16)[:, 0:C * T].rearrange("p (c t) -> p c t", c=C)
        peak = sb("peak", [P, FC])
        pk = sb("pk", [P, 4])
        pk1 = sb("pk1", [1, 4])
        scale = sb("scale", [P, 4])
        inv = sb("inv", [P, 4])
        sxw = sb("sxw", [P, 2])
        b1s = sb("b1s", [P, FC])
        b2s = sb("b2s", [P, C])
        eps = sb("eps", [P, 4])
        spare = sb("spare", [P, 16])
        rc = sb("rc", [P, G4 * S])

        psum = ctx.enter_context(nc.psum_tensor("psum", [P, 8, 512], f32))
        ps = [psum[:, i, :] for i in range(8)]

        def const(name, rows=P):
            a, b = CONST_COLS[name]
            return cst[0:rows, a:b]

        def vector(name):
            a, b = VEC_COLS[name]
            return vec[:, a:b]

        ident_bf = cstb[:, 0:P]
        causal_bf = cstb[:, P:P + S]
        select_bf = cstb[:, P + S:P + S + UNITS]

        def half(hf):
            return slice(hf * HALF, (hf + 1) * HALF)

        def image(b):
            return slice(b * S, (b + 1) * S)

        s_x = [sem(f"patches_loaded{k}") for k in range(KT)]
        s_cst = sem("constants_loaded")
        s_attn_w = [sem(f"attention_weights_loaded{a}") for a in range(2)]
        s_wo_w = sem("output_weights_loaded")
        s_ffw = sem("ffn_weights_loaded")
        s_moe_w = sem("router_and_last_attention_weights_loaded")
        s_ring = [sem(f"expert_loaded{i}") for i in range(NRING)]
        s_init = sem("buffers_initialised")
        s_vz = sem("zeros_and_ones_beside_the_values_ready")
        s_zero = sem("zeros_for_warming_up")
        s_tok = sem("embedding_summed")
        s_h = sem("stream_ready")
        s_mean = sem("mean_summed")
        s_cent = sem("tokens_centred")
        s_sq = sem("squares_ready")
        s_var = sem("variance_summed")
        s_ars = sem("table_rsqrt_ready")
        s_xw = sem("tokens_weighted")
        s_xy = sem("tokens_times_table_rsqrt")
        s_xn = sem("normalised_ready")
        s_x0 = sem("attention_stream_ready")
        s_lat = sem("latent_summed")
        s_latv = sem("latent_copied")
        s_proj = sem("qk_projected")
        s_qcp = sem("qk_copied")
        s_swap = sem("qk_rows_exchanged")
        s_rope = sem("rope_products_ready")
        s_rsum = sem("rope_summed")
        s_rscaled = sem("rope_scaled")
        s_qsq = sem("qk_squares_ready")
        s_qms = sem("qk_mean_square_summed")
        s_qars = sem("qk_table_rsqrt_ready")
        s_qk = sem("qk_ready")
        s_km = sem("key_variants_ready")
        s_kmv = sem("vector_key_variants_ready")
        s_vps = sem("values_projected")
        s_v = sem("values_copied")
        s_s = sem("scores_summed")
        s_e = sem("exponentials_ready")
        s_o = sem("outputs_summed")
        s_on = sem("outputs_normalised")
        s_ott = sem("outputs_transposed")
        s_ot = sem("outputs_copied")
        s_wo = sem("attention_projected")
        s_log = sem("router_logits_summed")
        s_sig = sem("router_scores_ready")
        s_wp = sem("weight_parts_ready")
        s_wt = sem("weight_parts_transposed")
        s_wrow = sem("weight_rows_ready")
        s_xh = sem("token_high_parts_ready")
        s_xs = sem("tokens_split")
        s_wsh = sem("expert_high_parts_ready")
        s_wsl = sem("expert_low_parts_ready")
        s_g = sem("gate_summed")
        s_u = sem("up_and_weight_summed")
        s_sg = sem("silu_ready")
        s_act = sem("weighted_activation_ready")
        s_ah = sem("activation_high_part_ready")
        s_alp = sem("shared_activation_low_part_ready")
        s_al = sem("activation_low_part_ready")
        s_down = sem("down_summed")
        s_acc = sem("experts_all_summed")
        s_qkps = sem("last_qk_projected")
        s_qkev = sem("last_q_copied")
        s_kev = sem("last_k_copied")
        s_kmr = sem("pair_blocks_rounded")
        s_kvar = sem("last_key_variants_ready")
        s_kvar1 = sem("last_key_variants_of_chunk_1_ready")
        s_qvar = sem("last_query_variants_ready")
        s_sq_s = sem("row_scores_summed")
        s_mx = sem("row_maxima_read")
        s_dg = sem("maxima_on_diagonals")
        s_pk = sem("peaks_ready")
        s_pkt = sem("peaks_in_a_row")
        s_pk1 = sem("peak_reduced")
        s_pkb = sem("peak_broadcast")
        s_sc = sem("scales_ready")
        s_wqt = sem("ffn_weight_scaled")
        s_wq = sem("ffn_weights_quantised")
        s_xq = sem("ffn_input_quantised")
        s_f1 = sem("ffn_first_summed")
        s_hid = sem("hidden_ready")
        s_hpk = sem("hidden_peak_read")
        s_hs = sem("hidden_scaled")
        s_hqp = sem("hidden_quantised_by_pool")
        s_hqs = sem("hidden_scaled_by_pool")
        s_hq = sem("hidden_quantised")
        s_f2 = sem("ffn_second_summed")
        s_fin = sem("result_ready")
        s_out = sem("result_stored")
        s_dve = sem("vector_step")
        s_act_own = sem("scalar_step")
        s_mulc = sem("expert_product_ready")
        s_pool_own = sem("pool_step")

        block = ctx.enter_context(nc.Block())
        NPROJ = 3 * 2

        def cent_count(n, hf):
            return 2 * {0: 0, 2: 1, 3: 2, 4: 3}[n] + hf + 1

        def score_bank(a, p):
            return 4 + 2 * (p % 2) if a < 2 else 6

        def variants(engine, dst, src, p, c):
            shape = [P, 8, 2 * S]
            return engine.tensor_tensor(dst[:, p % 2, c, :, :],
                                        src[:, c, 2 * p * S:2 * (p + 1) * S].unsqueeze(1).broadcast_to(shape),
                                        const("onehot8").unsqueeze(2).broadcast_to(shape), ALU.mult)

        @block.sync
        def _(sp):
            for k in range(KT):
                sp.dma_start(patches[:, k, :], x[:, k, :]).then_inc(s_x[k], 16)
            sp.dma_start(wq_sb[0][:], g_wq).then_inc(s_attn_w[0], 16)
            sp.dma_start(wq_sb[1][:], l_wq).then_inc(s_attn_w[1], 16)
            sp.dma_start(lk_sb[:], l_wk).then_inc(s_attn_w[1], 16)
            sp.dma_start(lv_sb[:], l_wv).then_inc(s_attn_w[1], 16)
            sp.dma_start(w1_sb[:], w1).then_inc(s_ffw, 16)
            sp.dma_start(w2_sb[:], w2).then_inc(s_ffw, 16)
            sp.wait_ge(s_tok, 2)
            sp.dma_start(wo_sb, g_wo).then_inc(s_wo_w, 16)
            sp.dma_start(gate_sb[:], gate_w).then_inc(s_moe_w, 16)
            sp.dma_start(qkv_sb[:], qkv_w).then_inc(s_moe_w, 16)
            sp.dma_start(outw_sb[:], out_w).then_inc(s_moe_w, 16)
            sp.wait_ge(s_wo, 2)
            sp.dma_start(wo_sb, l_wo).then_inc(s_wo_w, 16)
            sp.wait_ge(s_s, 2 * PAIRS)
            for i in range(NRING):
                sp.dma_start(ring[i], experts[i, :, :]).then_inc(s_ring[i], 16)
            with sp.Fori(1, UNITS // NRING) as r:
                for i in range(NRING):
                    sp.wait_ge(s_wsh, r * NRING + (i + 1 - NRING))
                    sp.wait_ge(s_wsl, r * NRING + (i + 1 - NRING))
                    sp.dma_start(ring[i],
                                 experts[bass.ds(r * NRING + i, 1), :, :].rearrange("a p n -> (a p) n"))\
                        .then_inc(s_ring[i], 16)
            for u in range(UNITS - UNITS % NRING, UNITS):
                i = u % NRING
                sp.wait_ge(s_wsh, u + 1 - NRING)
                sp.wait_ge(s_wsl, u + 1 - NRING)
                sp.dma_start(ring[i], experts[u, :, :]).then_inc(s_ring[i], 16)
            for hf in range(2):
                sp.wait_ge(s_fin, 2 * hf + 1)
                sp.dma_start(out[:, 0, half(hf)], x0[:, 0, half(hf)]).then_inc(s_out, 16)
            sp.wait_ge(s_out, 64)

        @block.gpsimd
        def _(pool):
            nc.gpsimd.memset(eps[:, 0:1], LN_EPS).then_inc(s_init, 1)
            nc.gpsimd.memset(eps[:, 1:2], RMS_EPS * LN_EPS / (1.0 + RMS_EPS)).then_inc(s_init, 1)
            nc.gpsimd.memset(eps[:, 2:3], RMS_EPS).then_inc(s_init, 1)
            nc.gpsimd.memset(xn[:, :, T:TP], 0.0).then_inc(s_init, 1)
            nc.gpsimd.memset(latent[:, T:TP], 0.0).then_inc(s_init, 1)
            nc.gpsimd.memset(qt[:, :, T:TP], 0.0).then_inc(s_init, 1)
            nc.gpsimd.memset(e[:, :, EC:], 1.0).then_inc(s_init, 1)

            def norm_scaled(n, weight=None):
                src = x0 if n == 1 else xc
                for hf in range(2):
                    if n == 1:
                        pool.wait_ge(s_x0, 2 + hf + 1)
                    else:
                        pool.wait_ge(s_cent, cent_count(n, hf))
                    if weight is not None:
                        for c in range(C):
                            ins = nc.gpsimd.tensor_scalar(xn[:, c, half(hf)], src[:, c, half(hf)],
                                                          weight[:, c:c + 1], 0.0, ALU.mult, ALU.add)
                        ins.then_inc(s_xw, 1)
                for hf in range(2):
                    if weight is not None:
                        pool.wait_ge(s_xw, 2 * n + hf + 1)
                    pool.wait_ge(s_ars, (0, 4, 6, 8, 10)[n] + hf + 1)
                    y = ars[:, half(hf)].unsqueeze(1).broadcast_to([P, C, HALF])
                    nc.gpsimd.tensor_tensor(xn[:, :, half(hf)], (src if weight is None else xn)[:, :, half(hf)], y,
                                            ALU.mult).then_inc(s_xy, 1)

            def rope_sums(a):
                for u in range(NPROJ):
                    n = a * NPROJ + u
                    pool.wait_ge(s_rope, n + 1)
                    if n >= 2:
                        pool.wait_ge(s_qk, n - 1)
                    nc.gpsimd.tensor_tensor(rt[:, u % 2, :], ra[:, u % 2, :], rb[:, u % 2, :], ALU.add)\
                        .then_inc(s_rsum, 1)
                    pool.wait_ge(s_rsum, n + 1)
                    pool.wait_ge(s_qars, n + 1)
                    nc.gpsimd.tensor_tensor(rt[:, u % 2, :], rt[:, u % 2, :], rs[:, u % 2, :], ALU.mult)\
                        .then_inc(s_rscaled, 1)

            pool.wait_ge(s_tok, 2)
            nc.gpsimd.memset(region[:, OT:OT + V4], 0.0).then_inc(s_vz, 1)
            norm_scaled(0, vector("norm1"))
            rope_sums(0)
            norm_scaled(1, vector("norm2"))
            rope_sums(1)
            def low_part(u, i):
                pool.wait_ge(s_wsh, u + 1)
                nc.gpsimd.tensor_tensor(wl[i], ring[i], wh[i].bitcast(f32), ALU.subtract)\
                    .then_inc(s_wsl, 1)

            def activation_low_part(n, j):
                pool.wait_ge(s_ah, n + 1)
                nc.gpsimd.tensor_tensor(al[:, j, :], act[:, j, :], ah[:, j, :].bitcast(f32), ALU.subtract)\
                    .then_inc(s_alp, 1)

            low_part(0, 0)
            low_part(1, 1)
            norm_scaled(2)
            activation_low_part(0, 0)
            low_part(2, 2)
            activation_low_part(1, 1)
            activation_low_part(2, 0)
            low_part(3, 3)
            activation_low_part(3, 1)
            with pool.Fori(1, UNITS // NRING) as r:
                for i in range(NRING):
                    low_part(r * NRING + i, i)
            for u in range(UNITS - UNITS % NRING, UNITS):
                low_part(u, u % NRING)

            pool.wait_ge(s_sc, 1)
            for k, (w, wq_) in enumerate(((w1_sb, w1q), (w2_sb, w2q))):
                nc.gpsimd.tensor_scalar(w[:], w[:], inv[:, k:k + 1], ROUND, ALU.mult, ALU.add).then_inc(s_wqt, 1)
            for k, (w, wq_) in enumerate(((w1_sb, w1q), (w2_sb, w2q))):
                pool.wait_ge(s_wqt, k + 1)
                nc.gpsimd.tensor_scalar(wq_[:].rearrange("p c n -> p (c n)"), w[:], 1.0, -ROUND, ALU.mult, ALU.add)\
                    .then_inc(s_wq, 1)
            nc.gpsimd.memset(region[:, 0:V16], 0.0).then_inc(s_vz, 1)
            pool.wait_ge(s_vz, 2)
            for b in range(2):
                nc.gpsimd.memset(v16[64 * b:64 * b + S, :, :, b, HD:HD + 1], 1.0).then_inc(s_vz, 1)
            pool.wait_ge(s_vz, 4)

            norm_scaled(3)
            pool.wait_ge(s_qkev, 4)
            for p in range(PAIRS):
                if p >= 2:
                    pool.wait_ge(s_s, 2 * PAIRS + p - 1)
                for c in range(C):
                    ins = variants(nc.gpsimd, qvar, qt, p, c)
                    if c == C - 1:
                        ins.then_inc(s_qvar, 1)

            norm_scaled(4)
            pool.wait_ge(s_sc, 5)
            for i, ch in enumerate(POOL_CHUNKS):
                nc.gpsimd.tensor_scalar(hid[:, ch, :], hid[:, ch, :], inv[:, 3:4], ROUND, ALU.mult, ALU.add)\
                    .then_inc(s_hqs, 1)
                pool.wait_ge(s_hqs, i + 1)
                nc.gpsimd.tensor_scalar(hidq[:, ch, :], hid[:, ch, :], 1.0, -ROUND, ALU.mult, ALU.add)\
                    .then_inc(s_hqp, 1)

        @block.scalar
        def _(act_e):
            own = [0]

            def link(ins):
                own[0] += 1
                ins.then_inc(s_act_own, 1)
                act_e.wait_ge(s_act_own, own[0])

            for k in range(LEAD):
                act_e.dma_start(w_lin_sb[:, k, :], w_lin[:, k, :]).then_inc(s_x[k], 16)
            act_e.dma_start(cst[:], consts).then_inc(s_cst, 16)
            act_e.dma_start(vec[:], vecs).then_inc(s_cst, 16)
            act_e.dma_start(nt[:, 0:NBF], consts_bf).then_inc(s_cst, 16)
            for k in range(LEAD, KT):
                act_e.dma_start(w_lin_sb[:, k, :], w_lin[:, k, :]).then_inc(s_x[k], 16)
            act_e.dma_start(down_sb[:], g_down).then_inc(s_attn_w[0], 16)
            act_e.dma_start(gk_sb[:], g_k).then_inc(s_attn_w[0], 16)
            act_e.dma_start(gv_sb[:], g_v).then_inc(s_attn_w[0], 16)
            act_e.wait_ge(s_init, 8)
            act_e.wait_ge(s_cst, 48)

            warmed = [0]

            def load_table(func):
                k = warmed[0]
                warmed[0] += 1
                nc.scalar.activation(spare[:, k:k + 1], eps[:, 0:1], func)

            def norm(n, mean=True, eps_at=0):
                load_table(ACT.Abs_reciprocal_sqrt)
                for hf in range(2):
                    if mean:
                        act_e.wait_ge(s_cent, cent_count(n, hf))
                        src = xc
                    else:
                        act_e.wait_ge(s_x0, 2 + hf + 1)
                        src = x0
                    nc.scalar.activation(sq[:, :, half(hf)], src[:, :, half(hf)], ACT.Square).then_inc(s_sq, 1)
                for hf in range(2):
                    act_e.wait_ge(s_var, 2 * n + hf + 1)
                    nc.scalar.activation(ars[:, half(hf)], ps[2 + hf][:, 0:HALF], ACT.Abs_reciprocal_sqrt,
                                         bias=eps[:, eps_at:eps_at + 1]).then_inc(s_ars, 1)

            def layer_norm_scale(hf):
                act_e.wait_ge(s_xn, hf + 1)
                nc.scalar.activation(var[:, half(hf)], ps[2 + hf][:, 0:HALF], ACT.Copy)
                nc.scalar.activation(ars0[:, half(hf)], ps[2 + hf][:, 0:HALF], ACT.Abs_reciprocal_sqrt,
                                     bias=eps[:, 0:1]).then_inc(s_ars, 1)

            def latent_copied(hf):
                act_e.wait_ge(s_lat, hf + 1)
                nc.scalar.activation(latent[:, half(hf)], ps[2 + hf][0:LAT, 0:HALF], ACT.Copy).then_inc(s_latv, 1)

            def key_variants(a, hf):
                act_e.wait_ge(s_qk, a * NPROJ + QK_UNITS.index((2, hf)) + 1)
                if a == 1:
                    act_e.wait_ge(s_s, PAIRS)
                for g in range(ACT_VARIANTS):
                    ins = nc.scalar.activation(km[:, g // 4, g % 4, half(hf)], sq[:, 0, half(hf)], ACT.Copy,
                                               scale=const("onehot8")[:, g:g + 1])
                ins.then_inc(s_km, 1)

            def qk_units(a):
                for u in range(NPROJ + 1):
                    n = a * NPROJ + u
                    if a == 0 and u < 2:
                        layer_norm_scale(u)
                    if a == 0 and 1 <= u < 3:
                        latent_copied(u - 1)
                    if u < NPROJ:
                        act_e.wait_ge(s_proj, n + 1)
                        if n >= 2:
                            act_e.wait_ge(s_swap, n - 1)
                        nc.scalar.activation(qcopy[:, u % 2, :], ps[4 + 2 * (u % 2)][:, 0:HALF], ACT.Copy)\
                            .then_inc(s_qcp, 1)
                        nc.scalar.activation(sq2[:, u % 2, :], ps[4 + 2 * (u % 2)][:, 0:HALF], ACT.Square)\
                            .then_inc(s_qsq, 1)
                    if u >= 1:
                        m = n - 1
                        act_e.wait_ge(s_qms, m + 1)
                        if m >= 2:
                            act_e.wait_ge(s_qk, m - 1)
                        nc.scalar.activation(rs[:, (u - 1) % 2, :], ps[(u - 1) % 2][:, 0:HALF],
                                             ACT.Abs_reciprocal_sqrt, bias=eps[:, 2:3]).then_inc(s_qars, 1)
                    if u >= 2 and QK_UNITS[u - 2][0] == 2:
                        key_variants(a, QK_UNITS[u - 2][1])

            def outputs_copied(g):
                act_e.wait_ge(s_ott, 2 * g + 2)
                src = ps[2 + g % 2][:].rearrange("p (i w) -> p i w", i=4)
                for c in range(C):
                    dst = ot[:, c, 4 * g * S:4 * (g + 1) * S].rearrange("p (i s) -> p i s", i=4)
                    ins = nc.scalar.activation(dst, src[:, :, 64 * c:64 * c + S], ACT.Identity,
                                               bias=vector("qkv_b")[:, 4 + c:5 + c])
                ins.then_inc(s_ot, 1)

            def last_key_variants(p):
                if p >= 2:
                    act_e.wait_ge(s_sq_s, p - 1)
                for g in range(8):
                    ins = nc.scalar.activation(kvar[:, p % 2, 1, g, :], kt[:, 1, 2 * p * S:2 * (p + 1) * S], ACT.Copy,
                                               scale=const("onehot8")[:, g:g + 1])
                ins.then_inc(s_kvar1, 1)

            def attention(a):
                for p in range(PAIRS + 2):
                    if a == 2 and p + 2 < PAIRS:
                        last_key_variants(p + 2)
                    if p < PAIRS:
                        n = a * PAIRS + p
                        act_e.wait_ge(s_s, n + 1)
                        if n >= 2:
                            act_e.wait_ge(s_o, n - 1)
                        sb0 = score_bank(a, p)
                        nc.scalar.activation(e[0:ROWS, p % 2, 0:EC].rearrange("p (k n) -> p k n", k=2),
                                             psum[0:ROWS, sb0:sb0 + 2, 0:HALFPOS * S], ACT.Exp,
                                             scale=HD ** -0.5).then_inc(s_e, 1)
                    if a == 2 and p >= 4 and p % 2 == 0:
                        outputs_copied((p - 4) // 2)
                if a == 2:
                    outputs_copied(PAIRS // 2 - 1)

            norm(0, eps_at=1)
            for a in range(2):
                if a == 1:
                    norm(1, mean=False, eps_at=2)
                qk_units(a)
                load_table(ACT.Exp)
                act_e.wait_ge(s_vps, a + 1)
                act_e.wait_ge(s_vz, 1)
                for b in range(2):
                    rows = slice(64 * b, 64 * b + S)
                    ins = nc.scalar.activation(v4[rows, :, :, b, :],
                                               ps[2][rows, :].rearrange("p (q h d) -> p q h d", q=PAIRS, h=KVH),
                                               ACT.Copy)
                ins.then_inc(s_v, 1)
                attention(a)

            def high_part(u, i, r, reused=True):
                act_e.wait_ge(s_ring[i], r * 16 + 16)
                if reused:
                    act_e.wait_ge(s_down, 2 * (u - NRING + 1))
                    act_e.wait_ge(s_wsl, u - NRING + 1)
                nc.scalar.activation(wh[i], ring[i], ACT.Copy).then_inc(s_wsh, 1)

            AHEAD = 2
            for i in range(AHEAD):
                high_part(i, i, 0, False)
            norm(2)
            for hf in range(2):
                act_e.wait_ge(s_xn, 4 + hf + 1)
                nc.scalar.activation(xh[:, :, half(hf)], xn[:, :, half(hf)], ACT.Copy).then_inc(s_xh, 1)
            load_table(ACT.Sigmoid)
            act_e.wait_ge(s_log, 1)
            nc.scalar.activation(sig[:].rearrange("p t n -> p (t n)"), ps[6][:, 0:TT * EXPERTS], ACT.Sigmoid)\
                .then_inc(s_sig, 1)
            load_table(ACT.Silu)

            def expert_unit(n, j):
                act_e.wait_ge(s_g, n + 1)
                nc.scalar.activation(sg[:, j, :], ps[4][:, 0:HALF], ACT.Silu).then_inc(s_sg, 1)
                act_e.wait_ge(s_act, n + 1)
                nc.scalar.activation(ah[:, j, :], act[:, j, :], ACT.Copy).then_inc(s_ah, 1)

            for i in range(NRING):
                expert_unit(2 * i, 0)
                high_part(i + AHEAD, (i + AHEAD) % NRING, (i + AHEAD) // NRING, i + AHEAD >= NRING)
                expert_unit(2 * i + 1, 1)
            with act_e.Fori(1, (UNITS - AHEAD) // NRING) as r:
                for i in range(NRING):
                    u = r * NRING + i
                    expert_unit(2 * u, 0)
                    high_part(u + AHEAD, (i + AHEAD) % NRING, r + (i + AHEAD) // NRING)
                    expert_unit(2 * u + 1, 1)
            for u in range(UNITS - AHEAD, UNITS):
                expert_unit(2 * u, 0)
                expert_unit(2 * u + 1, 1)
            act_e.wait_ge(s_acc, 1)
            for hf in range(2):
                for m in range(C):
                    ins = nc.scalar.activation(h[:, m, half(hf)], ps[2 * m + hf][:, 0:HALF], ACT.Copy)
                ins.then_inc(s_h, 1)

            norm(3)
            load_table(ACT.Exp)
            for hf in range(2):
                for c in range(C):
                    act_e.wait_ge(s_qkps, 4 * hf + c + 1)
                    nc.scalar.activation(qt[:, c, half(hf)], ps[4 + 2 * c + hf][:, 0:HALF], ACT.Identity,
                                         bias=vector("qkv_b")[:, c:c + 1]).then_inc(s_qkev, 1)
            for b in range(4):
                if b == 0:
                    act_e.wait_ge(s_kev, 4)
                    act_e.wait_ge(s_vz, 4)
                if b % 2 == 0:
                    last_key_variants(b // 2)
                act_e.wait_ge(s_vps, 2 + b + 1)
                for j in range(2):
                    rows = slice(64 * j, 64 * j + S)
                    ins = nc.scalar.activation(v16[rows, 2 * b:2 * b + 2, :, j, 0:HD],
                                               ps[4 + b][rows, :].rearrange("p (q h d) -> p q h d", q=2, h=HEADS),
                                               ACT.Copy)
                ins.then_inc(s_v, 1)
            attention(2)

            norm(4)
            load_table(ACT.Gelu)
            act_e.wait_ge(s_sc, 4)
            for ch in range(FC):
                act_e.wait_ge(s_f1, ch + 1)
                bank = 4 + 2 * (ch % 2)
                nc.scalar.activation(hid[:, ch, :].rearrange("p (h t) -> p h t", h=2), psum[:, bank:bank + 2, 0:HALF],
                                     ACT.Gelu, bias=b1s[:, ch:ch + 1], scale=sxw[:, 0:1]).then_inc(s_hid, 1)
            act_e.wait_ge(s_sc, 5)
            for ch in range(ACT_CHUNKS):
                nc.scalar.activation(hid[:, ch, :], hid[:, ch, :], ACT.Copy, bias=ROUND, scale=inv[:, 3:4])\
                    .then_inc(s_hs, 1)

            for hf in range(2):
                act_e.wait_ge(s_fin, 2 * hf + 2)
                act_e.dma_start(out[:, 1, half(hf)], x0[:, 1, half(hf)]).then_inc(s_out, 16)

        @block.vector
        def _(dve):
            own = [0]

            def link(ins):
                own[0] += 1
                ins.then_inc(s_dve, 1)
                dve.wait_ge(s_dve, own[0])

            def bc(ap, dims):
                return ap.broadcast_to(dims)

            def newton(y, v, t, eps_at, factor=1.0):
                link(nc.vector.scalar_tensor_tensor(t, v, eps[:, eps_at:eps_at + 1], y, ALU.add, ALU.mult))
                link(nc.vector.scalar_tensor_tensor(t, t, -0.5 * factor, y, ALU.mult, ALU.mult))
                link(nc.vector.scalar_tensor_tensor(y, t, 1.5 * factor, y, ALU.add, ALU.mult))

            def centre(n):
                for hf in range(2):
                    dve.wait_ge(s_mean, cent_count(n, hf))
                    nc.vector.tensor_tensor(xc[:, :, half(hf)], h[:, :, half(hf)],
                                            bc(ps[hf][:, 0:HALF].unsqueeze(1), [P, C, HALF]), ALU.subtract)\
                        .then_inc(s_cent, 1)

            def norm_apply(n, count, eps_at=0, factor=1.0):
                for hf in range(2):
                    dve.wait_ge(s_ars, count + hf + 1)
                    t, y = nt[:, half(hf)], ars[:, half(hf)]
                    link(nc.vector.scalar_tensor_tensor(t, ps[2 + hf][:, 0:HALF], eps[:, eps_at:eps_at + 1], y,
                                                        ALU.add, ALU.mult))
                    link(nc.vector.scalar_tensor_tensor(t, t, -0.5 * factor, y, ALU.mult, ALU.mult))
                    dve.wait_ge(s_xy, 2 * n + hf + 1)
                    for c in range(C):
                        ins = nc.vector.scalar_tensor_tensor(xn[:, c, half(hf)], t, 1.5 * factor, xn[:, c, half(hf)],
                                                             ALU.add, ALU.mult)
                    ins.then_inc(s_xn, 1)

            def layer_norm_stream(hf):
                dve.wait_ge(s_ars, 2 + hf + 1)
                newton(ars0[:, half(hf)], var[:, half(hf)], nt[:, half(hf)], 0)
                for c in range(C):
                    ins = nc.vector.tensor_tensor(x0[:, c, half(hf)], xc[:, c, half(hf)], ars0[:, half(hf)],
                                                  ALU.mult)
                ins.then_inc(s_x0, 1)

            def reduce_peaks(k, n, bank, count):
                dve.wait_ge(s_pkt, count)
                nc.vector.tensor_reduce(pk1[0:1, k:k + n], ps[bank][0:1, 0:n * P].rearrange("p (n c) -> p n c", n=n),
                                        AX.X, ALU.max).then_inc(s_pk1, 1)

            def scales_of(k, n, bank, count):
                dve.wait_ge(s_pkb, count)
                link(nc.vector.tensor_scalar(scale[:, k:k + n], ps[bank][:, 0:n], MIN_RANGE, 1.0 / QP,
                                             ALU.max, ALU.mult))
                return nc.vector.reciprocal(inv[:, k:k + n], scale[:, k:k + n])

            def qk_units(a):
                names = (("cos_g", "sin_g"), ("cos_l", "sin_l"))[a]
                cos, sin = (bc(const(x).unsqueeze(1), [P, HB, S]) for x in names)

                def images(ap):
                    return ap.rearrange("p (b s) -> p b s", s=S)

                for u in range(NPROJ + 1):
                    n = a * NPROJ + u
                    if u < NPROJ:
                        dve.wait_ge(s_swap, n + 1)
                        b0 = 4 + 2 * (u % 2)
                        if n >= 2:
                            dve.wait_ge(s_rsum, n - 1)
                        nc.vector.tensor_tensor(images(rb[:, u % 2, :]), images(ps[b0 + 1][:, 0:HALF]), sin,
                                                ALU.mult)
                        dve.wait_ge(s_qsq, n + 1)
                        nc.vector.tensor_tensor(images(ra[:, u % 2, :]), images(ps[b0][:, 0:HALF]), cos,
                                                ALU.mult).then_inc(s_rope, 1)
                    if u >= 1:
                        w, k = u - 1, (u - 1) % 2
                        dve.wait_ge(s_qars, n)
                        y, t = rs[:, k, :], rn[:]
                        if n >= 2:
                            dve.wait_ge(s_qk, n - 1)
                        link(nc.vector.scalar_tensor_tensor(t, ps[k][:, 0:HALF], eps[:, 2:3], y, ALU.add, ALU.mult))
                        link(nc.vector.scalar_tensor_tensor(t, t, -0.5, y, ALU.mult, ALU.mult))
                        dve.wait_ge(s_rscaled, n)
                        j, hf = QK_UNITS[w]
                        dst = qt[:, j, half(hf)] if j < 2 else sq[:, 0, half(hf)]
                        ins = nc.vector.scalar_tensor_tensor(dst, t, 1.5, rt[:, k, :], ALU.add, ALU.mult)
                        ins.then_inc(s_qk, 1)
                    if u >= 2 and QK_UNITS[u - 2][0] == 2:
                        hf = QK_UNITS[u - 2][1]
                        for g in range(ACT_VARIANTS, 8):
                            ins = nc.vector.tensor_scalar(km[:, g // 4, g % 4, half(hf)], sq[:, 0, half(hf)],
                                                          const("onehot8")[:, g:g + 1], None, ALU.mult)
                        ins.then_inc(s_kmv, 1)

            def normalise_grouped(a, p):
                n = a * PAIRS + p
                dve.wait_ge(s_o, n + 1)
                bank = ps[p % 2]
                if n >= 1:
                    dve.wait_ge(s_on, n)
                link(nc.vector.reciprocal(rc[:], bank[:, G4 * S:2 * G4 * S]))
                nc.vector.tensor_tensor(ot4[:, :, p * S:(p + 1) * S],
                                        bank[:, 0:G4 * S].rearrange("p (g s) -> p g s", g=G4),
                                        rc[:].rearrange("p (g s) -> p g s", g=G4), ALU.mult).then_inc(s_on, 1)

            def normalise_outputs(p):
                n = 2 * PAIRS + p
                dve.wait_ge(s_o, n + 1)
                o = ps[p % 2][:, 0:HEADS * (HD + 1)].rearrange("p (h b d) -> p h b d", h=HALFPOS, b=2)
                den = rden[:, p % 2, :].rearrange("p (h b) -> p h b", h=HALFPOS)
                if p >= 2:
                    dve.wait_ge(s_on, n - 1)
                link(nc.vector.reciprocal(den, o[:, :, :, HD]))
                if p >= 2:
                    dve.wait_ge(s_ott, p - 1)
                nc.vector.tensor_tensor(on[:, p % 2, :, :].rearrange("p b (h d) -> p h b d", h=HALFPOS),
                                        o[:, :, :, 0:HD],
                                        bc(den.unsqueeze(3), [P, HALFPOS, 2, HD]), ALU.mult).then_inc(s_on, 1)

            nc.vector.memset(wparts[:], 0.0).then_inc(s_zero, 1)
            dve.wait_ge(s_cst, 48)
            nc.vector.tensor_copy(cstb[:], nt[:, 0:NBF]).then_inc(s_init, 1)
            link(nc.vector.tensor_tensor(posb[:].rearrange("p c s -> p (c s)"), vector("pos"), vector("base"),
                                         ALU.add))
            for hf in range(2):
                dve.wait_ge(s_tok, hf + 1)
                for c in range(C):
                    ins = nc.vector.tensor_tensor(
                        h[:, c, half(hf)].rearrange("p (b s) -> p b s", s=S),
                        ps[2 * c + hf][:, 0:HALF].rearrange("p (b s) -> p b s", s=S),
                        bc(posb[:, c, :].unsqueeze(1), [P, HB, S]), ALU.add)
                ins.then_inc(s_h, 1)

            centre(0)
            norm_apply(0, 0, 1, (1.0 + RMS_EPS) ** -0.5)
            for a in range(2):
                if a == 1:
                    norm_apply(1, 4, 2)
                qk_units(a)
                for p in range(PAIRS):
                    normalise_grouped(a, p)
                    if a == 0 and p in (1, 3):
                        layer_norm_stream(p // 2)
                    if a == 1 and p == 1:
                        dve.wait_ge(s_ffw, 32)
                    if a == 1 and p in (1, 4):
                        nc.vector.tensor_reduce(pk[:, p // 4:p // 4 + 1], (w1_sb, w2_sb)[p // 4][:], AX.X, ALU.max,
                                                apply_absolute_value=True).then_inc(s_pk, 1)
                for hf in range(2):
                    dve.wait_ge(s_wo, 2 * a + hf + 1)
                    for m in range(C):
                        dst, src = (z[:, m, half(hf)].rearrange("p (q b s) -> p q b s", b=2, s=S)
                                    for z in ((x0, tmp)[a], x0))
                        ins = nc.vector.tensor_tensor(
                            dst, src, ps[4 + 2 * m + hf][:, 0:HALF].rearrange("p (b q s) -> p q b s", b=2, s=S),
                            ALU.add)
                    if a == 0:
                        ins.then_inc(s_x0, 1)
                    else:
                        link(ins)
                        nc.vector.tensor_tensor(h[:, :, half(hf)], h[:, :, half(hf)], tmp[:, :, half(hf)], ALU.add)\
                            .then_inc(s_h, 1)

            centre(2)
            norm_apply(2, 6)
            for hf in range(2):
                dve.wait_ge(s_xh, hf + 1)
                nc.vector.tensor_tensor(xl[:, :, half(hf)], xn[:, :, half(hf)], xh[:, :, half(hf)].bitcast(f32),
                                        ALU.subtract).then_inc(s_xs, 1)

            reduce_peaks(0, 2, 7, 1)

            def shared_product(n, j):
                dve.wait_ge(s_sg, n + 1)
                dve.wait_ge(s_u, n + 1)
                nc.vector.tensor_tensor(act[:, j, :], sg[:, j, :], ps[5][:, 0:HALF], ALU.mult).then_inc(s_act, 1)

            dve.wait_ge(s_sig, 1)
            bias = bc(vector("gate_bias").unsqueeze(1), [P, TT, EXPERTS])
            link(nc.vector.tensor_tensor(choice[:], sig[:], bias, ALU.add))
            for t in range(TT):
                for g in range(GROUPS):
                    ins = nc.vector.max(top[:, t, g, :], choice[:, t, g * PER_GROUP:(g + 1) * PER_GROUP])
            link(ins)
            link(nc.vector.tensor_tensor(gsum[:], top[:, :, :, 0], top[:, :, :, 1], ALU.add))
            mine = bc(gsum[:].unsqueeze(3), [P, TT, GROUPS, GROUPS])
            others = bc(gsum[:].unsqueeze(2), [P, TT, GROUPS, GROUPS])
            nc.vector.tensor_tensor(gcmp[:], others, mine, ALU.is_gt)
            link(nc.vector.tensor_tensor(geq[:], others, mine, ALU.is_equal))
            flat = lambda ap: ap.rearrange("p t a b -> p t (a b)")
            link(nc.vector.tensor_tensor(flat(geq[:]), flat(geq[:]),
                                         bc(const("tie").unsqueeze(1), [P, TT, 16]), ALU.mult))
            link(nc.vector.tensor_tensor(flat(gcmp[:]), flat(gcmp[:]), flat(geq[:]), ALU.add))
            link(nc.vector.tensor_reduce(grank[:], gcmp[:], AX.X, ALU.add))
            link(nc.vector.tensor_scalar(grank[:], grank[:], 2.0, None, ALU.is_lt))
            link(nc.vector.tensor_tensor(
                masked[:].rearrange("p t (g k) -> p t g k", g=GROUPS),
                choice[:].rearrange("p t (g k) -> p t g k", g=GROUPS),
                bc(grank[:].unsqueeze(3), [P, TT, GROUPS, PER_GROUP]), ALU.mult))
            shared_product(0, 0)
            scales_of(0, 2, 7, 1).then_inc(s_sc, 1)
            link(nc.vector.tensor_scalar(masked[:], masked[:], 0.0, None, ALU.add))
            for t in range(TT):
                ins = nc.vector.max(top[:, t, 0, :], masked[:, t, :])
            link(ins)
            for t in range(TT):
                ins = nc.vector.match_replace(repl[:, t, :], top[:, t, 0, :], masked[:, t, :], -3.0e38)
            link(ins)
            shared_product(1, 1)
            link(nc.vector.tensor_tensor(repl[:], repl[:], masked[:], ALU.not_equal))
            link(nc.vector.tensor_tensor(wts[:], repl[:], sig[:], ALU.mult))
            link(nc.vector.tensor_reduce(wsum[:], wts[:], AX.X, ALU.add))
            link(nc.vector.tensor_scalar(wsum[:], wsum[:], 1e-20, None, ALU.add))
            link(nc.vector.reciprocal(wsum[:], wsum[:]))
            link(nc.vector.tensor_scalar(wsum[:], wsum[:], ROUTED_SCALING, None, ALU.mult))
            link(nc.vector.tensor_tensor(wts[:], wts[:], bc(wsum[:].unsqueeze(2), [P, TT, EXPERTS]), ALU.mult))
            shared_product(2, 0)
            link(nc.vector.tensor_copy(wparts[:, :, 0:EXPERTS], wts[:]))
            link(nc.vector.tensor_tensor(wres[:], wts[:], wparts[:, :, 0:EXPERTS], ALU.subtract))
            link(nc.vector.tensor_copy(wparts[:, :, EXPERTS:2 * EXPERTS], wres[:]))
            link(nc.vector.tensor_tensor(wres[:], wres[:], wparts[:, :, EXPERTS:2 * EXPERTS], ALU.subtract))
            nc.vector.tensor_copy(wparts[:, :, 2 * EXPERTS:3 * EXPERTS], wres[:]).then_inc(s_wp, 1)
            shared_product(3, 1)
            dve.wait_ge(s_wt, 1)
            nc.vector.tensor_copy(wrow[0:96, :], ps[7][:].bitcast(bf16)[0:96, 0:TT * P]).then_inc(s_wrow, 1)

            def expert_unit(n, j):
                dve.wait_ge(s_sg, n + 1)
                dve.wait_ge(s_u, n + 1)
                ins = nc.vector.tensor_tensor(gu[:, j, :], sg[:, j, :], ps[5][:, 0:HALF], ALU.mult)
                ins.then_inc(s_mulc, 1)
                dve.wait_ge(s_mulc, n + (1 - 2 * SHARED))
                nc.vector.tensor_tensor(act[:, j, :], gu[:, j, :], ps[6][:, 0:HALF], ALU.mult).then_inc(s_act, 1)
                dve.wait_ge(s_ah, n + 1)
                nc.vector.tensor_tensor(al[:, j, :], act[:, j, :], ah[:, j, :].bitcast(f32), ALU.subtract)\
                    .then_inc(s_al, 1)

            with dve.Fori(1, UNITS // 2) as r:
                for j in range(4):
                    expert_unit(r * 4 + j, j % 2)

            centre(3)
            norm_apply(3, 8)
            for hf in range(2):
                for c in range(C):
                    dve.wait_ge(s_qkps, 4 * hf + 2 + c + 1)
                    nc.vector.tensor_scalar(kt[:, c, half(hf)], ps[2 * c + hf][:, 0:HALF],
                                            vector("qkv_b")[:, 2 + c:3 + c], None, ALU.add).then_inc(s_kev, 1)
            nc.vector.tensor_copy(pairs_r, const("pairs")).then_inc(s_kmr, 1)
            dve.wait_ge(s_kev, 4)
            for p in range(-1, PAIRS + 2):
                if p + 1 < PAIRS:
                    if p + 1 >= 2:
                        dve.wait_ge(s_sq_s, p)
                    variants(nc.vector, kvar, kt, p + 1, 0).then_inc(s_kvar, 1)
                if 0 <= p < PAIRS:
                    dve.wait_ge(s_sq_s, p + 1)
                    nc.vector.tensor_reduce(
                        mx[:, p % 2, :].rearrange("p (k h) -> p k h", k=2),
                        psum[:, 4:6, 0:HALFPOS * S].rearrange("p k (h s) -> p k h s", s=S), AX.X, ALU.max)\
                        .then_inc(s_mx, 1)
                    dve.wait_ge(s_mx, p + 1)
                    if p >= 2:
                        dve.wait_ge(s_s, 2 * PAIRS + p - 1)
                    nc.vector.tensor_tensor(dg[:, p % 2, :, :], bc(mx[:, p % 2, :].unsqueeze(2), [P, HEADS, S]),
                                            bc(const("minus_ident").unsqueeze(1), [P, HEADS, S]), ALU.mult)\
                        .then_inc(s_dg, 1)
                if p >= 2:
                    normalise_outputs(p - 2)
            for hf in range(2):
                dve.wait_ge(s_wo, 4 + hf + 1)
                for m in range(C):
                    ins = nc.vector.scalar_tensor_tensor(h[:, m, half(hf)], ps[4 + 2 * m + hf][:, 0:HALF],
                                                         vector("out_b")[:, m:m + 1], h[:, m, half(hf)],
                                                         ALU.add, ALU.add)
                ins.then_inc(s_h, 1)

            centre(4)
            norm_apply(4, 10)
            dve.wait_ge(s_xn, 10)
            nc.vector.tensor_reduce(pk[:, 2:3], xn[:, :, 0:T], AX.XY, ALU.max, apply_absolute_value=True)\
                .then_inc(s_pk, 1)
            reduce_peaks(2, 1, 7, 2)
            scales_of(2, 1, 7, 2).then_inc(s_sc, 1)
            dve.wait_ge(s_sc, 2)
            link(nc.vector.tensor_scalar(xn[:, :, 0:T], xn[:, :, 0:T], inv[:, 2:3], ROUND, ALU.mult, ALU.add))
            nc.vector.tensor_scalar(xq[:], xn[:, :, 0:T], -ROUND, None, ALU.add).then_inc(s_xq, 1)
            nc.vector.tensor_tensor(sxw[:, 0:1], scale[:, 0:1], scale[:, 2:3], ALU.mult).then_inc(s_sc, 1)
            dve.wait_ge(s_sc, 3)
            nc.vector.tensor_scalar(b1s[:], vector("b1"), sxw[:, 0:1], None, ALU.mult).then_inc(s_sc, 1)
            for ch in range(FC):
                dve.wait_ge(s_hid, ch + 1)
                ins = nc.vector.tensor_reduce(peak[:, ch:ch + 1], hid[:, ch, :], AX.X, ALU.max,
                                              apply_absolute_value=True)
            link(ins)
            nc.vector.tensor_reduce(pk[:, 3:4], peak[:], AX.X, ALU.max).then_inc(s_pk, 1)
            reduce_peaks(3, 1, 3, 3)
            scales_of(3, 1, 3, 3).then_inc(s_sc, 1)
            nc.vector.tensor_tensor(sxw[:, 1:2], scale[:, 1:2], scale[:, 3:4], ALU.mult).then_inc(s_sc, 1)
            dve.wait_ge(s_sc, 5)
            for ch in DVE_CHUNKS:
                ins = nc.vector.tensor_scalar(hid[:, ch, :], hid[:, ch, :], inv[:, 3:4], ROUND, ALU.mult, ALU.add)
            link(ins)
            for ch in (*DVE_CHUNKS, *range(ACT_CHUNKS)):
                if ch < ACT_CHUNKS:
                    dve.wait_ge(s_hs, ch + 1)
                nc.vector.tensor_scalar(hidq[:, ch, :], hid[:, ch, :], -ROUND, None, ALU.add).then_inc(s_hq, 1)
            dve.wait_ge(s_sc, 6)
            link(nc.vector.tensor_scalar(b2s[:], vector("b2"), sxw[:, 1:2], None, ALU.mult))
            for m in range(C):
                ins = nc.vector.tensor_scalar(x0[:, m, :], h[:, m, :], b2s[:, m:m + 1], None, ALU.add)
            link(ins)
            for hf in range(2):
                dve.wait_ge(s_f2, hf + 1)
                for m in range(C):
                    ins = nc.vector.scalar_tensor_tensor(x0[:, m, half(hf)], ps[2 * m + hf][:, 0:HALF], sxw[:, 1:2],
                                                         x0[:, m, half(hf)], ALU.mult, ALU.add)
                    ins.then_inc(s_fin, 1)

        @block.tensor
        def _(pe):
            def mm(out_, lhsT, rhs, start, stop):
                return nc.tensor.matmul(out_, lhsT, rhs, start=start, stop=stop, skip_group_check=True)

            def keep_busy(bank, count, lhsT=ident_bf, rhs=cstb[:, 0:1].broadcast_to([P, HALF])):
                for _ in range(count):
                    mm(ps[bank][:, 0:HALF], lhsT, rhs, True, True)

            def norm(n, mean=True):
                spare_bank, busy = BUSY[n]
                if n:
                    keep_busy(spare_bank, busy[0])
                if mean:
                    for hf in range(2):
                        pe.wait_ge(s_h, cent_count(n, hf))
                        for c in range(C):
                            ins = mm(ps[hf][:, 0:HALF], const("mean"), h[:, c, half(hf)], c == 0, c == C - 1)
                        ins.then_inc(s_mean, 1)
                    spare_bank = 7
                    keep_busy(spare_bank, busy[1])
                for hf in range(2):
                    pe.wait_ge(s_sq, 2 * n + hf + 1)
                    for c in range(C):
                        ins = mm(ps[2 + hf][:, 0:HALF], const("mean"), sq[:, c, half(hf)], c == 0, c == C - 1)
                    ins.then_inc(s_var, 1)
                keep_busy(spare_bank, busy[2])

            def latent_sums(hf):
                pe.wait_ge(s_xn, hf + 1)
                pe.wait_ge(s_ars, 2 + hf + 1)
                for c in range(C):
                    ins = mm(ps[2 + hf][0:LAT, 0:HALF], down_sb[:, c, :], xn[:, c, half(hf)], c == 0, c == C - 1)
                ins.then_inc(s_lat, 1)

            def qk_units(a):
                for u in range(NPROJ + 1):
                    n = a * NPROJ + u
                    if u < NPROJ:
                        j, hf = QK_UNITS[u]
                        if a == 0 and 1 <= u < 3:
                            latent_sums(u - 1)
                        pe.wait_ge(s_xn, 2 * a + hf + 1)
                        if a == 0 and j == 2:
                            pe.wait_ge(s_latv, hf + 1)
                        if u >= 2:
                            pe.wait_ge(s_rope, n - 1)
                        bank = ps[4 + 2 * (u % 2)][:, 0:HALF]
                        if j == 2 and a == 0:
                            ins = mm(bank, gk_sb[:], latent[:, half(hf)], True, True)
                        else:
                            for c in range(C):
                                w = wq_sb[a][:, c, j * P:(j + 1) * P] if j < 2 else lk_sb[:, c, :]
                                ins = mm(bank, w, xn[:, c, half(hf)], c == 0, c == C - 1)
                        ins.then_inc(s_proj, 1)
                    if u >= 1:
                        pe.wait_ge(s_qsq, n)
                        if u >= 3:
                            pe.wait_ge(s_qk, n - 2)
                        mm(ps[(u - 1) % 2][:, 0:HALF], const("headmean"), sq2[:, (u - 1) % 2, :], True, True)\
                            .then_inc(s_qms, 1)
                    if u < NPROJ:
                        pe.wait_ge(s_qcp, n + 1)
                        mm(ps[4 + 2 * (u % 2) + 1][:, 0:HALF], const("swap"), qcopy[:, u % 2, :], True, True)\
                            .then_inc(s_swap, 1)

            def row_scores(p):
                pe.wait_ge(s_kvar, p + 1)
                pe.wait_ge(s_kvar1, p + 1)
                if p >= 1:
                    pe.wait_ge(s_mx, p)
                for c in range(C):
                    for b in range(2):
                        at = (2 * p + b) * S
                        ins = mm(ps[4 + c][64 * b:64 * b + 64, 0:HALF].rearrange("p (g s) -> p g s", g=8),
                                 qt[:, c, at:at + 64], kvar[:, p % 2, c, :, b * S:(b + 1) * S], True, True)
                ins.then_inc(s_sq_s, 1)

            def scores(a, p):
                n = a * PAIRS + p
                b0 = score_bank(a, p)
                if a < 2:
                    if p >= 2:
                        pe.wait_ge(s_e, n - 1)
                    for gp in range(2):
                        mm(ps[b0 + gp][0:ROWS, 0:HALFPOS * S].rearrange("p (h s) -> p h s", s=S),
                           ident_bf[:, 0:ROWS], causal_bf.unsqueeze(1).broadcast_to([P, HALFPOS, S]), True, False)
                else:
                    pe.wait_ge(s_dg, p + 1)
                    pe.wait_ge(s_qvar, p + 1)
                    if p >= 1:
                        pe.wait_ge(s_e, n)
                    for gp in range(2):
                        mm(ps[b0 + gp][0:ROWS, 0:HALFPOS * S], pairs_r[:, 0:ROWS],
                           dg[:, p % 2, gp * HALFPOS:(gp + 1) * HALFPOS, :].rearrange("p h s -> p (h s)"),
                           True, False)
                if a == 2:
                    for c in range(C):
                        for b in range(2):
                            ins = mm(ps[b0 + c][64 * b:64 * b + S, 0:HALF].rearrange("p (g s) -> p g s", g=8),
                                     kt[:, c, image(2 * p + b)], qvar[:, p % 2, c, :, b * S:(b + 1) * S], False, True)
                    ins.then_inc(s_s, 1)
                    return
                for k in range(0, HALFPOS, 2):
                    for gp in range(2):
                        for b in range(2):
                            cols = image(2 * p + b)
                            out_ = ps[b0 + gp][64 * b:64 * b + S, :]
                            ins = mm(out_[:, k * S:(k + 2) * S].rearrange("p (c s) -> p c s", c=C),
                                     km[:, gp, k // 2, cols], qt[:, :, cols], False, True)
                ins.then_inc(s_s, 1)

            def grouped_values(a, p):
                n = a * PAIRS + p
                pe.wait_ge(s_e, n + 1)
                if p >= 2:
                    pe.wait_ge(s_on, n - 1)
                for part in range(2):
                    for kv in range(KVH):
                        w = v4[0:ROWS, p, kv, :, :].rearrange("p b d -> p (b d)") if part == 0 else \
                            const("pair_ones", ROWS)
                        ex = e[0:ROWS, p % 2, 0:EC].rearrange("p (g n) -> p g n", g=2)
                        ins = mm(ps[p % 2][VP * kv:VP * (kv + 1), part * G4 * S:(part + 1) * G4 * S]
                                 .rearrange("p (g n) -> p g n", g=2),
                                 w, ex[:, :, kv * 2 * S:(kv + 1) * 2 * S], True, True)
                ins.then_inc(s_o, 1)

            def weighted_values(p):
                pe.wait_ge(s_e, 2 * PAIRS + p + 1)
                if p >= 2:
                    pe.wait_ge(s_on, 2 * PAIRS + p - 1)
                for hd in range(HEADS):
                    rows = slice(64 * (hd % 2), 64 * (hd % 2) + EP)
                    cols = slice(hd // 2 * 2 * (HD + 1), (hd // 2 + 1) * 2 * (HD + 1))
                    ins = mm(ps[p % 2][rows, cols], e[0:ROWS, p % 2, hd * S:hd * S + EP],
                             v16[0:ROWS, p, hd, :, :].rearrange("p b d -> p (b d)"), True, True)
                ins.then_inc(s_o, 1)

            def transposes(p):
                pe.wait_ge(s_on, 2 * PAIRS + p + 1)
                g = p // 2
                if p % 2 == 0 and g >= 2:
                    pe.wait_ge(s_ot, g - 1)
                for b in range(2):
                    at = ((p % 2) * 2 + b) * P
                    ins = nc.tensor.transpose(ps[2 + g % 2][:, at:at + P], on[:, p % 2, b, :], const("ident"))
                ins.then_inc(s_ott, 1)

            def project_grouped(a):
                N = HALF // 2
                for hf in range(2):
                    pe.wait_ge(s_on, a * PAIRS + PAIRS // 2 * (hf + 1))
                    for m in range(C):
                        for b in range(2):
                            for g in range(G4):
                                ins = mm(ps[4 + 2 * m + hf][:, b * N:(b + 1) * N], wo_sb[:, b, g, m * P:(m + 1) * P],
                                         ot4[:, g, hf * N:(hf + 1) * N], g == 0, g == G4 - 1)
                    ins.then_inc(s_wo, 1)

            def project_out():
                for hf in range(2):
                    pe.wait_ge(s_ot, 2 * (hf + 1))
                    for m in range(C):
                        for c in range(C):
                            ins = mm(ps[4 + 2 * m + hf][:, 0:HALF], outw_sb[:, c, m * P:(m + 1) * P],
                                     ot[:, c, half(hf)], c == 0, c == C - 1)
                    ins.then_inc(s_wo, 1)

            def half_ready(a, hf):
                pe.wait_ge(s_qk, a * NPROJ + (NPROJ // 2, NPROJ)[hf])
                pe.wait_ge(s_km, 2 * a + hf + 1)
                pe.wait_ge(s_kmv, 2 * a + hf + 1)

            def attention(a):
                lead = 1 if a == 2 else 0
                for p in range(PAIRS + 2 + lead):
                    if a == 2 and p < PAIRS:
                        row_scores(p)
                    if a == 2 and p == lead:
                        pe.wait_ge(s_v, 6)
                    if a < 2 and p == PAIRS // 2:
                        half_ready(a, 1)
                    if 0 <= p - lead < PAIRS:
                        scores(a, p - lead)
                    if 0 <= p - lead - 1 < PAIRS:
                        if a < 2 and p == 1:
                            pe.wait_ge(s_v, a + 1)
                            pe.wait_ge(s_qk, NPROJ * (a + 1))
                        if a < 2:
                            grouped_values(a, p - 1)
                        else:
                            weighted_values(p - 2)
                    if a == 2 and 0 <= p - lead - 2:
                        transposes(p - 3)

            def peak_rows(k, n, bank, count):
                pe.wait_ge(s_pk, count)
                for q in range(n):
                    ins = mm(ps[bank][0:1, q * P:(q + 1) * P], pk[:, k + q:k + q + 1], const("ident"), True, True)
                ins.then_inc(s_pkt, 1)

            def peak_broadcast(k, n, bank, count):
                pe.wait_ge(s_pk1, count)
                mm(ps[bank][:, 0:n], const("ones", 1), pk1[0:1, k:k + n], True, True).then_inc(s_pkb, 1)

            pe.wait_ge(s_zero, 1)
            zeros = wparts[:].rearrange("p t n -> p (t n)")
            keep_busy(7, START_BUSY, zeros[:, 0:P], zeros[:, 0:HALF])
            for k in range(KT):
                pe.wait_ge(s_x[k], 32)
                for hf in range(2):
                    for c in range(C):
                        ins = mm(ps[2 * c + hf][:, 0:HALF], w_lin_sb[:, k, c * P:(c + 1) * P],
                                 patches[:, k, half(hf)], k == 0, k == KT - 1)
                    if k == KT - 1:
                        ins.then_inc(s_tok, 1)

            pe.wait_ge(s_init, 8)
            pe.wait_ge(s_cst, 48)
            norm(0)
            pe.wait_ge(s_attn_w[0], 64)
            for a in range(2):
                if a == 1:
                    norm(1, mean=False)
                    pe.wait_ge(s_attn_w[1], 48)
                qk_units(a)
                for q in range(PAIRS):
                    for c in range(a + 1):
                        for b in range(2):
                            out_ = ps[2][64 * b:64 * b + 64, q * KVH * HD:(q + 1) * KVH * HD]
                            at = (2 * q + b) * S
                            if a == 0:
                                ins = mm(out_, latent[:, at:at + 64], gv_sb[:], True, True)
                            else:
                                ins = mm(out_, xn[:, c, at:at + 64], lv_sb[:, c, :], c == 0, c == C - 1)
                ins.then_inc(s_vps, 1)
                pe.wait_ge(s_rope, NPROJ * (a + 1))
                half_ready(a, 0)
                attention(a)
                pe.wait_ge(s_wo_w, 16 * (a + 1))
                project_grouped(a)

            norm(2)

            def seed(m):
                for hf in range(2):
                    mm(ps[2 * m + hf][:, 0:HALF], const("ident"), h[:, m, half(hf)], True, False)

            peak_rows(0, 2, 7, 2)
            pe.wait_ge(s_cent, cent_count(2, 1))
            seed(0)
            pe.wait_ge(s_moe_w, 48)
            pe.wait_ge(s_xn, 5)
            for t in range(TT):
                if t == HALF // P:
                    pe.wait_ge(s_xn, 6)
                for c in range(C):
                    ins = mm(ps[6][:, t * EXPERTS:(t + 1) * EXPERTS], xn[:, c, t * P:(t + 1) * P],
                             gate_sb[:, c, :], c == 0, c == C - 1)
            ins.then_inc(s_log, 1)

            def three(out_, parts_w, parts_x, start, stop):
                (w_hi, w_lo), (x_hi, x_lo) = parts_w, parts_x
                mm(out_, w_hi, x_hi, start, False)
                mm(out_, w_hi, x_lo, False, False)
                return mm(out_, w_lo, x_hi, False, stop)

            def up_sums(u, i, hf, first=False, shared=False, wait_for_weights=False):
                n = 2 * u + hf
                if hf == 0:
                    pe.wait_ge(s_wsl, u + 1)
                if not first:
                    pe.wait_ge(s_sg, n)
                for c in range(C):
                    cols = slice(c * INNER, (c + 1) * INNER)
                    ins = three(ps[4][:, 0:HALF], (wh[i][:, cols], wl[i][:, cols]),
                                (xh[:, c, half(hf)], xl[:, c, half(hf)]), c == 0, c == C - 1)
                ins.then_inc(s_g, 1)
                if not first:
                    pe.wait_ge(s_act, n)
                for c in range(C):
                    cols = slice(D + c * INNER, D + (c + 1) * INNER)
                    ins = three(ps[5][:, 0:HALF], (wh[i][:, cols], wl[i][:, cols]),
                                (xh[:, c, half(hf)], xl[:, c, half(hf)]), c == 0, c == C - 1)
                if wait_for_weights:
                    pe.wait_ge(s_wrow, 1)
                if not shared:
                    sel = select_bf[0:96, bass.ds(u, 1)].broadcast_to([96, P])
                    ins = mm(ps[6][:, 0:HALF], sel, wrow[0:96, half(hf)], True, True)
                ins.then_inc(s_u, 1)

            def down_sums(u, i, hf, shared=False):
                n = 2 * u + hf
                if shared:
                    pe.wait_ge(s_alp, n + 1)
                else:
                    pe.wait_ge(s_al, n + (1 - 2 * SHARED))
                for m in range(C):
                    cols = slice(2 * D + m * P, 2 * D + (m + 1) * P)
                    ins = three(ps[2 * m + hf][:, 0:HALF], (wh[i][:, cols], wl[i][:, cols]),
                                (ah[:, hf, :], al[:, hf, :]), False, False)
                ins.then_inc(s_down, 1)

            pe.wait_ge(s_xs, 1)
            up_sums(0, 0, 0, first=True, shared=True)
            seed(1)
            peak_broadcast(0, 2, 7, 1)
            pe.wait_ge(s_xs, 2)
            up_sums(0, 0, 1, shared=True)
            down_sums(0, 0, 0, shared=True)
            up_sums(1, 1, 0, shared=True)
            down_sums(0, 0, 1, shared=True)
            up_sums(1, 1, 1, shared=True)
            down_sums(1, 1, 0, shared=True)
            pe.wait_ge(s_wp, 1)
            for t in range(TT):
                ins = nc.tensor.transpose(ps[7][:].bitcast(bf16)[0:96, t * P:(t + 1) * P], wparts[:, t, :],
                                          ident_bf)
            ins.then_inc(s_wt, 1)
            up_sums(2, 2, 0, wait_for_weights=True)
            down_sums(1, 1, 1, shared=True)
            for u in (2, 3):
                up_sums(u, u, 1)
                down_sums(u, u, 0)
                up_sums(u + 1, (u + 1) % NRING, 0)
                down_sums(u, u, 1)
            with pe.Fori(1, (UNITS - 1) // NRING) as r:
                for i in range(NRING):
                    u, nxt = r * NRING + i, (i + 1) % NRING
                    up_sums(u, i, 1)
                    down_sums(u, i, 0)
                    up_sums(u + 1, nxt, 0)
                    down_sums(u, i, 1)
            for u in range((UNITS - 1) // NRING * NRING, UNITS):
                i = u % NRING
                up_sums(u, i, 1)
                down_sums(u, i, 0)
                if u + 1 < UNITS:
                    up_sums(u + 1, (i + 1) % NRING, 0)
                down_sums(u, i, 1)
            pe.wait_ge(s_down, 2 * UNITS)
            mm(ps[7][0:1, 0:1], const("ones")[:, 0:1], const("ones")[:, 0:1], True, True).then_inc(s_acc, 1)

            norm(3)
            for hf in range(2):
                pe.wait_ge(s_xn, 6 + hf + 1)
                for part in range(2):
                    for c in range(C):
                        bank = ps[4 * (1 - part) + 2 * c + hf][:, 0:HALF]
                        for k in range(C):
                            ins = mm(bank, qkv_sb[:, k, part * D + c * P:part * D + (c + 1) * P],
                                     xn[:, k, half(hf)], k == 0, k == C - 1)
                        ins.then_inc(s_qkps, 1)
            for b in range(4):
                pe.wait_ge(s_qkev, (1, 3, 2, 4)[b])
                for q in range(2):
                    for k in range(C):
                        for j in range(2):
                            at = (4 * b + 2 * q + j) * S
                            ins = mm(ps[4 + b][64 * j:64 * j + 64, q * D:(q + 1) * D],
                                     xn[:, k, at:at + 64], qkv_sb[:, k, 2 * D:3 * D], k == 0, k == C - 1)
                ins.then_inc(s_vps, 1)
            pe.wait_ge(s_kev, 4)
            pe.wait_ge(s_kmr, 1)
            pe.wait_ge(s_v, 4)
            pe.wait_ge(s_vz, 4)
            attention(2)
            project_out()

            norm(4)
            keep_busy(7, 8)
            peak_rows(2, 1, 7, 3)
            peak_broadcast(2, 1, 7, 2)
            keep_busy(0, 10)
            pe.wait_ge(s_wq, 2)
            pe.wait_ge(s_xq, 1)
            for ch in range(FC):
                if ch >= 2:
                    pe.wait_ge(s_hid, ch - 1)
                for hf in range(2):
                    for c in range(C):
                        ins = mm(ps[4 + 2 * (ch % 2) + hf][:, 0:HALF], w1q[:, c, ch * P:(ch + 1) * P],
                                 xq[:, c, half(hf)], c == 0, c == C - 1)
                ins.then_inc(s_f1, 1)
            keep_busy(0, 10)
            peak_rows(3, 1, 3, 4)
            peak_broadcast(3, 1, 3, 3)
            keep_busy(0, 10)
            order = (*DVE_CHUNKS, *range(ACT_CHUNKS), *POOL_CHUNKS)
            for n, ch in enumerate(order):
                if ch in POOL_CHUNKS:
                    pe.wait_ge(s_hqp, POOL_CHUNKS.index(ch) + 1)
                else:
                    pe.wait_ge(s_hq, n + 1)
                for hf in range(2):
                    for m in range(C):
                        ins = mm(ps[2 * m + hf][:, 0:HALF], w2q[:, ch, m * P:(m + 1) * P],
                                 hidq[:, ch, half(hf)], n == 0, n == FC - 1)
                    if n == FC - 1:
                        ins.then_inc(s_f2, 1)


def constants():
    import numpy as np

    f = np.float32
    c = np.zeros((P, NCONST), f)
    row = np.arange(P)

    def put(name, a):
        lo, hi = CONST_COLS[name]
        c[:, lo:hi] = a

    put("ident", np.eye(P))
    put("mean", 1.0 / D)
    put("swap", row[:, None] == (row[None, :] ^ 1))
    put("headmean", (row[:, None] // HD == row[None, :] // HD) / HD)
    put("ones", 1.0)
    token = row % 64
    real = token < S
    put("pair_ones", (row[:, None] // 64 == np.arange(VP)[None, :] // HD) & real[:, None])
    put("pairs", (row[:, None] // 64 == row[None, :] // 64) & real[:, None] & real[None, :])
    put("minus_ident", -((token[:, None] == np.arange(S)[None, :]) & real[:, None]).astype(f))
    d = row % HD
    for name, base in (("g", 1000000.0), ("l", 10000.0)):
        inv_freq = f(1.0) / f(base) ** (np.arange(0, HD, 2, dtype=f) / f(HD))
        freqs = np.arange(S, dtype=f)[:, None] * inv_freq[None, :].astype(f)
        put("cos_" + name, np.cos(freqs).astype(f).T[d // 2, :])
        put("sin_" + name, np.sin(freqs).astype(f).T[d // 2, :] * np.where(d % 2 == 0, -1, 1)[:, None])
    put("onehot8", row[:, None] // HD == np.arange(8)[None, :])
    g = np.arange(GROUPS)
    put("tie", (g[None, :] < g[:, None]).astype(f).reshape(1, 16))
    b = np.zeros((P, NBF), f)
    b[:, 0:P] = np.eye(P)
    b[:, P:P + S] = np.where(real[:, None] & (token[:, None] > np.arange(S)[None, :]), -32768.0, 0.0)
    for u in range(SHARED, UNITS):
        for part in range(3):
            b[part * EXPERTS + u - SHARED, P + S + u] = 1.0
    return c, b


def layouts(i):
    import numpy as np

    def chunks(w):
        k, n = w.shape
        return np.ascontiguousarray(w.reshape(k // P, P, n).transpose(1, 0, 2))

    x = i["x"].reshape(B, 3, GRID, PATCH, GRID, PATCH).transpose(1, 3, 5, 0, 2, 4).reshape(KT * P, B, S - 1)
    xp = np.zeros((KT * P, B, S), x.dtype)
    xp[:, :, 1:] = x
    a = {"x": chunks(xp.reshape(KT * P, T)), "w_lin": chunks(i["L0_tok_W_lin"].T)}

    v = np.zeros((P, NVEC), np.float32)

    def put(name, rows):
        lo, hi = VEC_COLS[name]
        v[:, lo:hi] = rows.reshape(P, hi - lo)

    put("pos", chunks(i["L0_tok_position_embeddings"][0].T))
    base = np.concatenate([i["L0_tok_class_token"][0], np.repeat(i["L0_tok_b_lin"][None], S - 1, 0)], 0)
    put("base", chunks(base.T))
    col = lambda w: w.reshape(-1, P).T
    put("norm1", col(i["L0_attn_norm1_w"]))
    put("norm2", col(i["L0_attn_norm2_w"]))
    o_row = np.arange(D).reshape(HALFPOS, 2, HD).transpose(1, 0, 2).reshape(D)
    put("qkv_b", np.concatenate([col(i["L1_attn_qkv_b"][:2 * D]), col(i["L1_attn_qkv_b"][2 * D:][o_row])], 1))
    put("out_b", col(i["L1_attn_out_b"]))
    put("b1", col(i["L1_ffn_b1"]))
    put("b2", col(i["L1_ffn_b2"]))
    put("gate_bias", np.repeat(i["L0_ffn_gate_bias"][None], P, 0))
    a["vecs"] = v

    c, gp, kv, d = np.meshgrid(np.arange(C), np.arange(2), np.arange(KVH), np.arange(HD), indexing="ij")
    q_col = ((kv * 4 + 2 * c + gp) * HD + d).reshape(-1)
    k_col = (kv * HD + d)[0].reshape(-1)

    def by_group(w):
        rows = w.reshape(KVH, C, 2, HD, D).transpose(0, 3, 2, 1, 4).reshape(KVH, HD, G4, D)
        padded = np.zeros((KVH, 2, HD, 2, G4, D), w.dtype)
        for b in range(2):
            padded[:, b, :, b] = rows
        return padded.reshape(P, 2, G4, D)

    a["g_wq"] = chunks(i["L0_attn_g_wq"])[..., q_col]
    a["g_down"] = chunks(i["L0_attn_g_kv_down"])
    a["g_k"] = i["L0_attn_g_k_up"][..., k_col]
    a["g_v"] = i["L0_attn_g_v_up"]
    a["g_wo"] = by_group(i["L0_attn_g_wo"])
    a["l_wq"] = chunks(i["L0_attn_l_wq"])[..., q_col]
    a["l_wk"] = chunks(i["L0_attn_l_wk"])[..., k_col]
    a["l_wv"] = chunks(i["L0_attn_l_wv"])
    a["l_wo"] = by_group(i["L0_attn_l_wo"])
    a["gate_w"] = chunks(i["L0_ffn_gate_w"].T)
    wg = np.concatenate([i["L0_ffn_shared_gate"].reshape(SHARED, INNER, D), i["L0_ffn_expert_gate"]], 0)
    wu = np.concatenate([i["L0_ffn_shared_up"].reshape(SHARED, INNER, D), i["L0_ffn_expert_up"]], 0)
    wd = np.concatenate([i["L0_ffn_shared_down"].reshape(D, SHARED, INNER).transpose(1, 0, 2),
                         i["L0_ffn_expert_down"]], 0)
    up = lambda w: w.reshape(UNITS, INNER, C, P).transpose(0, 3, 2, 1).reshape(UNITS, P, D)
    a["experts"] = np.concatenate([up(wg), up(wu), wd.transpose(0, 2, 1)], 2)
    a["qkv_w"] = chunks(i["L1_attn_qkv_w"].T)
    a["out_w"] = chunks(i["L1_attn_out_w"].T[o_row])
    a["w1"] = chunks(i["L1_ffn_w1"].T).reshape(P, C * FF)
    a["w2"] = chunks(i["L1_ffn_w2"].T).reshape(P, FC * D)
    return {k: np.ascontiguousarray(w) for k, w in a.items()}


_ORDER = ["x", "w_lin", "consts", "consts_bf", "vecs", "g_wq", "g_down", "g_k", "g_v", "g_wo", "l_wq", "l_wk",
          "l_wv", "l_wo", "gate_w", "experts", "qkv_w", "out_w", "w1", "w2"]


def kernel(**inputs):
    import numpy as np
    import concourse.bacc as bacc
    from concourse.bass_utils import run_bass_kernel_spmd

    arrays = layouts({k: np.asarray(v) for k, v in inputs.items()})
    arrays["consts"], arrays["consts_bf"] = constants()
    nc = bacc.Bacc("TRN2", target_bir_lowering=False, num_devices=1)
    args = [nc.dram_tensor(f"in_{k}", arrays[k].shape, mybir.dt.from_np(arrays[k].dtype), kind="ExternalInput").ap()
            for k in _ORDER]
    out = nc.dram_tensor("out", (P, C, T), mybir.dt.float32, kind="ExternalOutput").ap()
    program(nc, *args, out)
    r = run_bass_kernel_spmd(nc, [{f"in_{k}": arrays[k] for k in _ORDER}], core_ids=[0])
    got = r.results[0]["out"]
    return np.ascontiguousarray(got.transpose(2, 1, 0).reshape(B, S, D))
```
